# Optimizing a Trainium2 kernel written in Bass

```python
import numpy as np
import jax
import jax.numpy as jnp

def _softmax(x, axis=-1):
    return jax.nn.softmax(x, axis=axis)

def _gelu(x):
    return jax.nn.gelu(x, approximate=True)

def _silu(x):
    return jax.nn.silu(x)

def _sigmoid(x):
    return jax.nn.sigmoid(x)

def _layernorm(x, axis=-1, eps=1e-05):
    m = jnp.mean(x, axis=axis, keepdims=True)
    v = jnp.var(x, axis=axis, keepdims=True)
    return (x - m) / jnp.sqrt(v + eps)

def _scatter_add(tgt, idx, src, axis=0):
    return tgt.at[idx].add(src)

def _segment_sum(src, seg, n):
    return jax.ops.segment_sum(src, seg, n)
kernel_name = 'mk_adaln_d2_jaxref_r8_3db664'

def setup_inputs(seed: int=0):
    np.random.seed(seed)
    _w = jnp.asarray

    def _L0_attn_setup():
        import jax, jax.numpy as jnp
        import numpy as np
        H = 16
        G = 4
        MAX_POS = 128
        key = jax.random.key(seed)
        ks = jax.random.split(key, 6)
        B, T, D = (8, 128, 128)
        hd = D // H
        s = 0.02
        return {'x': jax.random.normal(ks[0], (B, T, D), jnp.float32), 'Wq': jax.random.normal(ks[1], (D, D), jnp.float32) * s, 'Wk': jax.random.normal(ks[2], (hd * G, D), jnp.float32) * s, 'Wv': jax.random.normal(ks[3], (hd * G, D), jnp.float32) * s, 'Wo': jax.random.normal(ks[4], (D, D), jnp.float32) * s, 'E': jax.random.normal(ks[5], (2 * MAX_POS - 1, hd), jnp.float32) * s}
    _L0_attn_in = _L0_attn_setup()

    def _L0_ffn_setup():
        import jax, jax.numpy as jnp
        import numpy as np
        TOPK = 4
        N_GROUPS = 4
        TOPK_GROUPS = 2
        ROUTE_SCALE = 2.5

        def _gate(x2, Wg):
            T = x2.shape[0]
            E = Wg.shape[0]
            scores = x2 @ Wg.T
            s = jax.nn.sigmoid(scores)
            g = s.reshape(T, N_GROUPS, E // N_GROUPS)
            group_scores = g.max(axis=-1)
            _, gidx = jax.lax.top_k(group_scores, TOPK_GROUPS)
            group_mask = jnp.any(jax.nn.one_hot(gidx, N_GROUPS, dtype=jnp.bool_), axis=1)
            masked = jnp.where(group_mask[:, :, None], g, -jnp.inf).reshape(T, E)
            _, idx = jax.lax.top_k(masked, TOPK)
            w = jnp.take_along_axis(s, idx, axis=1)
            w = w / jnp.sum(w, axis=-1, keepdims=True)
            w = w * ROUTE_SCALE
            return (w.astype(x2.dtype), idx)
        key = jax.random.key(seed)
        ks = jax.random.split(key, 6)
        B, S, D, I, E = (2, 256, 128, 128, 16)
        scale = 0.02
        return {'x': jax.random.normal(ks[0], (B, S, D), dtype=jnp.float32), 'Wg': jax.random.normal(ks[1], (E, D), dtype=jnp.float32) * scale, 'W1': jax.random.normal(ks[2], (E, I, D), dtype=jnp.float32) * scale, 'b1': jnp.zeros((E, I), dtype=jnp.float32), 'W2': jax.random.normal(ks[3], (E, D, I), dtype=jnp.float32) * scale, 'b2': jnp.zeros((E, D), dtype=jnp.float32), 'W3': jax.random.normal(ks[4], (E, I, D), dtype=jnp.float32) * scale, 'b3': jnp.zeros((E, I), dtype=jnp.float32)}
    _L0_ffn_in = _L0_ffn_setup()
    _L0_c = _w((lambda *s: np.random.randn(*s).astype(np.float32) * 0.05)(32, 128))
    _L0_wmod = _w((lambda *s: np.random.randn(*s).astype(np.float32) * 0.05)(128, 6 * 128) * 128 ** (-0.5))

    def _L1_attn_setup():
        import jax, jax.numpy as jnp
        import numpy as np
        import math
        D_MODEL = 128
        D_STATE = 16
        D_CONV = 4
        EXPAND = 2
        D_INNER = EXPAND * D_MODEL
        DT_RANK = math.ceil(D_MODEL / 16)
        B_SZ, T_LEN = (2, 128)
        DT_MIN, DT_MAX, DT_FLOOR = (0.001, 0.1, 0.0001)
        key = jax.random.key(seed)
        ks = jax.random.split(key, 10)
        s = 0.02
        x = jax.random.normal(ks[0], (B_SZ, T_LEN, D_MODEL), jnp.float32)
        W_in = jax.random.normal(ks[1], (2 * D_INNER, D_MODEL), jnp.float32) * s
        conv_w = jax.random.normal(ks[2], (D_INNER, 1, D_CONV), jnp.float32) * 0.2
        conv_b = jax.random.normal(ks[3], (D_INNER,), jnp.float32) * 0.02
        W_x = jax.random.normal(ks[4], (DT_RANK + 2 * D_STATE, D_INNER), jnp.float32) * s
        dt_std = DT_RANK ** (-0.5)
        W_dt = jax.random.uniform(ks[5], (D_INNER, DT_RANK), jnp.float32, -dt_std, dt_std)
        dt = jnp.exp(jax.random.uniform(ks[6], (D_INNER,), jnp.float32) * (math.log(DT_MAX) - math.log(DT_MIN)) + math.log(DT_MIN))
        dt = jnp.clip(dt, DT_FLOOR, None)
        b_dt = dt + jnp.log(-jnp.expm1(-dt))
        A_log = jnp.log(jnp.broadcast_to(jnp.arange(1, D_STATE + 1, dtype=jnp.float32), (D_INNER, D_STATE)))
        D_param = jnp.ones((D_INNER,), jnp.float32)
        W_out = jax.random.normal(ks[7], (D_MODEL, D_INNER), jnp.float32) * s
        return {'x': x, 'W_in': W_in, 'conv_w': conv_w, 'conv_b': conv_b, 'W_x': W_x, 'W_dt': W_dt, 'b_dt': b_dt, 'A_log': A_log, 'D_param': D_param, 'W_out': W_out}
    _L1_attn_in = _L1_attn_setup()

    def _L1_ffn_setup():
        import jax, jax.numpy as jnp
        import numpy as np
        D_MODEL = 128
        key = jax.random.key(seed)
        k_x, k_w, k_a1, k_a2 = jax.random.split(key, 4)
        x = jax.random.normal(k_x, (4, 256, D_MODEL), dtype=jnp.float32)
        weight = jax.random.normal(k_w, (D_MODEL, D_MODEL), dtype=jnp.float32) * 0.02
        aux_weight1 = jax.random.normal(k_a1, (D_MODEL, D_MODEL), dtype=jnp.float32) * 0.02
        aux_weight2 = jax.random.normal(k_a2, (D_MODEL, D_MODEL), dtype=jnp.float32) * 0.02
        bias = jnp.zeros((D_MODEL,), dtype=jnp.float32)
        return {'x': x, 'weight': weight, 'aux_weight1': aux_weight1, 'aux_weight2': aux_weight2, 'bias': bias}
    _L1_ffn_in = _L1_ffn_setup()
    _L1_c = _w((lambda *s: np.random.randn(*s).astype(np.float32) * 0.05)(32, 128))
    _L1_wmod = _w((lambda *s: np.random.randn(*s).astype(np.float32) * 0.05)(128, 6 * 128) * 128 ** (-0.5))
    _d = {'L0_attn_x': _L0_attn_in['x'], 'L0_attn_Wq': _L0_attn_in['Wq'], 'L0_attn_Wk': _L0_attn_in['Wk'], 'L0_attn_Wv': _L0_attn_in['Wv'], 'L0_attn_Wo': _L0_attn_in['Wo'], 'L0_attn_E': _L0_attn_in['E'], 'L0_ffn_Wg': _L0_ffn_in['Wg'], 'L0_ffn_W1': _L0_ffn_in['W1'], 'L0_ffn_b1': _L0_ffn_in['b1'], 'L0_ffn_W2': _L0_ffn_in['W2'], 'L0_ffn_b2': _L0_ffn_in['b2'], 'L0_ffn_W3': _L0_ffn_in['W3'], 'L0_ffn_b3': _L0_ffn_in['b3'], 'L0_c': _L0_c, 'L0_wmod': _L0_wmod, 'L1_attn_W_in': _L1_attn_in['W_in'], 'L1_attn_conv_w': _L1_attn_in['conv_w'], 'L1_attn_conv_b': _L1_attn_in['conv_b'], 'L1_attn_W_x': _L1_attn_in['W_x'], 'L1_attn_W_dt': _L1_attn_in['W_dt'], 'L1_attn_b_dt': _L1_attn_in['b_dt'], 'L1_attn_A_log': _L1_attn_in['A_log'], 'L1_attn_D_param': _L1_attn_in['D_param'], 'L1_attn_W_out': _L1_attn_in['W_out'], 'L1_ffn_weight': _L1_ffn_in['weight'], 'L1_ffn_aux_weight1': _L1_ffn_in['aux_weight1'], 'L1_ffn_aux_weight2': _L1_ffn_in['aux_weight2'], 'L1_ffn_bias': _L1_ffn_in['bias'], 'L1_c': _L1_c, 'L1_wmod': _L1_wmod}
    _x0 = _d['L0_attn_x']
    _d['L0_attn_x'] = jax.random.normal(jax.random.fold_in(jax.random.key(seed), 1), (32, 256, 128), dtype=_x0.dtype)
    del _x0
    return _d

def reference(L0_attn_x, L0_attn_Wq, L0_attn_Wk, L0_attn_Wv, L0_attn_Wo, L0_attn_E, L0_ffn_Wg, L0_ffn_W1, L0_ffn_b1, L0_ffn_W2, L0_ffn_b2, L0_ffn_W3, L0_ffn_b3, L0_c, L0_wmod, L1_attn_W_in, L1_attn_conv_w, L1_attn_conv_b, L1_attn_W_x, L1_attn_W_dt, L1_attn_b_dt, L1_attn_A_log, L1_attn_D_param, L1_attn_W_out, L1_ffn_weight, L1_ffn_aux_weight1, L1_ffn_aux_weight2, L1_ffn_bias, L1_c, L1_wmod):

    def _L0_attn_ref(x, Wq, Wk, Wv, Wo, E):
        import jax, jax.numpy as jnp
        import numpy as np
        H = 16
        G = 4
        MAX_POS = 128
        B, T, D = x.shape
        hd = D // H
        r = H // G
        q = (x @ Wq.T).reshape(B, T, H, hd).transpose(0, 2, 1, 3)
        k = (x @ Wk.T).reshape(B, T, G, hd)
        v = (x @ Wv.T).reshape(B, T, G, hd)
        k = jnp.repeat(k, r, axis=2).transpose(0, 2, 1, 3)
        v = jnp.repeat(v, r, axis=2).transpose(0, 2, 1, 3)
        q = q * (1.0 / hd) ** 0.5
        scores = jnp.einsum('bhqd,bhkd->bhqk', q, k)
        pos = jnp.arange(T)
        dist = jnp.clip(pos[None, :] - pos[:, None], -MAX_POS + 1, MAX_POS - 1) + MAX_POS - 1
        R = E[dist]
        bias = jnp.einsum('bhqd,kqd->bhqk', q, R)
        scores = scores + bias
        attn = jax.nn.softmax(scores, axis=-1)
        out = jnp.einsum('bhqk,bhkd->bhqd', attn, v)
        out = out.transpose(0, 2, 1, 3).reshape(B, T, D)
        return out @ Wo.T

    def _L0_ffn_ref(x, Wg, W1, b1, W2, b2, W3, b3):
        import jax, jax.numpy as jnp
        import numpy as np
        TOPK = 4
        N_GROUPS = 4
        TOPK_GROUPS = 2
        ROUTE_SCALE = 2.5

        def _gate(x2, Wg):
            T = x2.shape[0]
            E = Wg.shape[0]
            scores = x2 @ Wg.T
            s = jax.nn.sigmoid(scores)
            g = s.reshape(T, N_GROUPS, E // N_GROUPS)
            group_scores = g.max(axis=-1)
            _, gidx = jax.lax.top_k(group_scores, TOPK_GROUPS)
            group_mask = jnp.any(jax.nn.one_hot(gidx, N_GROUPS, dtype=jnp.bool_), axis=1)
            masked = jnp.where(group_mask[:, :, None], g, -jnp.inf).reshape(T, E)
            _, idx = jax.lax.top_k(masked, TOPK)
            w = jnp.take_along_axis(s, idx, axis=1)
            w = w / jnp.sum(w, axis=-1, keepdims=True)
            w = w * ROUTE_SCALE
            return (w.astype(x2.dtype), idx)
        shape = x.shape
        D = shape[-1]
        x2 = x.reshape(-1, D)
        weights, indices = _gate(x2, Wg)
        E = Wg.shape[0]
        y = jnp.zeros_like(x2)
        for e in range(E):
            we = jnp.sum(weights * (indices == e), axis=-1)
            h = jax.nn.silu(x2 @ W1[e].T + b1[e]) * (x2 @ W3[e].T + b3[e])
            y = y + (h @ W2[e].T + b2[e]) * we[:, None]
        return y.reshape(shape)

    def _L1_attn_ref(x, W_in, conv_w, conv_b, W_x, W_dt, b_dt, A_log, D_param, W_out):
        import jax, jax.numpy as jnp
        import numpy as np
        import math
        D_MODEL = 128
        D_STATE = 16
        D_CONV = 4
        EXPAND = 2
        D_INNER = EXPAND * D_MODEL
        DT_RANK = math.ceil(D_MODEL / 16)
        B_SZ, T_LEN = (2, 128)
        DT_MIN, DT_MAX, DT_FLOOR = (0.001, 0.1, 0.0001)
        silu = jax.nn.silu
        xz = jnp.einsum('btd,ed->bte', x, W_in)
        x_inner, z = (xz[..., :D_INNER], xz[..., D_INNER:])
        xc = jnp.transpose(x_inner, (0, 2, 1))
        xc = jax.lax.conv_general_dilated(xc, conv_w, window_strides=(1,), padding=[(D_CONV - 1, 0)], feature_group_count=D_INNER, dimension_numbers=('NCH', 'OIH', 'NCH')) + conv_b[None, :, None]
        x_conv = jnp.transpose(silu(xc), (0, 2, 1))
        x_dbl = jnp.einsum('btd,ed->bte', x_conv, W_x)
        dt_low = x_dbl[..., :DT_RANK]
        B_ssm = x_dbl[..., DT_RANK:DT_RANK + D_STATE]
        C_ssm = x_dbl[..., DT_RANK + D_STATE:]
        dt = jax.nn.softplus(jnp.einsum('btr,dr->btd', dt_low, W_dt) + b_dt)
        A = -jnp.exp(A_log)
        dA = jnp.exp(dt[..., None] * A)
        dBx = dt[..., None] * B_ssm[:, :, None, :] * x_conv[..., None]

        def comb(c1, c2):
            a1, b1 = c1
            a2, b2 = c2
            return (a1 * a2, a2 * b1 + b2)
        _, h = jax.lax.associative_scan(comb, (dA, dBx), axis=1)
        y = jnp.einsum('btdn,btn->btd', h, C_ssm)
        y = y * silu(z) + D_param * x_conv
        out = jnp.einsum('btd,ed->bte', y, W_out)
        return out

    def _L1_ffn_ref(x, weight, aux_weight1, aux_weight2, bias):
        import jax, jax.numpy as jnp
        import numpy as np
        D_MODEL = 128
        h = jnp.einsum('btc,cd->btd', x, weight)
        h = jnp.einsum('btc,cd->btd', h, aux_weight1)
        h = jnp.einsum('btc,cd->btd', h, aux_weight2)
        return jnp.tanh(h + bias)
    x = L0_attn_x
    mod = (_silu(L0_c) @ L0_wmod).reshape(L0_c.shape[0], 6, 1, -1)
    sa, ca, ga, sb, cb, gb = (mod[:, 0], mod[:, 1], mod[:, 2], mod[:, 3], mod[:, 4], mod[:, 5])
    ga = (2 * (ga >= 0) - 1) * jnp.maximum(jnp.abs(ga), 0.25)
    gb = (2 * (gb >= 0) - 1) * jnp.maximum(jnp.abs(gb), 0.25)
    h = _layernorm(x, axis=-1) * (1 + ca) + sa
    x = x + ga * _L0_attn_ref(h, L0_attn_Wq, L0_attn_Wk, L0_attn_Wv, L0_attn_Wo, L0_attn_E)
    h = _layernorm(x, axis=-1) * (1 + cb) + sb
    x = x + gb * _L0_ffn_ref(h, L0_ffn_Wg, L0_ffn_W1, L0_ffn_b1, L0_ffn_W2, L0_ffn_b2, L0_ffn_W3, L0_ffn_b3)
    mod = (_silu(L1_c) @ L1_wmod).reshape(L1_c.shape[0], 6, 1, -1)
    sa, ca, ga, sb, cb, gb = (mod[:, 0], mod[:, 1], mod[:, 2], mod[:, 3], mod[:, 4], mod[:, 5])
    ga = (2 * (ga >= 0) - 1) * jnp.maximum(jnp.abs(ga), 0.25)
    gb = (2 * (gb >= 0) - 1) * jnp.maximum(jnp.abs(gb), 0.25)
    h = _layernorm(x, axis=-1) * (1 + ca) + sa
    x = x + ga * _L1_attn_ref(h, L1_attn_W_in, L1_attn_conv_w, L1_attn_conv_b, L1_attn_W_x, L1_attn_W_dt, L1_attn_b_dt, L1_attn_A_log, L1_attn_D_param, L1_attn_W_out)
    h = _layernorm(x, axis=-1) * (1 + cb) + sb
    x = x + gb * _L1_ffn_ref(h, L1_ffn_weight, L1_ffn_aux_weight1, L1_ffn_aux_weight2, L1_ffn_bias)
    return x

_drawn_inputs = setup_inputs


def setup_inputs(seed=0):
    import zlib

    import numpy as np

    out = dict(_drawn_inputs(seed))
    spreads = {'L0_ffn_b1': (0.0, 0.1),
     'L0_ffn_b2': (0.0, 0.1),
     'L0_ffn_b3': (0.0, 0.1),
     'L1_attn_D_param': (1.0, 0.2),
     'L1_ffn_bias': (0.0, 0.1)}
    factors = {}
    for name, (base, spread) in spreads.items():
        noise = np.random.default_rng([zlib.crc32(name.encode()), seed]).standard_normal(out[name].shape)
        drawn = base * np.exp(spread * noise) if base else spread * noise
        out[name] = jnp.asarray(drawn.astype(out[name].dtype))
    for name, factor in factors.items():
        out[name] = (out[name] * factor).astype(out[name].dtype)
    return out
```

```python
from contextlib import ExitStack

import concourse.bass as bass
from concourse import mybir

F32 = mybir.dt.float32
BF16 = mybir.dt.bfloat16
ALU = mybir.AluOpType
ACT = mybir.ActivationFunctionType
AX_X = mybir.AxisListType.X

P = 128
B, T, D = 32, 256, 128
PAIRS = B // 2
TOK = 2 * T
TILES = TOK // P
EPS = 1e-5
H, G, HD = 16, 4, 8
QB = 8
NB = T // QB
KROWS = G * HD
QROWS = KROWS + QB * HD
MAX_POS = 128
CHUNKS = 2 * NB // 2
GROUPS = 4
CPG = CHUNKS // GROUPS
BPG = 2 * CPG
PIECES = 4
NE, NG, TOPK, TOPG, ROUTE_SCALE = 16, 4, 4, 2, 2.5
DI, NH, NS, DTR, KC = 256, 2, 16, 8, 4
PARTS = 3
SROWS = PARTS * 32
RING = 3
SA, CA, GA, SB, CB, GB = range(6)

IN_SHAPES = [
    ("x", (PAIRS + 1, TOK, D)), ("wq_rep", (P, H * QROWS)), ("wk_t", (P, KROWS)), ("wv_t", (P, P)),
    ("wo_x", (P, G * D)), ("e_shift", (QB * HD, NB * T)), ("wg_t", (P, P)), ("w1_t", (P, NE * P)),
    ("w3_t", (P, NE * P)), ("w2_t", (P, NE * P)), ("b1_c", (P, NE)), ("b3_c", (P, NE)), ("b2_r", (SROWS, D)),
    ("c_t", (P, 2 * B)), ("wmod", (P, 2 * 6 * D)), ("win_t", (P, 2 * DI)), ("conv_w", (P, NH * KC)),
    ("conv_b", (P, NH)), ("wx_bc", (P, NH * SROWS)), ("wx_dt", (DTR, DI)), ("wdt_t", (DTR, DI)),
    ("b_dt", (P, NH)), ("a_log", (P, NH * NS)), ("d_par", (P, NH)), ("wout_t", (P, NH * D)),
    ("ffn_w_t", (P, D)), ("ffn_a1", (P, D)), ("ffn_a2", (P, D)), ("ffn_b", (P, 1)),
    ("ident", (P, P)), ("mask_q", (QROWS, G * QB)), ("mask_d", (P, G * QB)), ("sel_r", (P, P)),
    ("tie", (P, NG * NG)), ("sel_n", (SROWS, 32 * P)),
]


def build(nc, dram, out):
    ctx = ExitStack()
    with ctx:
        sems = []

        def sb(name, shape, dt=F32):
            return ctx.enter_context(nc.sbuf_tensor(name, shape, dt))

        def sem(name):
            s = ctx.enter_context(nc.semaphore(name))
            sems.append(s)
            return s

        bank = [ctx.enter_context(nc.psum_tensor(f"bank{k}", [P, 512], F32)) for k in range(8)]

        wq_rep = sb("wq_rep", [P, H, QROWS])
        wk_t = sb("wk_t", [P, KROWS])
        wv_t = sb("wv_t", [P, P])
        wo_x = sb("wo_x", [P, G, D])
        wg_t = sb("wg_t", [P, P])
        w1_t = sb("w1_t", [P, NE, P])
        w3_t = sb("w3_t", [P, NE, P])
        w2_t = sb("w2_t", [P, NE, P])
        b1_c = sb("b1_c", [P, NE])
        b3_c = sb("b3_c", [P, NE])
        b2_r = sb("b2_r", [SROWS, D])
        win_t = sb("win_t", [P, 2 * DI])
        conv_w = sb("conv_w", [P, NH, KC])
        conv_b = sb("conv_b", [P, NH])
        wx_bc = sb("wx_bc", [P, NH, SROWS])
        w_dtx = sb("w_dtx", [P, NH, DI])
        b_dt = sb("b_dt", [P, NH])
        neg_a = sb("neg_a", [P, NH * NS])
        d_par = sb("d_par", [P, NH])
        wout_t = sb("wout_t", [P, NH, D])
        ffn_w = sb("ffn_w", [P, D])
        ffn_b = sb("ffn_b", [P, 1])
        ident = sb("ident", [P, P])
        mask_q = sb("mask_q", [QROWS, G, QB])
        mask_d = sb("mask_d", [P, G * QB])
        sel_r = sb("sel_r", [P, P])
        tie = sb("tie", [P, NG * NG])
        sel_n = sb("sel_n", [SROWS, 32, P], BF16)
        mod = sb("mod", [P, 12, B])
        eps_c = sb("eps_c", [P, 1])
        zero64 = sb("zero64", [P, NE])

        x_a = sb("x_a", [P, TILES, D])
        x_res = sb("x_res", [P, TILES, D])
        st_a = sb("st_a", [P, TILES, 6])
        mv_a = sb("mv_a", [P, TILES, 2])
        sd_a = sb("sd_a", [P, TILES])
        rstd_a = sb("rstd_a", [P, TILES])
        h_a = sb("h_a", [P, TOK])
        k_t = sb("k_t", [KROWS, TOK])
        v_s = sb("v_s", [P, TILES, KROWS])
        q_all = sb("q_all", [P, 2 * NB, H, QB])
        q_st = q_all[0:QROWS]
        ke = sb("ke", [QROWS, NB, T])
        nmax = sb("nmax", [P, 2 * NB])
        rsum = sb("rsum", [P, 2 * NB])
        rinv = sb("rinv", [P, 2 * NB])
        probs = sb("probs", [P, 2, 2, T])
        probs_t = sb("probs_t", [P, 2, BPG, P])
        dg = h_a[:, :].rearrange("p (i c) -> p i c", i=BPG)
        ao_raw = sb("ao_raw", [P, 512])
        ao = q_all[:, 0:BPG].rearrange("p i h a -> p (i h a)").rearrange("p (i g a) -> p i g a", g=G, a=QB)
        y_a = sb("y_a", [P, TOK])
        xn_a = y_a[:, :].rearrange("p (t d) -> p t d", t=TILES)
        x1 = sb("x1", [P, TILES, D])

        x_b = sb("x_b", [P, TILES, D])
        st_b = sb("st_b", [P, TILES, 6])
        mv_b = sb("mv_b", [P, TILES, 2])
        sd_b = sb("sd_b", [P, TILES])
        rstd_b = sb("rstd_b", [P, TILES])
        h_b = sb("h_b", [P, TOK])
        y_b = sb("y_b", [P, TOK])
        xn_b = y_b[:, :].rearrange("p (t d) -> p t d", t=TILES)
        x_out = sb("x_out", [P, TILES, D])
        gate = sb("gate", [P, TILES, NE])
        score = sb("score", [P, TILES, NE])
        masked = sb("masked", [P, TILES, NE])
        picked = sb("picked", [P, TILES, NE])
        equal = sb("equal", [P, TILES, NE])
        prefix = sb("prefix", [P, TILES, NE])
        top8 = sb("top8", [P, TILES, 8])
        few = sb("few", [P, TILES])
        gmax = sb("gmax", [P, TILES, NG])
        beats = sb("beats", [P, TILES, NG, NG])
        ties = sb("ties", [P, TILES, NG, NG])
        grank = sb("grank", [P, TILES, NG])
        we96 = sb("we96", [P, TILES, SROWS])
        w_parts = sb("w_parts", [SROWS, TOK], BF16)
        bc_parts = sb("bc_parts", [SROWS, TOK], BF16)
        x_conv = sb("x_conv", [P, NH, TOK])
        z_gate = sb("z_gate", [P, NH, TOK])
        dt_s = sb("dt_s", [P, NH, TOK])
        dt_x = sb("dt_x", [P, NH, TOK])
        work = sb("work", [P, 6 * 1024 + 64])

        def cut(lo, n):
            return work[:, lo:lo + n]

        th = [cut(k * 512, 512) for k in range(2)]
        zh = [cut(1024 + k * 512, 512) for k in range(2)]
        rest = cut(2048, 512)
        w_rows = cut(2560, 512)
        x_pad = cut(0, NH * 2 * (T + KC - 1)).rearrange("p (h b t) -> p h b t", h=NH, b=2)
        PADW = NH * 2 * (T + KC - 1)
        acc = cut(PADW, 1024).rearrange("p (h t) -> p h t", h=NH)
        act_t = cut(PADW + 1024, 1024).rearrange("p (h t) -> p h t", h=NH)
        act_z = cut(PADW + 2048, 1024).rearrange("p (h t) -> p h t", h=NH)
        gz_t = cut(PADW + 3072, 1024).rearrange("p (h t) -> p h t", h=NH)
        sp_e = acc
        sp_l = act_t
        sp_u = act_z
        sp_r = gz_t
        bc_rest = x_pad.rearrange("p h b t -> p (h b t)")[:, 0:TOK]
        da = [cut(k * 1024, 1024).rearrange("p (h t) -> p h t", h=NH) for k in range(2)]
        ring = [cut(2048 + k * 1024, 1024).rearrange("p (h t) -> p h t", h=NH) for k in range(RING)]
        c_s = [cut(5120 + k * 512, 512) for k in range(2)]

        loaded = sem("loaded")
        cleared = sem("cleared")
        g0 = sem("g0")
        s_silu = sem("s_silu")
        s_mod = sem("s_mod")
        s_modv = sem("s_modv")
        s_nega = sem("s_nega")
        s_dtx = sem("s_dtx")
        s_m1 = sem("s_m1")
        s_m1c = sem("s_m1c")
        s_wc = sem("s_wc")

        wmod = probs_t[:, :, :, :].rearrange("p a b c -> p (a b c)")[:, 0:2 * 6 * D]
        c_t = x_out[:, 0, 0:2 * B]
        c_silu = x_out[:, 1, 0:2 * B]
        ffn_w_t, ffn_a1, ffn_a2, ffn_m1 = (x_b[:, k, :] for k in range(4))
        wx_dt = y_b[0:DTR, 0:DI]
        wdt_t = y_b[0:DTR, DI:2 * DI]
        sgn = y_a[:, 0:B]

        def flat(t):
            n = len(t.shape)
            return t[:, :] if n == 2 else t[:, :, :].rearrange("p a b -> p (a b)")

        loads = [("wq_rep", flat(wq_rep)), ("wk_t", flat(wk_t)), ("wv_t", flat(wv_t)), ("wo_x", flat(wo_x)),
                 ("e_shift", ke[KROWS:QROWS, :, :].rearrange("p a b -> p (a b)")), ("wg_t", flat(wg_t)),
                 ("w1_t", flat(w1_t)), ("w3_t", flat(w3_t)), ("w2_t", flat(w2_t)), ("b1_c", flat(b1_c)),
                 ("b3_c", flat(b3_c)), ("b2_r", flat(b2_r)), ("c_t", c_t), ("wmod", wmod), ("win_t", flat(win_t)),
                 ("conv_w", flat(conv_w)), ("conv_b", flat(conv_b)), ("wx_bc", flat(wx_bc)), ("wx_dt", wx_dt),
                 ("wdt_t", wdt_t), ("b_dt", flat(b_dt)), ("a_log", flat(neg_a)), ("d_par", flat(d_par)),
                 ("wout_t", flat(wout_t)), ("ffn_w_t", ffn_w_t), ("ffn_a1", ffn_a1), ("ffn_a2", ffn_a2),
                 ("ffn_b", flat(ffn_b)), ("ident", flat(ident)), ("mask_q", flat(mask_q)), ("mask_d", flat(mask_d)),
                 ("sel_r", flat(sel_r)), ("tie", flat(tie)), ("sel_n", flat(sel_n))]
        LOADED = 16 * (len(loads) + 1)

        def x_pair(p):
            return dram["x"][p].rearrange("(t q) d -> q t d", q=P)

        with nc.Block() as block:
            @block.sync
            def _(sp):
                for name, dst in loads:
                    sp.dma_start(dst, dram[name]).then_inc(loaded, 16)
                sp.dma_start(x_a[:, :, :], x_pair(0)).then_inc(loaded, 16)

            @block.gpsimd
            def _(pool):
                nc.gpsimd.memset(we96[:, :, :], 0.0)
                nc.gpsimd.memset(eps_c[:, :], EPS)
                nc.gpsimd.memset(zero64[:, :], 0.0)

            @block.tensor
            def _(pe):
                pe.wait_ge(loaded, LOADED)
                pe.wait_ge(s_silu, 1)
                for m in range(12):
                    last = nc.tensor.matmul(bank[0][:, m * B:(m + 1) * B], wmod[:, m * D:(m + 1) * D],
                                            c_silu[:, (m // 6) * B:(m // 6 + 1) * B], start=True, stop=True)
                last.then_inc(s_mod, 1)
                for k in range(NH):
                    last = nc.tensor.matmul(bank[1 + k][:, 0:DI], wx_dt[:, k * P:(k + 1) * P], wdt_t, start=True, stop=True)
                last.then_inc(s_dtx, 1)
                nc.tensor.matmul(bank[3][:, 0:D], ffn_a1, ffn_w_t, start=True, stop=True).then_inc(s_m1, 1)
                pe.wait_ge(s_m1c, 1)
                nc.tensor.matmul(bank[4][:, 0:D], ffn_m1, ffn_a2, start=True, stop=True).then_inc(s_wc, 1)

            @block.scalar
            def _(act):
                act.wait_ge(loaded, LOADED)
                nc.scalar.activation(c_silu, c_t, ACT.Silu).then_inc(s_silu, 1)
                nc.scalar.activation(neg_a[:, :], neg_a[:, :], ACT.Exp).then_inc(s_nega, 1)
                act.wait_ge(s_dtx, 1)
                for k in range(NH):
                    nc.scalar.activation(w_dtx[:, k, :], bank[1 + k][:, 0:DI], ACT.Copy)
                act.wait_ge(s_m1, 1)
                nc.scalar.activation(ffn_m1, bank[3][:, 0:D], ACT.Copy).then_inc(s_m1c, 1)
                act.wait_ge(s_wc, 1)
                nc.scalar.activation(ffn_w[:, :], bank[4][:, 0:D], ACT.Copy)

            @block.vector
            def _(dve):
                dve.wait_ge(loaded, LOADED)
                nc.vector.tensor_scalar(b1_c[:, :], b1_c[:, :], 0.5, None, ALU.mult)
                nc.vector.tensor_scalar(conv_b[:, :], conv_b[:, :], 0.5, None, ALU.mult)
                dve.wait_ge(s_nega, 1)
                nc.vector.tensor_scalar(neg_a[:, :], neg_a[:, :], -1.0, None, ALU.mult)
                dve.wait_ge(s_mod, 1)
                n = 0
                for m in range(12):
                    src = bank[0][:, m * B:(m + 1) * B]
                    if m % 6 in (SA, SB):
                        nc.vector.tensor_copy(mod[:, m, :], src)
                    elif m % 6 in (CA, CB):
                        nc.vector.tensor_scalar(mod[:, m, :], src, 1.0, None, ALU.add)
                    else:
                        nc.vector.tensor_scalar(sgn, src, 0.0, 2.0, ALU.is_ge, ALU.mult).then_inc(s_modv, 1)
                        nc.vector.tensor_scalar(mod[:, m, :], src, -1.0, None, ALU.mult).then_inc(s_modv, 1)
                        dve.wait_ge(s_modv, n + 2)
                        nc.vector.tensor_tensor(mod[:, m, :], mod[:, m, :], src, ALU.max).then_inc(s_modv, 1)
                        dve.wait_ge(s_modv, n + 3)
                        nc.vector.tensor_scalar(mod[:, m, :], mod[:, m, :], 0.25, None, ALU.max).then_inc(s_modv, 1)
                        n += 4
                        dve.wait_ge(s_modv, n)
                        nc.vector.scalar_tensor_tensor(mod[:, m, :], sgn, -1.0, mod[:, m, :], ALU.add, ALU.mult).then_inc(s_modv, 1)
                        n += 1
                        dve.wait_ge(s_modv, n)

        xa_next, xr_in = sem("xa_next"), sem("xr_in")
        ke_in = [sem(f"ke_in{q}") for q in range(PIECES)]
        a_st, a_mv, a_sd, a_rstd, a_xn, a_tr, a_h = (sem("a_" + n) for n in ("st", "mv", "sd", "rstd", "xn", "tr", "h"))
        b_st, b_mv, b_sd, b_rstd, b_xn, b_tr, b_h = (sem("b_" + n) for n in ("st", "mv", "sd", "rstd", "xn", "tr", "h"))
        a_k, a_kc, a_v, a_vc, a_q, a_qm = (sem("a_" + n) for n in ("k", "kc", "v", "vc", "q", "qm"))
        a_s, a_max, a_exp, a_t, a_tc, a_pv, a_ao, a_inv, a_dg, a_r, a_on = (
            sem("a_" + n) for n in ("s", "max", "exp", "t", "tc", "pv", "ao", "inv", "dg", "r", "on"))
        a_wo, a_y, a_back, a_res = (sem("a_" + n) for n in ("wo", "y", "back", "res"))
        m_logit, m_exp, m_ch, m_we, m_wt, m_cp, m_rest, m_mid, m_parts = (
            sem("m_" + n) for n in ("logit", "exp", "ch", "we", "wt", "cp", "rest", "mid", "parts"))
        m_h1, m_h3, m_wb, m_tz, m_a, m_b, m_hh, m_w2 = (sem("m_" + n) for n in ("h1", "h3", "wb", "tz", "a", "b", "hh", "w2"))
        b_y, b_back, b_x = sem("b_y"), sem("b_back"), sem("b_x")
        s_xz, s_xp, s_pad, s_z, s_zg, s_cv, s_ct, s_xc, s_bc, s_bcc, s_bcr, s_bcm, s_bcp = (
            sem("s_" + n) for n in ("xz", "xp", "pad", "z", "zg", "cv", "ct", "xc", "bc", "bcc", "bcr", "bcm", "bcp"))
        s_dtp, s_sp1, s_sp2, s_sp3, s_spv, s_dt = (sem("s_" + n) for n in ("dtp", "sp1", "sp2", "sp3", "spv", "dt"))
        s_bb, s_cb, s_da, s_cs, s_dbx, s_h, s_hc, s_y, s_g, s_yv, s_o = (
            sem("s_" + n) for n in ("bb", "cb", "da", "cs", "dbx", "h", "hc", "y", "g", "yv", "o"))
        f_m, f_t, f_g, f_x, o_out = sem("f_m"), sem("f_t"), sem("f_g"), sem("f_x"), sem("o_out")
        numbers = sorted(s.num for s in sems)
        assert numbers == list(range(numbers[0], numbers[0] + len(sems)))

        def clear_semaphores():
            with nc.Block() as block:
                @block.sync
                def _(sp):
                    sp.sem_clear(range(numbers[0], numbers[-1] + 1))

        clear_semaphores()

        LN_A = dict(st=st_a, mv=mv_a, sd=sd_a, rstd=rstd_a, xn=xn_a, h=h_a, s_st=a_st, s_mv=a_mv, s_sd=a_sd,
                    s_rstd=a_rstd, s_xn=a_xn, s_tr=a_tr, s_h=a_h)
        LN_B = dict(st=st_b, mv=mv_b, sd=sd_b, rstd=rstd_b, xn=xn_b, h=h_b, s_st=b_st, s_mv=b_mv, s_sd=b_sd,
                    s_rstd=b_rstd, s_xn=b_xn, s_tr=b_tr, s_h=b_h)

        def scale_of(m, p, b):
            return mod[:, m, bass.ds(2 * p + b, 1)]

        def half(ap, b):
            return ap[:, b * T:(b + 1) * T]

        def tile(ap, t):
            return ap[:, t * P:(t + 1) * P]

        def ln_vector(dve, L, x, n):
            for t in range(TILES):
                last = nc.vector.bn_stats(L["st"][:, t, :], x[:, t, :])
            last.then_inc(L["s_st"], 1)
            dve.wait_ge(L["s_st"], n)
            for t in range(TILES):
                last = nc.vector.bn_aggr(L["mv"][:, t, :], L["st"][:, t, :])
            last.then_inc(L["s_mv"], 1)
            dve.wait_ge(L["s_sd"], n)
            nc.vector.reciprocal(L["rstd"][:, :], L["sd"][:, :]).then_inc(L["s_rstd"], 1)
            dve.wait_ge(L["s_rstd"], n)
            for t in range(TILES):
                last = nc.vector.tensor_scalar(L["xn"][:, t, :], x[:, t, :], L["mv"][:, t, 0:1], L["rstd"][:, t:t + 1],
                                               ALU.subtract, ALU.mult)
            last.then_inc(L["s_xn"], 1)

        def ln_std_scalar(act, L, n):
            act.wait_ge(L["s_mv"], n)
            nc.scalar.activation(L["sd"][:, :], L["mv"][:, :, 1], ACT.Sqrt, bias=eps_c[:, :]).then_inc(L["s_sd"], 1)

        def ln_out_scalar(act, L, p, shift, scale, src, n):
            act.wait_ge(L["s_tr"], n)
            for b in range(2):
                last = nc.scalar.activation(half(L["h"], b), half(src, b), ACT.Identity, bias=scale_of(shift, p, b),
                                            scale=scale_of(scale, p, b))
            last.then_inc(L["s_h"], 1)

        def ln_tensor(pe, L, dst, n):
            pe.wait_ge(L["s_xn"], n)
            for t in range(TILES):
                last = nc.tensor.transpose(tile(dst, t), L["xn"][:, t, :], ident[:, :])
            last.then_inc(L["s_tr"], 1)

        def gate_scalar(src, y, p, m, done):
            for b in range(2):
                last = nc.scalar.activation(half(y, b), half(src, b), ACT.Identity, bias=0.0, scale=scale_of(m, p, b))
            last.then_inc(done, 1)

        def back_tensor(y, dst, done):
            for t in range(TILES):
                last = nc.tensor.transpose(tile(dst, t), tile(y, t), ident[:, :])
            last.then_inc(done, 1)

        def tokens(ap):
            return ap.rearrange("p (t d) -> p t d", t=TILES)

        def a_start_vector(dve):
            ln_vector(dve, LN_A, x_a, 1)

        def a_start_tensor(pe):
            ln_tensor(pe, LN_A, bank[0], 1)
            pe.wait_ge(a_h, 1)
            nc.tensor.matmul(bank[1][0:KROWS, :], wk_t[:, :], h_a[:, :], start=True, stop=True).then_inc(a_k, 1)
            for t in range(TILES):
                last = nc.tensor.matmul(tile(bank[0], t), tile(h_a, t), wv_t[:, :], start=True, stop=True)
            last.then_inc(a_v, 1)

        def a_start_scalar(act, p):
            ln_std_scalar(act, LN_A, 1)
            ln_out_scalar(act, LN_A, p, SA, CA, bank[0], 1)
            act.wait_ge(a_k, 1)
            nc.scalar.activation(k_t[:, :], bank[1][0:KROWS, :], ACT.Copy).then_inc(a_kc, 1)
            act.wait_ge(a_v, 1)
            nc.scalar.activation(v_s[:, :, :], tokens(bank[0])[:, :, 0:KROWS], ACT.Copy).then_inc(a_vc, 1)

        def a_loads_sync(sp, p):
            sp.dma_start(x_res[:, :, :], x_pair(p)).then_inc(xr_in, 16)
            sp.wait_ge(a_xn, 1)
            sp.dma_start(x_a[:, :, :], x_pair(p + 1)).then_inc(xa_next, 16)
            sp.wait_ge(a_kc, 1)
            for b in range(2):
                for q in range(PIECES):
                    if b:
                        sp.wait_ge(a_s, CHUNKS // 2 // PIECES * (q + 1))
                    n = NB // PIECES
                    sp.dma_start(ke[0:KROWS, q * n:(q + 1) * n, :],
                                 half(k_t, b).unsqueeze(1).broadcast_to([KROWS, n, T])).then_inc(ke_in[q], 16)

        def a_query_tensor(pe, h):
            if h == 0:
                pe.wait_ge(a_vc, 1)
            elif h == 1:
                pe.wait_ge(a_kc, 1)
            else:
                pe.wait_ge(a_qm, h - 1)
            nc.tensor.matmul(bank[h % 2][0:QROWS, :], wq_rep[:, h, :], h_a[:, :], start=True, stop=True).then_inc(a_q, 1)

        def a_query_vector(dve, h):
            dve.wait_ge(a_q, h + 1)
            m = mask_q[:, h // (H // G), :].unsqueeze(1).broadcast_to([QROWS, 2 * NB, QB])
            nc.vector.tensor_tensor(q_st[:, :, h, :], bank[h % 2][0:QROWS, :].rearrange("p (i a) -> p i a", a=QB),
                                    m, ALU.mult).then_inc(a_qm, 1)

        def a_chunk_tensor(pe, c):
            if c < CHUNKS:
                if c == 0:
                    pe.wait_ge(a_qm, H)
                b, i0 = c // (CHUNKS // 2), 2 * (c % (CHUNKS // 2))
                q = i0 // (NB // PIECES)
                pe.wait_ge(ke_in[q], 16 * (b + 1))
                if c >= 2:
                    pe.wait_ge(a_exp, c - 1)
                for k in range(2):
                    last = nc.tensor.matmul(bank[c % 2][:, k * T:(k + 1) * T],
                                            q_st[:, 2 * c + k, :, :].rearrange("p h a -> p (h a)"), ke[:, i0 + k, :],
                                            start=True, stop=True)
                last.then_inc(a_s, 1)
            if c >= 2 and (c - 1) % CPG == 0:
                a_values_tensor(pe, (c - 2) // CPG)
            c -= 1
            if 0 <= c < CHUNKS:
                pe.wait_ge(a_exp, c + 1)
                if c:
                    pe.wait_ge(a_tc, c)
                if c and c % CPG == 0:
                    pe.wait_ge(a_on, c // CPG)
                for kh in range(2):
                    for k in range(2):
                        last = nc.tensor.transpose(tile(bank[2], 2 * kh + k), probs[:, c % 2, k, kh * P:(kh + 1) * P],
                                                   ident[:, :])
                last.then_inc(a_t, 1)

        def a_values_tensor(pe, g):
            pe.wait_ge(a_tc, CPG * (g + 1))
            if g:
                pe.wait_ge(a_ao, g)
            pt = probs_t[:, :, :, :].rearrange("p k i (g r a) -> p k i g r a", g=G, r=H // G)
            for kh in range(2):
                for r in range(H // G):
                    last = nc.tensor.matmul(
                        bank[3][32 * r:32 * r + 32, :].rearrange("p (i g a) -> p i g a", g=G, a=QB),
                        v_s[:, 2 * (g // 2) + kh, :], pt[:, kh, :, :, r, :], start=(kh == 0), stop=(kh == 1))
            last.then_inc(a_pv, 1)
            pe.wait_ge(a_dg, g + 1)
            nc.tensor.matmul(bank[2][:, :], sel_r[:, :], h_a[:, :],
                             start=True, stop=True).then_inc(a_r, 1)

        def a_chunk_vector(dve, c):
            if c < CHUNKS:
                dve.wait_ge(a_s, c + 1)
                nc.vector.tensor_reduce(nmax[:, 2 * c:2 * c + 2], bank[c % 2][:, :].rearrange("p (k t) -> p k t", k=2),
                                        AX_X, ALU.max, negate=True).then_inc(a_max, 1)
            if c >= 2 and (c - 1) % CPG == 0:
                g = (c - 2) // CPG
                dve.wait_ge(a_exp, CPG * (g + 1))
                cols = slice(BPG * g, BPG * (g + 1))
                nc.vector.reciprocal(rinv[:, cols], rsum[:, cols]).then_inc(a_inv, 1)
                dve.wait_ge(a_inv, g + 1)
                if g:
                    dve.wait_ge(a_r, g)
                nc.vector.tensor_tensor(dg[:, :, :], rinv[:, cols].unsqueeze(2).broadcast_to([P, BPG, G * QB]),
                                        mask_d[:, :].unsqueeze(1).broadcast_to([P, BPG, G * QB]), ALU.mult).then_inc(a_dg, 1)
                dve.wait_ge(a_ao, g + 1)
                dve.wait_ge(a_r, g + 1)
                nc.vector.tensor_tensor(ao[:, cols, :, :].rearrange("p i g a -> p (i g a)"), ao_raw[:, :], bank[2][:, :],
                                        ALU.mult).then_inc(a_on, 1)

        def a_chunk_scalar(act, c):
            if c < CHUNKS:
                act.wait_ge(a_max, c + 1)
                if c >= 2:
                    act.wait_ge(a_t, c - 1)
                for k in range(2):
                    i = 2 * c + k
                    last = nc.scalar.activation(probs[:, c % 2, k, :], bank[c % 2][:, k * T:(k + 1) * T], ACT.Exp,
                                                bias=nmax[:, i:i + 1], accum_out=rsum[:, i:i + 1])
                last.then_inc(a_exp, 1)
            if c >= 2 and (c - 1) % CPG == 0:
                g = (c - 2) // CPG
                act.wait_ge(a_pv, g + 1)
                if g:
                    act.wait_ge(a_on, g)
                nc.scalar.activation(ao_raw[:, :], bank[3][:, :], ACT.Copy).then_inc(a_ao, 1)
            c -= 1
            if 0 <= c < CHUNKS:
                act.wait_ge(a_t, c + 1)
                i0 = 2 * (c % CPG)
                nc.scalar.activation(probs_t[:, :, i0:i0 + 2, :].rearrange("p k i c -> p k (i c)"),
                                     bank[2][:, :].rearrange("p (k c) -> p k c", k=2), ACT.Copy).then_inc(a_tc, 1)

        def a_end_tensor(pe):
            pe.wait_ge(a_on, GROUPS)
            for g in range(G):
                last = nc.tensor.matmul(bank[3][:, :].rearrange("p (i a) -> p i a", a=QB), wo_x[:, g, :], ao[:, :, g, :],
                                        start=(g == 0), stop=(g == G - 1))
            last.then_inc(a_wo, 1)
            pe.wait_ge(a_y, 1)
            back_tensor(y_a, bank[2], a_back)

        def a_end_scalar(act, p):
            act.wait_ge(a_wo, 1)
            gate_scalar(bank[3], y_a, p, GA, a_y)

        def a_end_vector(dve, with_b):
            dve.wait_ge(a_back, 1)
            dve.wait_ge(xr_in, 16)
            if with_b:
                dve.wait_ge(b_x, 1)
            nc.vector.tensor_tensor(x1[:, :, :], x_res[:, :, :], tokens(bank[2]), ALU.add).then_inc(a_res, 1)

        def m_start_tensor(pe):
            ln_tensor(pe, LN_B, bank[4], 1)
            pe.wait_ge(b_h, 1)
            for t in range(TILES):
                last = nc.tensor.matmul(tile(bank[5], t), tile(h_b, t), wg_t[:, :], start=True, stop=True)
            last.then_inc(m_logit, 1)

        def m_route_tensor(pe):
            pe.wait_ge(m_we, 1)
            for t in range(TILES):
                last = nc.tensor.transpose(tile(bank[6], t)[0:SROWS, :], we96[:, t, :], ident[:, :])
            last.then_inc(m_wt, 1)
            m_up_tensor(pe, 0)

        def m_start_scalar(act, p):
            ln_std_scalar(act, LN_B, 1)
            ln_out_scalar(act, LN_B, p, SB, CB, bank[4], 1)
            act.wait_ge(m_logit, 1)
            nc.scalar.activation(gate[:, :, :], tokens(bank[5])[:, :, 0:NE], ACT.Exp, scale=-1.0).then_inc(m_exp, 1)

        def split_scalar(act, src, keep, parts, rest_ap, ready, s_cp, s_rest, s_mid):
            act.wait_ge(ready, 1)
            last = nc.scalar.activation(parts[:, :], src[0:SROWS, :], ACT.Copy)
            if keep is not None:
                last = nc.scalar.activation(keep[0:SROWS, :], src[0:SROWS, :], ACT.Copy)
            last.then_inc(s_cp, 1)
            act.wait_ge(s_rest, 1)
            for k in range(1, PARTS):
                last = nc.scalar.activation(parts[32 * k:32 * k + 32, :], rest_ap[32 * k:32 * k + 32, :], ACT.Copy)
            last.then_inc(s_mid, 1)

        def split_vector(dve, src, parts, rest_ap, s_cp, s_rest, s_mid, s_done):
            dve.wait_ge(s_cp, 1)
            nc.vector.tensor_tensor(rest_ap[0:SROWS, :], src[0:SROWS, :], parts[:, :], ALU.subtract).then_inc(s_rest, 1)
            dve.wait_ge(s_mid, 1)
            nc.vector.tensor_tensor(parts[64:96, :], rest_ap[64:96, :], parts[64:96, :], ALU.subtract).then_inc(s_done, 1)

        def m_route_vector(dve):
            n = [0]

            def link(ins):
                n[0] += 1
                ins.then_inc(m_ch, 1)
                dve.wait_ge(m_ch, n[0])

            dve.wait_ge(m_exp, 1)
            link(nc.vector.tensor_scalar(gate[:, :, :], gate[:, :, :], 1.0, None, ALU.add))
            link(nc.vector.reciprocal(score[:, :, :], gate[:, :, :]))
            by_group = [P, TILES, NG, NG]
            link(nc.vector.tensor_reduce(gmax[:, :, :], score[:, :, :].rearrange("p t (g k) -> p t g k", g=NG), AX_X, ALU.max))
            other, own = gmax[:, :, :].unsqueeze(2).broadcast_to(by_group), gmax[:, :, :].unsqueeze(3).broadcast_to(by_group)
            nc.vector.tensor_tensor(beats[:, :, :, :], other, own, ALU.is_gt)
            link(nc.vector.tensor_tensor(ties[:, :, :, :], other, own, ALU.is_equal))
            fl = "p t j i -> p t (j i)"
            link(nc.vector.tensor_tensor(ties[:, :, :, :].rearrange(fl), ties[:, :, :, :].rearrange(fl),
                                         tie[:, :].unsqueeze(1).broadcast_to([P, TILES, NG * NG]), ALU.mult))
            link(nc.vector.tensor_tensor(beats[:, :, :, :], beats[:, :, :, :], ties[:, :, :, :], ALU.add))
            link(nc.vector.tensor_reduce(grank[:, :, :], beats[:, :, :, :], AX_X, ALU.add))
            link(nc.vector.tensor_scalar(grank[:, :, :], grank[:, :, :], TOPG - 0.5, None, ALU.is_lt))
            open_ = grank[:, :, :].rearrange("p t g -> p (t g)").unsqueeze(2).broadcast_to([P, TILES * NG, NE // NG])
            flg = "p t (g k) -> p (t g) k"
            link(nc.vector.tensor_tensor(masked[:, :, :].rearrange(flg, g=NG), score[:, :, :].rearrange(flg, g=NG), open_, ALU.mult))
            link(nc.vector.scalar_tensor_tensor(masked[:, :, :].rearrange(flg, g=NG), open_, -1.0,
                                                masked[:, :, :].rearrange(flg, g=NG), ALU.add, ALU.add))
            for t in range(TILES):
                last = nc.vector.max(top8[:, t, :], masked[:, t, :])
            link(last)
            fourth = top8[:, :, TOPK - 1:TOPK].broadcast_to([P, TILES, NE])
            nc.vector.tensor_tensor(picked[:, :, :], masked[:, :, :], fourth, ALU.is_gt)
            link(nc.vector.tensor_tensor(equal[:, :, :], masked[:, :, :], fourth, ALU.is_equal))
            for t in range(TILES):
                nc.vector.tensor_tensor_scan(prefix[:, t, :], equal[:, t, :], zero64[:, :], 0.0, ALU.add, ALU.add)
            link(nc.vector.tensor_reduce(few[:, :], picked[:, :, :], AX_X, ALU.add))
            link(nc.vector.tensor_tensor(prefix[:, :, :], prefix[:, :, :], few[:, :].unsqueeze(2).broadcast_to([P, TILES, NE]), ALU.add))
            link(nc.vector.scalar_tensor_tensor(equal[:, :, :], prefix[:, :, :], TOPK + 0.5, equal[:, :, :], ALU.is_lt, ALU.mult))
            link(nc.vector.tensor_tensor(picked[:, :, :], picked[:, :, :], equal[:, :, :], ALU.add))
            link(nc.vector.tensor_tensor(picked[:, :, :], picked[:, :, :], score[:, :, :], ALU.mult))
            link(nc.vector.tensor_reduce(few[:, :], picked[:, :, :], AX_X, ALU.add))
            link(nc.vector.reciprocal(few[:, :], few[:, :]))
            link(nc.vector.tensor_scalar(few[:, :], few[:, :], ROUTE_SCALE, None, ALU.mult))
            for k in range(PARTS):
                last = nc.vector.tensor_tensor(we96[:, :, 32 * k:32 * k + NE], picked[:, :, :],
                                               few[:, :].unsqueeze(2).broadcast_to([P, TILES, NE]), ALU.mult)
            last.then_inc(m_we, 1)
            split_vector(dve, bank[6], w_parts, rest, m_cp, m_rest, m_mid, m_parts)

        def m_route_scalar(act):
            split_scalar(act, bank[6], w_rows, w_parts, rest, m_wt, m_cp, m_rest, m_mid)

        UP1, UP3 = (2, 4), (3, 5)

        def m_up_tensor(pe, e):
            if e >= 2:
                pe.wait_ge(m_hh, e - 1)
            nc.tensor.matmul(bank[UP1[e % 2]][:, :], w1_t[:, e, :], h_b[:, :], start=True, stop=True).then_inc(m_h1, 1)
            nc.tensor.matmul(bank[UP3[e % 2]][:, :], w3_t[:, e, :], h_b[:, :], start=True, stop=True).then_inc(m_h3, 1)

        def m_down_tensor(pe, e):
            pe.wait_ge(m_hh, e + 1)
            nc.tensor.matmul(bank[7][:, :], w2_t[:, e, :], zh[e % 2], start=False, stop=(e == NE - 1)).then_inc(m_w2, 1)

        def m_expert_tensor(pe, e):
            if e == 0:
                pe.wait_ge(m_parts, 1)
                nc.tensor.matmul(bank[7][:, :], b2_r[:, :], w_rows[0:SROWS, :], start=True, stop=False)
            else:
                pe.wait_ge(m_hh, e)
            nc.tensor.matmul(bank[6][:, :], sel_n[:, e, :], w_parts[:, :], start=True, stop=True).then_inc(m_wb, 1)
            if e + 1 < NE:
                m_up_tensor(pe, e + 1)
            if e:
                m_down_tensor(pe, e - 1)

        def m_expert_scalar(act, e):
            act.wait_ge(m_h1, e + 1)
            if e >= 2:
                act.wait_ge(m_w2, e - 1)
            src = bank[UP1[e % 2]][:, :]
            nc.scalar.activation(th[e % 2], src, ACT.Tanh, bias=b1_c[:, e:e + 1], scale=0.5)
            nc.scalar.activation(zh[e % 2], src, ACT.Identity, bias=b1_c[:, e:e + 1], scale=0.5).then_inc(m_tz, 1)

        def m_expert_vector(dve, e):
            dve.wait_ge(m_tz, e + 1)
            nc.vector.scalar_tensor_tensor(zh[e % 2], th[e % 2], 1.0, zh[e % 2], ALU.add, ALU.mult).then_inc(m_a, 1)
            dve.wait_ge(m_h3, e + 1)
            dve.wait_ge(m_a, e + 1)
            nc.vector.scalar_tensor_tensor(zh[e % 2], bank[UP3[e % 2]][:, :], b3_c[:, e:e + 1], zh[e % 2], ALU.add,
                                           ALU.mult).then_inc(m_b, 1)
            dve.wait_ge(m_wb, e + 1)
            dve.wait_ge(m_b, e + 1)
            nc.vector.tensor_tensor(zh[e % 2], zh[e % 2], bank[6][:, :], ALU.mult).then_inc(m_hh, 1)

        def m_end_tensor(pe):
            m_down_tensor(pe, NE - 1)
            pe.wait_ge(b_y, 1)
            back_tensor(y_b, bank[4], b_back)

        def m_end_scalar(act, p):
            act.wait_ge(m_w2, NE)
            gate_scalar(bank[7], y_b, p, GB, b_y)

        def m_end_vector(dve):
            dve.wait_ge(b_back, 1)
            nc.vector.tensor_tensor(x_b[:, :, :], x1[:, :, :], tokens(bank[4]), ALU.add).then_inc(b_x, 1)
            dve.wait_ge(b_x, 1)
            ln_vector(dve, LN_B, x_b, 2)

        def s_in_tensor(pe):
            pe.wait_ge(b_h, 2)
            for k in range(4):
                nc.tensor.matmul(bank[4 + k][:, :], win_t[:, k * P:(k + 1) * P], h_b[:, :], start=True, stop=True).then_inc(s_xz, 1)

        def s_in_scalar(act):
            act.wait_ge(s_pad, 1)
            for h in range(NH):
                act.wait_ge(s_xz, h + 1)
                nc.scalar.activation(x_pad[:, h, :, KC - 1:], bank[4 + h][:, :].rearrange("p (b t) -> p b t", b=2),
                                     ACT.Copy).then_inc(s_xp, 1)

        def s_z_scalar(act):
            for h in range(NH):
                act.wait_ge(s_xz, NH + h + 1)
                nc.scalar.activation(gz_t[:, h, :], bank[6 + h][:, :], ACT.Tanh, scale=0.5)
                nc.scalar.activation(z_gate[:, h, :], bank[6 + h][:, :], ACT.Copy, scale=0.5).then_inc(s_z, 1)

        def s_pad_vector(dve):
            dve.wait_ge(m_w2, NE)
            nc.vector.memset(x_pad[:, :, :, 0:KC - 1], 0.0).then_inc(s_pad, 1)

        def s_conv_vector(dve, h):
            dve.wait_ge(s_xp, h + 1)
            a = acc[:, h, :].rearrange("p (b t) -> p b t", b=2)
            for k in range(KC):
                tap = x_pad[:, h, :, k:k + T]
                if k == 0:
                    ins = nc.vector.tensor_scalar(a, tap, conv_w[:, h, k:k + 1], None, ALU.mult)
                else:
                    dve.wait_ge(s_cv, KC * h + k)
                    ins = nc.vector.scalar_tensor_tensor(a, tap, conv_w[:, h, k:k + 1], a, ALU.mult, ALU.add)
                ins.then_inc(s_cv, 1)

        def s_conv_scalar(act, h):
            act.wait_ge(s_cv, KC * (h + 1))
            nc.scalar.activation(act_t[:, h, :], acc[:, h, :], ACT.Tanh, bias=conv_b[:, h:h + 1], scale=0.5)
            nc.scalar.activation(act_z[:, h, :], acc[:, h, :], ACT.Identity, bias=conv_b[:, h:h + 1], scale=0.5).then_inc(s_ct, 1)

        def s_gate_vector(dve, h):
            dve.wait_ge(s_ct, h + 1)
            nc.vector.scalar_tensor_tensor(x_conv[:, h, :], act_t[:, h, :], 1.0, act_z[:, h, :], ALU.add, ALU.mult).then_inc(s_xc, 1)

        def s_zgate_vector(dve):
            dve.wait_ge(s_z, NH)
            nc.vector.scalar_tensor_tensor(z_gate[:, :, :], gz_t[:, :, :], 1.0, z_gate[:, :, :], ALU.add, ALU.mult).then_inc(s_zg, 1)

        def s_proj_tensor(pe):
            pe.wait_ge(s_xc, NH)
            for k in range(NH):
                last = nc.tensor.matmul(bank[4][0:SROWS, :], wx_bc[:, k, :], x_conv[:, k, :], start=(k == 0), stop=(k == NH - 1))
            last.then_inc(s_bc, 1)
            pe.wait_ge(s_z, 1)
            for h in range(NH):
                for k in range(NH):
                    last = nc.tensor.matmul(bank[5 + h][:, :], w_dtx[:, k, h * P:(h + 1) * P], x_conv[:, k, :],
                                            start=(k == 0), stop=(k == NH - 1))
                last.then_inc(s_dtp, 1)

        def s_parts_scalar(act):
            split_scalar(act, bank[4], None, bc_parts, bc_rest, s_bc, s_bcc, s_bcr, s_bcm)

        def s_parts_vector(dve):
            split_vector(dve, bank[4], bc_parts, bc_rest, s_bcc, s_bcr, s_bcm, s_bcp)

        def s_step_scalar(act):
            act.wait_ge(s_zg, 1)
            for h in range(NH):
                act.wait_ge(s_dtp, h + 1)
                nc.scalar.activation(sp_e[:, h, :], bank[5 + h][:, :], ACT.Abs, bias=b_dt[:, h:h + 1])
                nc.scalar.activation(sp_r[:, h, :], bank[5 + h][:, :], ACT.Relu, bias=b_dt[:, h:h + 1]).then_inc(s_sp1, 1)
            act.wait_ge(s_sp1, NH)
            nc.scalar.activation(sp_e[:, :, :], sp_e[:, :, :], ACT.Exp, scale=-1.0).then_inc(s_sp2, 1)
            act.wait_ge(s_sp2, 1)
            nc.scalar.activation(sp_l[:, :, :], sp_e[:, :, :], ACT.Ln, bias=1.0).then_inc(s_sp3, 1)

        def s_step_vector(dve):
            dve.wait_ge(s_sp2, 1)
            nc.vector.tensor_scalar(sp_u[:, :, :], sp_e[:, :, :], 1.0, None, ALU.add).then_inc(s_spv, 1)
            dve.wait_ge(s_spv, 1)
            nc.vector.scalar_tensor_tensor(sp_u[:, :, :], sp_u[:, :, :], 1.0, sp_e[:, :, :], ALU.subtract, ALU.subtract).then_inc(s_spv, 1)
            dve.wait_ge(s_spv, 2)
            nc.vector.tensor_tensor(sp_r[:, :, :], sp_r[:, :, :], sp_u[:, :, :], ALU.subtract).then_inc(s_spv, 1)
            dve.wait_ge(s_spv, 3)
            dve.wait_ge(s_sp3, 1)
            nc.vector.tensor_tensor(dt_s[:, :, :], sp_r[:, :, :], sp_l[:, :, :], ALU.add).then_inc(s_dt, 1)
            dve.wait_ge(s_dt, 1)
            nc.vector.tensor_tensor(dt_x[:, :, :], dt_s[:, :, :], x_conv[:, :, :], ALU.mult).then_inc(s_dt, 1)

        def s_rows_tensor(pe, n):
            if n == 0:
                pe.wait_ge(s_bcp, 1)
                pe.wait_ge(s_sp1, NH)
            else:
                pe.wait_ge(s_dbx, n)
                pe.wait_ge(s_cs, n)
            nc.tensor.matmul(bank[4][:, :], sel_n[:, n, :], bc_parts[:, :], start=True, stop=True).then_inc(s_bb, 1)
            nc.tensor.matmul(bank[5][:, :], sel_n[:, NS + n, :], bc_parts[:, :], start=True, stop=True).then_inc(s_cb, 1)

        def s_sum_tensor(pe, n):
            pe.wait_ge(s_hc, n + 1)
            for h in range(NH):
                last = nc.tensor.matmul(bank[6 + h][:, :], ident[:, :], ring[n % RING][:, h, :], start=(n == 0), stop=(n == NS - 1))
            last.then_inc(s_y, 1)

        def s_decay_scalar(act, n):
            act.wait_ge(s_dt, 2)
            if n >= 2:
                act.wait_ge(s_h, n - 1)
            for h in range(NH):
                last = nc.scalar.activation(da[n % 2][:, h, :], dt_s[:, h, :], ACT.Exp, scale=neg_a[:, h * NS + n:h * NS + n + 1])
            last.then_inc(s_da, 1)
            act.wait_ge(s_cb, n + 1)
            if n >= 2:
                act.wait_ge(s_hc, n - 1)
            nc.scalar.activation(c_s[n % 2], bank[5][:, :], ACT.Copy).then_inc(s_cs, 1)

        def s_scan_vector(dve, n):
            dve.wait_ge(s_bb, n + 1)
            if n == 0:
                dve.wait_ge(s_dt, 2)
            if n >= RING:
                dve.wait_ge(s_y, n - RING + 1)
            r = ring[n % RING]
            nc.vector.tensor_tensor(r, dt_x[:, :, :], bank[4][:, :].unsqueeze(1).broadcast_to([P, NH, TOK]), ALU.mult).then_inc(s_dbx, 1)
            dve.wait_ge(s_dbx, n + 1)
            dve.wait_ge(s_da, n + 1)
            for h in range(NH):
                for b in range(2):
                    last = nc.vector.tensor_tensor_scan(half(r[:, h, :], b), half(da[n % 2][:, h, :], b), half(r[:, h, :], b),
                                                        0.0, ALU.mult, ALU.add)
            last.then_inc(s_h, 1)

        def s_read_gpsimd(pool, n):
            pool.wait_ge(s_h, n + 1)
            pool.wait_ge(s_cs, n + 1)
            r = ring[n % RING]
            nc.gpsimd.tensor_tensor(r, r, c_s[n % 2].unsqueeze(1).broadcast_to([P, NH, TOK]), ALU.mult).then_inc(s_hc, 1)

        def s_end_vector(dve):
            dve.wait_ge(s_y, NS)
            for h in range(NH):
                last = nc.vector.tensor_tensor(z_gate[:, h, :], z_gate[:, h, :], bank[6 + h][:, :], ALU.mult)
            last.then_inc(s_g, 1)
            dve.wait_ge(s_g, 1)
            for h in range(NH):
                last = nc.vector.scalar_tensor_tensor(z_gate[:, h, :], x_conv[:, h, :], d_par[:, h:h + 1], z_gate[:, h, :],
                                                      ALU.mult, ALU.add)
            last.then_inc(s_yv, 1)

        def s_end_tensor(pe):
            pe.wait_ge(s_yv, 1)
            for k in range(NH):
                last = nc.tensor.matmul(bank[4][:, :], wout_t[:, k, :], z_gate[:, k, :], start=(k == 0), stop=(k == NH - 1))
            last.then_inc(s_o, 1)

        def s_gate_scalar(act, p):
            act.wait_ge(s_o, 1)
            gate_scalar(bank[4], y_b, p, 6 + GA, b_y)

        def s_back_tensor(pe):
            pe.wait_ge(b_y, 2)
            back_tensor(y_b, bank[5], b_back)

        def s_res_vector(dve):
            dve.wait_ge(b_back, 2)
            nc.vector.tensor_tensor(x_b[:, :, :], x_b[:, :, :], tokens(bank[5]), ALU.add).then_inc(b_x, 1)
            dve.wait_ge(b_x, 2)
            ln_vector(dve, LN_B, x_b, 3)

        def f_tensor(pe):
            pe.wait_ge(b_h, 3)
            nc.tensor.matmul(bank[5][:, :], ffn_w[:, :], h_b[:, :], start=True, stop=True).then_inc(f_m, 1)

        def f_scalar(act, p):
            act.wait_ge(f_m, 1)
            nc.scalar.activation(y_b[:, :], bank[5][:, :], ACT.Tanh, bias=ffn_b[:, :]).then_inc(f_t, 1)

        def f_gate_vector(dve, p):
            dve.wait_ge(f_t, 1)
            for b in range(2):
                last = nc.vector.tensor_scalar(half(y_b, b), half(y_b, b), scale_of(6 + GB, p, b), None, ALU.mult)
            last.then_inc(f_g, 1)

        def f_back_tensor(pe):
            pe.wait_ge(f_g, 1)
            back_tensor(y_b, bank[6], b_back)

        def f_res_vector(dve):
            dve.wait_ge(b_back, 3)
            nc.vector.tensor_tensor(x_out[:, :, :], x_b[:, :, :], tokens(bank[6]), ALU.add).then_inc(f_x, 1)

        BEFORE, AFTER = 8, 8
        assert BEFORE + NS + AFTER == CHUNKS
        SCANNED = BEFORE + NS

        def beside_tensor(pe, c):
            if c == 0:
                m_end_tensor(pe)
            elif c == 2:
                ln_tensor(pe, LN_B, bank[4], 2)
                s_in_tensor(pe)
            elif c == 6:
                s_proj_tensor(pe)
            elif c == BEFORE - 1:
                s_rows_tensor(pe, 0)
            elif BEFORE <= c < SCANNED:
                if c + 1 < SCANNED:
                    s_rows_tensor(pe, c - BEFORE + 1)
                if c > BEFORE:
                    s_sum_tensor(pe, c - BEFORE - 1)
            elif c == SCANNED:
                s_sum_tensor(pe, NS - 1)
            elif c == SCANNED + 1:
                s_end_tensor(pe)
            elif c == SCANNED + 2:
                s_back_tensor(pe)
            elif c == SCANNED + 4:
                ln_tensor(pe, LN_B, bank[4], 3)
            elif c == SCANNED + 5:
                f_tensor(pe)
            elif c == SCANNED + 6:
                f_back_tensor(pe)

        def beside_scalar(act, c, p):
            if c == 0:
                m_end_scalar(act, p)
            elif c == 1:
                ln_std_scalar(act, LN_B, 2)
            elif c == 2:
                ln_out_scalar(act, LN_B, p, 6 + SA, 6 + CA, bank[4], 2)
            elif c == 3:
                s_in_scalar(act)
            elif c == 4:
                s_z_scalar(act)
                s_conv_scalar(act, 0)
            elif c == 5:
                s_conv_scalar(act, 1)
            elif c == 6:
                s_parts_scalar(act)
            elif c == BEFORE - 1:
                s_step_scalar(act)
            elif BEFORE <= c < SCANNED:
                if c == BEFORE:
                    s_decay_scalar(act, 0)
                if c + 1 < SCANNED:
                    s_decay_scalar(act, c - BEFORE + 1)
            elif c == SCANNED + 1:
                s_gate_scalar(act, p)
            elif c == SCANNED + 3:
                ln_std_scalar(act, LN_B, 3)
            elif c == SCANNED + 4:
                ln_out_scalar(act, LN_B, p, 6 + SB, 6 + CB, bank[4], 3)
            elif c == SCANNED + 5:
                f_scalar(act, p)

        def beside_vector(dve, c, p):
            if c == 0:
                s_pad_vector(dve)
            elif c == 1:
                m_end_vector(dve)
            elif c == 4:
                s_conv_vector(dve, 0)
                s_conv_vector(dve, 1)
            elif c == 5:
                s_gate_vector(dve, 0)
                s_gate_vector(dve, 1)
                s_zgate_vector(dve)
            elif c == 6:
                s_parts_vector(dve)
            elif c == BEFORE - 1:
                s_step_vector(dve)
            elif BEFORE <= c < SCANNED:
                s_scan_vector(dve, c - BEFORE)
            elif c == SCANNED + 1:
                s_end_vector(dve)
            elif c == SCANNED + 3:
                s_res_vector(dve)
            elif c == SCANNED + 6:
                f_gate_vector(dve, p)
                f_res_vector(dve)

        def turn(pa, pb):
            with_a, with_b = pa is not None, pb is not None
            slots = CHUNKS + 2 if with_a else CHUNKS
            with nc.Block() as block:
                @block.sync
                def _(sp):
                    if with_a:
                        a_loads_sync(sp, pa)
                        sp.wait_ge(xa_next, 16)
                    if with_b:
                        sp.wait_ge(f_x, 1)
                        sp.dma_start(out[pb].rearrange("(t q) d -> q t d", q=P), x_out[:, :, :]).then_inc(o_out, 16)
                        sp.wait_ge(o_out, 16)

                @block.gpsimd
                def _(pool):
                    if with_b:
                        for n in range(NS):
                            s_read_gpsimd(pool, n)

                @block.tensor
                def _(pe):
                    if with_a:
                        a_start_tensor(pe)
                    if with_b:
                        m_start_tensor(pe)
                        m_route_tensor(pe)
                    for e in range(NE):
                        if with_a:
                            a_query_tensor(pe, e)
                        if with_b:
                            m_expert_tensor(pe, e)
                    for c in range(slots):
                        if with_b:
                            beside_tensor(pe, c)
                        if with_a:
                            a_chunk_tensor(pe, c)
                    if with_a:
                        a_end_tensor(pe)

                @block.scalar
                def _(act):
                    if with_a:
                        a_start_scalar(act, pa)
                    if with_b:
                        m_start_scalar(act, pb)
                        m_route_scalar(act)
                        for e in range(NE):
                            m_expert_scalar(act, e)
                    for c in range(slots):
                        if with_b:
                            beside_scalar(act, c, pb)
                        if with_a:
                            a_chunk_scalar(act, c)
                    if with_a:
                        a_end_scalar(act, pa)

                @block.vector
                def _(dve):
                    if with_a:
                        a_start_vector(dve)
                    if with_b:
                        ln_vector(dve, LN_B, x1, 1)
                        m_route_vector(dve)
                    for e in range(NE):
                        if with_a:
                            a_query_vector(dve, e)
                        if with_b:
                            m_expert_vector(dve, e)
                    for c in range(slots):
                        if with_b:
                            beside_vector(dve, c, pb)
                        if with_a:
                            a_chunk_vector(dve, c)
                    if with_a:
                        a_end_vector(dve, with_b)
            clear_semaphores()

        turn(0, None)
        with nc.Fori(0, PAIRS - 1) as p:
            turn(p + 1, p)
        turn(None, PAIRS - 1)


def kernel(**inputs):
    import numpy as np
    import concourse.bacc as bacc
    from concourse.bass_utils import run_bass_kernel_spmd as run

    f = {k: np.asarray(v) for k, v in inputs.items()}
    one = np.float32

    def cols(w):
        return w.transpose(2, 0, 1).reshape(w.shape[2], -1)

    def halves(w):
        return w.reshape(NH, P, -1).transpose(1, 0, 2).reshape(P, -1)

    x = np.zeros((PAIRS + 1, TOK, D), one)
    x[:PAIRS] = f["L0_attn_x"].reshape(PAIRS, TOK, D)
    wq = f["L0_attn_Wq"].reshape(H, HD, D)
    wo = f["L0_attn_Wo"].reshape(D, G, H // G, HD)
    wo_x = np.zeros((H // G, G, HD, G, D), one)
    for g in range(G):
        wo_x[:, g, :, g, :] = wo[:, g].transpose(1, 2, 0)
    i, a, k = np.arange(NB), np.arange(QB), np.arange(T)
    dist = np.clip(QB * i[None, :, None] + a[:, None, None] - k[None, None, :], 1 - MAX_POS, MAX_POS - 1) + MAX_POS - 1
    e_shift = f["L0_attn_E"][dist].transpose(0, 3, 1, 2)
    b2 = np.zeros((SROWS, D), one)
    b2[:NE] = f["L0_ffn_b2"]
    w_x = f["L1_attn_W_x"]
    rows = np.arange(QROWS)
    mask_q = np.zeros((QROWS, G, QB), one)
    for r in rows:
        if r < KROWS:
            mask_q[r, r // HD, :] = (1.0 / HD) ** 0.5
        else:
            mask_q[r, :, (r - KROWS) // HD] = (1.0 / HD) ** 0.5
    ha = np.arange(P)
    mask_d = ((ha[:, None] // QB // (H // G) == np.arange(G * QB)[None, :] // QB)
              & (ha[:, None] % QB == np.arange(G * QB)[None, :] % QB)).astype(one)
    sel_r = (ha[:, None] // QB % (H // G) == np.arange(P)[None, :] // 32).astype(one)
    j = np.arange(NG)
    tie = np.tile((j[None, :] < j[:, None]).astype(one).reshape(1, -1), (P, 1))
    bf16 = mybir.dt.np(BF16)
    sel_n = np.repeat((np.arange(SROWS)[:, None] % 32 == np.arange(32)[None, :]), P, axis=1).astype(bf16)

    arrays = {
        "x": x, "wq_rep": np.tile(wq.transpose(2, 0, 1), (1, 1, QROWS // HD)), "wk_t": f["L0_attn_Wk"].T,
        "wv_t": np.tile(f["L0_attn_Wv"].T, (1, P // KROWS)), "wo_x": wo_x, "e_shift": e_shift,
        "wg_t": np.tile(f["L0_ffn_Wg"].T, (1, P // NE)), "w1_t": cols(f["L0_ffn_W1"]), "w3_t": cols(f["L0_ffn_W3"]),
        "w2_t": cols(f["L0_ffn_W2"]), "b1_c": f["L0_ffn_b1"].T, "b3_c": f["L0_ffn_b3"].T, "b2_r": b2,
        "c_t": np.concatenate([f["L0_c"].T, f["L1_c"].T], 1), "wmod": np.concatenate([f["L0_wmod"], f["L1_wmod"]], 1),
        "win_t": f["L1_attn_W_in"].T, "conv_w": halves(f["L1_attn_conv_w"][:, 0, :]), "conv_b": halves(f["L1_attn_conv_b"][:, None]),
        "wx_bc": halves(np.tile(w_x[DTR:].T, (1, PARTS))), "wx_dt": w_x[:DTR], "wdt_t": f["L1_attn_W_dt"].T,
        "b_dt": halves(f["L1_attn_b_dt"][:, None]), "a_log": halves(f["L1_attn_A_log"]), "d_par": halves(f["L1_attn_D_param"][:, None]),
        "wout_t": halves(f["L1_attn_W_out"].T), "ffn_w_t": f["L1_ffn_weight"].T, "ffn_a1": f["L1_ffn_aux_weight1"],
        "ffn_a2": f["L1_ffn_aux_weight2"], "ffn_b": f["L1_ffn_bias"][:, None], "ident": np.eye(P, dtype=one),
        "mask_q": mask_q, "mask_d": mask_d, "sel_r": sel_r, "tie": tie, "sel_n": sel_n,
    }
    nc = bacc.Bacc("TRN2", target_bir_lowering=False, num_devices=1)
    dram, given = {}, {}
    for name, shape in IN_SHAPES:
        v = np.ascontiguousarray(arrays[name].reshape(shape))
        given[f"in_{name}"] = v
        dram[name] = nc.dram_tensor(f"in_{name}", shape, BF16 if name == "sel_n" else F32, kind="ExternalInput").ap()
    out = nc.dram_tensor("out", (PAIRS, TOK, D), F32, kind="ExternalOutput").ap()
    build(nc, dram, out)
    r = run(nc, [given], core_ids=[0])
    return r.results[0]["out"].reshape(B, T, D)
```

```python
from contextlib import ExitStack

import concourse.bass as bass
from concourse import mybir

F32 = mybir.dt.float32
BF16 = mybir.dt.bfloat16
I32 = mybir.dt.int32
ALU = mybir.AluOpType
ACT = mybir.ActivationFunctionType
AX_X = mybir.AxisListType.X

P = 128
B, T, D = 32, 256, 128
PAIRS = B // 2
TOK = 2 * T
TILES = TOK // P
EPS = 1e-5
H, G, HD = 16, 4, 8
QB = 8
NB = T // QB
KROWS = G * HD
QROWS = KROWS + QB * HD
MAX_POS = 128
CHUNKS = 2 * NB // 2
GROUPS = 4
CPG = CHUNKS // GROUPS
BPG = 2 * CPG
PIECES = 4
NE, NG, TOPK, TOPG, ROUTE_SCALE = 16, 4, 4, 2, 2.5
DI, NH, NS, DTR, KC = 256, 2, 16, 8, 4
PARTS = 3
SROWS = PARTS * 32
RING = 3
ROOT_SEED = 0x5F3759DF
ROOT_STEPS = 3
SA, CA, GA, SB, CB, GB = range(6)

IN_SHAPES = [
    ("x", (PAIRS, TOK, D)), ("wq_rep", (P, H * QROWS)), ("wk_t", (P, KROWS)), ("wv_t", (P, P)),
    ("wo_x", (P, G * D)), ("e_shift", (QB * HD, NB * T)), ("wg_t", (P, P)), ("w1_t", (P, NE * P)),
    ("w3_t", (P, NE * P)), ("w2_t", (P, NE * P)), ("b1_c", (P, NE)), ("b3_c", (P, NE)), ("b2_r", (SROWS, D)),
    ("c_t", (P, 2 * B)), ("wmod", (P, 2 * 6 * D)), ("win_t", (P, 2 * DI)), ("conv_w", (P, NH * KC)),
    ("conv_b", (P, NH)), ("wx_bc", (P, NH * SROWS)), ("wx_dt", (DTR, DI)), ("wdt_t", (DTR, DI)),
    ("b_dt", (P, NH)), ("a_log", (P, NH * NS)), ("d_par", (P, NH)), ("wout_t", (P, NH * D)),
    ("ffn_w_t", (P, D)), ("ffn_a1", (P, D)), ("ffn_a2", (P, D)), ("ffn_b", (P, 1)),
    ("ident", (P, P)), ("mask_q", (QROWS, G * QB)), ("mask_d", (P, G * QB)), ("sel_r", (P, P)),
    ("tie", (P, NG * NG)), ("sel_n", (SROWS, 32 * P)),
]


def build(nc, dram, out):
    ctx = ExitStack()
    with ctx:
        sems = []

        def sb(name, shape, dt=F32):
            return ctx.enter_context(nc.sbuf_tensor(name, shape, dt))

        def sem(name):
            s = ctx.enter_context(nc.semaphore(name))
            sems.append(s)
            return s

        bank = [ctx.enter_context(nc.psum_tensor(f"bank{k}", [P, 512], F32)) for k in range(8)]

        wq_rep = sb("wq_rep", [P, H, QROWS])
        wk_t = sb("wk_t", [P, KROWS])
        wv_t = sb("wv_t", [P, P])
        wo_x = sb("wo_x", [P, G, D])
        wg_t = sb("wg_t", [P, P])
        w1_t = sb("w1_t", [P, NE, P])
        w3_t = sb("w3_t", [P, NE, P])
        w2_t = sb("w2_t", [P, NE, P])
        b1_c = sb("b1_c", [P, NE])
        b3_c = sb("b3_c", [P, NE])
        b2_r = sb("b2_r", [SROWS, D])
        win_t = sb("win_t", [P, 2 * DI])
        conv_w = sb("conv_w", [P, NH, KC])
        conv_b = sb("conv_b", [P, NH])
        wx_bc = sb("wx_bc", [P, NH, SROWS])
        w_dtx = sb("w_dtx", [P, NH, DI])
        b_dt = sb("b_dt", [P, NH])
        neg_a = sb("neg_a", [P, NH * NS])
        d_par = sb("d_par", [P, NH])
        wout_t = sb("wout_t", [P, NH, D])
        ffn_w = sb("ffn_w", [P, D])
        ffn_b = sb("ffn_b", [P, 1])
        ident = sb("ident", [P, P])
        mask_q = sb("mask_q", [QROWS, G, QB])
        mask_d = sb("mask_d", [P, G * QB])
        sel_r = sb("sel_r", [P, P])
        tie = sb("tie", [P, NG * NG])
        sel_n = sb("sel_n", [SROWS, 32, P], BF16)
        mod = sb("mod", [P, 12, B])
        eps_c = sb("eps_c", [P, 1])
        zero64 = sb("zero64", [P, NE])

        x_a = sb("x_a", [P, TILES, D])
        x_res = sb("x_res", [P, TILES, D])
        st_a = sb("st_a", [P, TILES, 6])
        mv_a = sb("mv_a", [P, TILES, 2])
        sd_a = sb("sd_a", [P, TILES])
        rstd_a = sb("rstd_a", [P, TILES])
        nw_a = sb("nw_a", [P, TILES])
        h_a = sb("h_a", [P, TOK])
        k_t = sb("k_t", [KROWS, TOK])
        v_s = sb("v_s", [P, TILES, KROWS])
        q_all = sb("q_all", [P, 2 * NB, H, QB])
        q_st = q_all[0:QROWS]
        ke = sb("ke", [QROWS, NB, T])
        nmax = sb("nmax", [P, 2 * NB])
        rsum = sb("rsum", [P, 2 * NB])
        rinv = sb("rinv", [P, 2 * NB])
        probs = sb("probs", [P, 2, 2, T])
        probs_t = sb("probs_t", [P, 2, BPG, P])
        ao_raw = sb("ao_raw", [P, 512])
        ao = q_all[:, 0:BPG].rearrange("p i h a -> p (i h a)").rearrange("p (i g a) -> p i g a", g=G, a=QB)
        y_a = sb("y_a", [P, TOK])
        xn_a = y_a[:, :].rearrange("p (t d) -> p t d", t=TILES)
        x1 = sb("x1", [P, TILES, D])

        x_b = sb("x_b", [P, TILES, D])
        st_b = sb("st_b", [P, TILES, 6])
        mv_b = sb("mv_b", [P, TILES, 2])
        sd_b = sb("sd_b", [P, TILES])
        rstd_b = sb("rstd_b", [P, TILES])
        nw_b = sb("nw_b", [P, TILES])
        h_b = sb("h_b", [P, TOK])
        y_b = sb("y_b", [P, TOK])
        xn_b = y_b[:, :].rearrange("p (t d) -> p t d", t=TILES)
        st_f = sb("st_f", [P, TILES, 6])
        mv_f = sb("mv_f", [P, TILES, 2])
        sd_f = sb("sd_f", [P, TILES])
        rstd_f = sb("rstd_f", [P, TILES])
        nw_f = sb("nw_f", [P, TILES])
        h_f = sb("h_f", [P, TOK])
        dg = h_f[:, :].rearrange("p (i c) -> p i c", i=BPG)
        y_f = sb("y_f", [P, TOK])
        xn_f = y_f[:, :].rearrange("p (t d) -> p t d", t=TILES)
        gate = sb("gate", [P, TILES, NE])
        score = sb("score", [P, TILES, NE])
        masked = sb("masked", [P, TILES, NE])
        picked = sb("picked", [P, TILES, NE])
        equal = sb("equal", [P, TILES, NE])
        prefix = sb("prefix", [P, TILES, NE])
        top8 = sb("top8", [P, TILES, 8])
        few = sb("few", [P, TILES])
        gmax = sb("gmax", [P, TILES, NG])
        beats = sb("beats", [P, TILES, NG, NG])
        ties = sb("ties", [P, TILES, NG, NG])
        grank = sb("grank", [P, TILES, NG])
        we96 = sb("we96", [P, TILES, SROWS])
        w_parts = sb("w_parts", [SROWS, TOK], BF16)
        bc_parts = sb("bc_parts", [SROWS, TOK], BF16)
        x_conv = sb("x_conv", [P, NH, TOK])
        z_gate = sb("z_gate", [P, NH, TOK])
        dt_s = sb("dt_s", [P, NH, TOK])
        dt_x = sb("dt_x", [P, NH, TOK])
        work = sb("work", [P, 6 * 1024])

        def cut(lo, n):
            return work[:, lo:lo + n]

        th = [cut(k * 512, 512) for k in range(2)]
        zh = [cut(1024 + k * 512, 512) for k in range(2)]
        w_rest = h_f[:, :]
        w_rows = ao_raw[:, :]
        CONV = 512
        acc = cut(CONV, 1024).rearrange("p (h t) -> p h t", h=NH)
        act_t = cut(CONV + 1024, 1024).rearrange("p (h t) -> p h t", h=NH)
        act_z = cut(CONV + 2048, 1024).rearrange("p (h t) -> p h t", h=NH)
        gz_t = cut(CONV + 3072, 1024).rearrange("p (h t) -> p h t", h=NH)
        sp_e = acc
        sp_l = act_t
        sp_u = act_z
        sp_r = gz_t
        bc_rest = cut(5120, 512)
        da = [cut(k * 1024, 1024).rearrange("p (h t) -> p h t", h=NH) for k in range(2)]
        ring = [cut(2048 + k * 1024, 1024).rearrange("p (h t) -> p h t", h=NH) for k in range(RING)]
        c_s = [cut(5120 + k * 512, 512) for k in range(2)]

        loaded = sem("loaded")
        cleared = sem("cleared")
        g0 = sem("g0")
        s_silu = sem("s_silu")
        s_mod = sem("s_mod")
        s_modv = sem("s_modv")
        s_nega = sem("s_nega")
        s_dtx = sem("s_dtx")
        s_m1 = sem("s_m1")
        s_m1c = sem("s_m1c")
        s_wc = sem("s_wc")

        wmod = probs_t[:, :, :, :].rearrange("p a b c -> p (a b c)")[:, 0:2 * 6 * D]
        c_t = h_f[:, 0:2 * B]
        c_silu = h_f[:, 2 * B:4 * B]
        ffn_w_t, ffn_a1, ffn_a2, ffn_m1 = (x_b[:, k, :] for k in range(4))
        wx_dt = y_b[0:DTR, 0:DI]
        wdt_t = y_b[0:DTR, DI:2 * DI]
        sgn = y_a[:, 0:B]

        def flat(t):
            n = len(t.shape)
            return t[:, :] if n == 2 else t[:, :, :].rearrange("p a b -> p (a b)")

        loads = [("wq_rep", flat(wq_rep)), ("wk_t", flat(wk_t)), ("wv_t", flat(wv_t)), ("wo_x", flat(wo_x)),
                 ("e_shift", ke[KROWS:QROWS, :, :].rearrange("p a b -> p (a b)")), ("wg_t", flat(wg_t)),
                 ("w1_t", flat(w1_t)), ("w3_t", flat(w3_t)), ("w2_t", flat(w2_t)), ("b1_c", flat(b1_c)),
                 ("b3_c", flat(b3_c)), ("b2_r", flat(b2_r)), ("c_t", c_t), ("wmod", wmod), ("win_t", flat(win_t)),
                 ("conv_w", flat(conv_w)), ("conv_b", flat(conv_b)), ("wx_bc", flat(wx_bc)), ("wx_dt", wx_dt),
                 ("wdt_t", wdt_t), ("b_dt", flat(b_dt)), ("a_log", flat(neg_a)), ("d_par", flat(d_par)),
                 ("wout_t", flat(wout_t)), ("ffn_w_t", ffn_w_t), ("ffn_a1", ffn_a1), ("ffn_a2", ffn_a2),
                 ("ffn_b", flat(ffn_b)), ("ident", flat(ident)), ("mask_q", flat(mask_q)), ("mask_d", flat(mask_d)),
                 ("sel_r", flat(sel_r)), ("tie", flat(tie)), ("sel_n", flat(sel_n))]
        LOADED = 16 * len(loads)

        def x_pair(p):
            return dram["x"][p].rearrange("(t q) d -> q t d", q=P)

        with nc.Block() as block:
            @block.sync
            def _(sp):
                for name, dst in loads:
                    sp.dma_start(dst, dram[name]).then_inc(loaded, 16)

            @block.gpsimd
            def _(pool):
                nc.gpsimd.memset(we96[:, :, :], 0.0)
                nc.gpsimd.memset(eps_c[:, :], EPS)
                nc.gpsimd.memset(zero64[:, :], 0.0)

            @block.tensor
            def _(pe):
                pe.wait_ge(loaded, LOADED)
                pe.wait_ge(s_silu, 1)
                for m in range(12):
                    last = nc.tensor.matmul(bank[0][:, m * B:(m + 1) * B], wmod[:, m * D:(m + 1) * D],
                                            c_silu[:, (m // 6) * B:(m // 6 + 1) * B], start=True, stop=True)
                last.then_inc(s_mod, 1)
                for k in range(NH):
                    last = nc.tensor.matmul(bank[1 + k][:, 0:DI], wx_dt[:, k * P:(k + 1) * P], wdt_t, start=True, stop=True)
                last.then_inc(s_dtx, 1)
                nc.tensor.matmul(bank[3][:, 0:D], ffn_a1, ffn_w_t, start=True, stop=True).then_inc(s_m1, 1)
                pe.wait_ge(s_m1c, 1)
                nc.tensor.matmul(bank[4][:, 0:D], ffn_m1, ffn_a2, start=True, stop=True).then_inc(s_wc, 1)

            @block.scalar
            def _(act):
                act.wait_ge(loaded, LOADED)
                nc.scalar.activation(c_silu, c_t, ACT.Silu).then_inc(s_silu, 1)
                nc.scalar.activation(neg_a[:, :], neg_a[:, :], ACT.Exp).then_inc(s_nega, 1)
                act.wait_ge(s_dtx, 1)
                for k in range(NH):
                    nc.scalar.activation(w_dtx[:, k, :], bank[1 + k][:, 0:DI], ACT.Copy)
                act.wait_ge(s_m1, 1)
                nc.scalar.activation(ffn_m1, bank[3][:, 0:D], ACT.Copy).then_inc(s_m1c, 1)
                act.wait_ge(s_wc, 1)
                nc.scalar.activation(ffn_w[:, :], bank[4][:, 0:D], ACT.Copy)

            @block.vector
            def _(dve):
                dve.wait_ge(loaded, LOADED)
                nc.vector.tensor_scalar(b1_c[:, :], b1_c[:, :], 0.5, None, ALU.mult)
                nc.vector.tensor_scalar(conv_b[:, :], conv_b[:, :], 0.5, None, ALU.mult)
                dve.wait_ge(s_nega, 1)
                nc.vector.tensor_scalar(neg_a[:, :], neg_a[:, :], -1.0, None, ALU.mult)
                dve.wait_ge(s_mod, 1)
                n = 0
                for m in range(12):
                    src = bank[0][:, m * B:(m + 1) * B]
                    if m % 6 in (SA, SB):
                        nc.vector.tensor_copy(mod[:, m, :], src)
                    elif m % 6 in (CA, CB):
                        nc.vector.tensor_scalar(mod[:, m, :], src, 1.0, None, ALU.add)
                    else:
                        nc.vector.tensor_scalar(sgn, src, 0.0, 2.0, ALU.is_ge, ALU.mult).then_inc(s_modv, 1)
                        nc.vector.tensor_scalar(mod[:, m, :], src, -1.0, None, ALU.mult).then_inc(s_modv, 1)
                        dve.wait_ge(s_modv, n + 2)
                        nc.vector.tensor_tensor(mod[:, m, :], mod[:, m, :], src, ALU.max).then_inc(s_modv, 1)
                        dve.wait_ge(s_modv, n + 3)
                        nc.vector.tensor_scalar(mod[:, m, :], mod[:, m, :], 0.25, None, ALU.max).then_inc(s_modv, 1)
                        n += 4
                        dve.wait_ge(s_modv, n)
                        nc.vector.scalar_tensor_tensor(mod[:, m, :], sgn, -1.0, mod[:, m, :], ALU.add, ALU.mult).then_inc(s_modv, 1)
                        n += 1
                        dve.wait_ge(s_modv, n)

        xa_in, xr_in = sem("xa_in"), sem("xr_in")
        ke_in = [sem(f"ke_in{q}") for q in range(PIECES)]
        a_st, a_mv, a_sd, a_rstd, a_xn, a_tr, a_h = (sem("a_" + n) for n in ("st", "mv", "sd", "rstd", "xn", "tr", "h"))
        b_st, b_mv, b_sd, b_rstd, b_xn, b_tr, b_h = (sem("b_" + n) for n in ("st", "mv", "sd", "rstd", "xn", "tr", "h"))
        a_k, a_kc, a_v, a_vc, a_q, a_qm = (sem("a_" + n) for n in ("k", "kc", "v", "vc", "q", "qm"))
        a_s, a_max, a_exp, a_t, a_tc, a_pv, a_ao, a_inv, a_dg, a_r, a_on = (
            sem("a_" + n) for n in ("s", "max", "exp", "t", "tc", "pv", "ao", "inv", "dg", "r", "on"))
        a_wo, a_y, a_back, a_res = (sem("a_" + n) for n in ("wo", "y", "back", "res"))
        m_logit, m_exp, m_ch, m_wt, m_cp, m_rest, m_mid, m_parts = (
            sem("m_" + n) for n in ("logit", "exp", "ch", "wt", "cp", "rest", "mid", "parts"))
        m_h1, m_h3, m_wb, m_tz, m_a, m_b, m_hh, m_w2 = (sem("m_" + n) for n in ("h1", "h3", "wb", "tz", "a", "b", "hh", "w2"))
        b_y, b_back, b_x = sem("b_y"), sem("b_back"), sem("b_x")
        s_xz, s_z, s_zg, s_cv, s_ct, s_xc, s_bc, s_bcc, s_bcr, s_bcm, s_bcp = (
            sem("s_" + n) for n in ("xz", "z", "zg", "cv", "ct", "xc", "bc", "bcc", "bcr", "bcm", "bcp"))
        s_dtp, s_sp1, s_sp2, s_sp3, s_spv, s_dt = (sem("s_" + n) for n in ("dtp", "sp1", "sp2", "sp3", "spv", "dt"))
        s_bb, s_cb, s_da, s_cs, s_dbx, s_h, s_hc, s_y, s_g, s_yv = (
            sem("s_" + n) for n in ("bb", "cb", "da", "cs", "dbx", "h", "hc", "y", "g", "yv"))
        a_nw, n_nw, f_nw = sem("a_nw"), sem("n_nw"), sem("f_nw")
        n_st, n_mv, n_sd, n_rstd, n_xn, n_tr, n_h = (sem("n_" + n) for n in ("st", "mv", "sd", "rstd", "xn", "tr", "h"))
        f_o, f_y, f_back, f_x3, f_m, f_t, f_g, f_x, o_out = (
            sem(n) for n in ("f_o", "f_y", "f_back", "f_x3", "f_m", "f_t", "f_g", "f_x", "o_out"))
        f_st, f_mv, f_sd, f_rstd, f_xn, f_tr, f_h = (sem("f_" + n) for n in ("st", "mv", "sd", "rstd", "xn", "tr", "h"))
        numbers = sorted(s.num for s in sems)
        assert numbers == list(range(numbers[0], numbers[0] + len(sems)))

        def clear_semaphores():
            with nc.Block() as block:
                @block.sync
                def _(sp):
                    sp.sem_clear(range(numbers[0], numbers[-1] + 1))

        clear_semaphores()

        LN_A = dict(nw=nw_a, s_nw=a_nw, st=st_a, mv=mv_a, sd=sd_a, rstd=rstd_a, xn=xn_a, h=h_a, s_st=a_st, s_mv=a_mv, s_sd=a_sd,
                    s_rstd=a_rstd, s_xn=a_xn, s_tr=a_tr, s_h=a_h)
        LN_B = dict(st=st_b, mv=mv_b, sd=sd_b, rstd=rstd_b, xn=xn_b, h=h_b, s_st=b_st, s_mv=b_mv, s_sd=b_sd,
                    s_rstd=b_rstd, s_xn=b_xn, s_tr=b_tr, s_h=b_h)
        LN_S = dict(nw=nw_b, s_nw=n_nw, st=st_b, mv=mv_b, sd=sd_b, rstd=rstd_b, xn=xn_b, h=h_b, s_st=n_st, s_mv=n_mv, s_sd=n_sd,
                    s_rstd=n_rstd, s_xn=n_xn, s_tr=n_tr, s_h=n_h)
        LN_F = dict(nw=nw_f, s_nw=f_nw, st=st_f, mv=mv_f, sd=sd_f, rstd=rstd_f, xn=xn_f, h=h_f, s_st=f_st, s_mv=f_mv, s_sd=f_sd,
                    s_rstd=f_rstd, s_xn=f_xn, s_tr=f_tr, s_h=f_h)

        def scale_of(m, p, b):
            return mod[:, m, bass.ds(2 * p + b, 1)]

        def half(ap, b):
            return ap[:, b * T:(b + 1) * T]

        def tile(ap, t):
            return ap[:, t * P:(t + 1) * P]

        def ln_stats_vector(dve, L, x):
            for t in range(TILES):
                last = nc.vector.bn_stats(L["st"][:, t, :], x[:, t, :])
            last.then_inc(L["s_st"], 1)
            dve.wait_ge(L["s_st"], 1)
            for t in range(TILES):
                last = nc.vector.bn_aggr(L["mv"][:, t, :], L["st"][:, t, :])
            last.then_inc(L["s_mv"], 1)

        def ln_std_scalar(act, L):
            act.wait_ge(L["s_mv"], 1)
            nc.scalar.activation(L["sd"][:, :], L["mv"][:, :, 1], ACT.Sqrt, bias=eps_c[:, :]).then_inc(L["s_sd"], 1)

        def ln_inverse_vector(dve, L):
            dve.wait_ge(L["s_sd"], 1)
            nc.vector.reciprocal(L["rstd"][:, :], L["sd"][:, :]).then_inc(L["s_rstd"], 1)

        def ln_root_gpsimd(pool, L):
            v, y, t, n = L["sd"][:, :], L["rstd"][:, :], L["nw"][:, :], 2
            pool.wait_ge(L["s_mv"], 1)
            nc.gpsimd.tensor_scalar(v, L["mv"][:, :, 1], EPS, None, ALU.add).then_inc(L["s_nw"], 1)
            pool.wait_ge(L["s_nw"], 1)
            nc.gpsimd.tensor_scalar(y.bitcast(I32), v.bitcast(I32), -0.5, float(ROOT_SEED), ALU.mult, ALU.add).then_inc(L["s_nw"], 1)
            for k in range(ROOT_STEPS):
                pool.wait_ge(L["s_nw"], n)
                nc.gpsimd.tensor_tensor(t, v, y, ALU.mult).then_inc(L["s_nw"], 1)
                pool.wait_ge(L["s_nw"], n + 1)
                nc.gpsimd.tensor_tensor(t, t, y, ALU.mult).then_inc(L["s_nw"], 1)
                pool.wait_ge(L["s_nw"], n + 2)
                nc.gpsimd.tensor_scalar(t, t, -0.5, 1.5, ALU.mult, ALU.add).then_inc(L["s_nw"], 1)
                pool.wait_ge(L["s_nw"], n + 3)
                nc.gpsimd.tensor_tensor(y, y, t, ALU.mult).then_inc(L["s_rstd"] if k == ROOT_STEPS - 1 else L["s_nw"], 1)
                n += 4

        def ln_norm_vector(dve, L, x):
            dve.wait_ge(L["s_rstd"], 1)
            for t in range(TILES):
                last = nc.vector.tensor_scalar(L["xn"][:, t, :], x[:, t, :], L["mv"][:, t, 0:1], L["rstd"][:, t:t + 1],
                                               ALU.subtract, ALU.mult)
            last.then_inc(L["s_xn"], 1)

        def ln_tensor(pe, L, dst):
            pe.wait_ge(L["s_xn"], 1)
            for t in range(TILES):
                last = nc.tensor.transpose(tile(dst, t), L["xn"][:, t, :], ident[:, :])
            last.then_inc(L["s_tr"], 1)

        def ln_out_scalar(act, L, p, shift, scale, src):
            act.wait_ge(L["s_tr"], 1)
            for b in range(2):
                last = nc.scalar.activation(half(L["h"], b), half(src, b), ACT.Identity, bias=scale_of(shift, p, b),
                                            scale=scale_of(scale, p, b))
            last.then_inc(L["s_h"], 1)

        def gate_scalar(src, y, p, m, done):
            for b in range(2):
                last = nc.scalar.activation(half(y, b), half(src, b), ACT.Identity, bias=0.0, scale=scale_of(m, p, b))
            last.then_inc(done, 1)

        def back_tensor(y, dst, done):
            for t in range(TILES):
                last = nc.tensor.transpose(tile(dst, t), tile(y, t), ident[:, :])
            last.then_inc(done, 1)

        def tokens(ap):
            return ap.rearrange("p (t d) -> p t d", t=TILES)

        def a_keys_tensor(pe):
            pe.wait_ge(a_h, 1)
            nc.tensor.matmul(bank[7][0:KROWS, :], wk_t[:, :], h_a[:, :], start=True, stop=True).then_inc(a_k, 1)

        def a_values_in_tensor(pe):
            for t in range(TILES):
                last = nc.tensor.matmul(tile(bank[2], t), tile(h_a, t), wv_t[:, :], start=True, stop=True)
            last.then_inc(a_v, 1)

        def a_keys_scalar(act, after_scores):
            act.wait_ge(a_k, 1)
            if after_scores:
                for q in range(PIECES):
                    act.wait_ge(ke_in[q], 16)
            nc.scalar.activation(k_t[:, :], bank[7][0:KROWS, :], ACT.Copy).then_inc(a_kc, 1)

        def a_values_in_scalar(act):
            act.wait_ge(a_v, 1)
            nc.scalar.activation(v_s[:, :, :], tokens(bank[2])[:, :, 0:KROWS], ACT.Copy).then_inc(a_vc, 1)

        def a_spread_sync(sp, b, q):
            n = NB // PIECES
            sp.dma_start(ke[0:KROWS, q * n:(q + 1) * n, :],
                         half(k_t, b).unsqueeze(1).broadcast_to([KROWS, n, T])).then_inc(ke_in[q], 16)

        UNITS = H
        assert H // 2 * 2 == UNITS

        def unit(u):
            return 1 - u // (H // 2), 2 * (u % (H // 2))

        def a_query_tensor(pe, u):
            b, h = unit(u)
            if u == 0:
                pe.wait_ge(a_kc, 1)
            else:
                pe.wait_ge(a_qm, u)
            for k in range(2):
                last = nc.tensor.matmul(half(bank[0], k)[0:QROWS, :], wq_rep[:, h + k, :], half(h_a, b), start=True, stop=True)
            last.then_inc(a_q, 1)

        def a_query_vector(dve, u):
            b, h = unit(u)
            dve.wait_ge(a_q, u + 1)
            m = mask_q[:, h // (H // G), :].unsqueeze(1).unsqueeze(1).broadcast_to([QROWS, NB, 2, QB])
            nc.vector.tensor_tensor(q_st[:, NB * b:NB * (b + 1), h:h + 2, :],
                                    bank[0][0:QROWS, :].rearrange("p (h i a) -> p i h a", h=2, a=QB), m, ALU.mult).then_inc(a_qm, 1)

        VALUES, INVERSE, SCALED = 2, 4, 5
        TRAIL = SCALED

        def group_at(c, k):
            return c // CPG - 1 if c % CPG == k and c >= CPG else None

        def a_chunk_tensor(pe, c, after_f):
            if c < CHUNKS:
                b, i0 = c // (CHUNKS // 2), 2 * (c % (CHUNKS // 2))
                if b:
                    pe.wait_ge(ke_in[i0 // (NB // PIECES)], 16)
                if c >= 2:
                    pe.wait_ge(a_exp, c - 1)
                for k in range(2):
                    last = nc.tensor.matmul(bank[c % 2][:, k * T:(k + 1) * T],
                                            q_st[:, 2 * c + k, :, :].rearrange("p h a -> p (h a)"), ke[:, i0 + k, :],
                                            start=True, stop=True)
                last.then_inc(a_s, 1)
            g = group_at(c, VALUES)
            if g is not None:
                a_values_tensor(pe, g, after_f)
            g = group_at(c, INVERSE)
            if g is not None:
                pe.wait_ge(a_dg, g + 1)
                pe.wait_ge(a_ao, g + 1)
                nc.tensor.matmul(bank[3][:, :], sel_r[:, :], dg[:, :, :].rearrange("p i c -> p (i c)"), start=True, stop=True).then_inc(a_r, 1)
            c -= 2
            if 0 <= c < CHUNKS:
                pe.wait_ge(a_exp, c + 1)
                if c:
                    pe.wait_ge(a_tc, c)
                for kh in range(2):
                    for k in range(2):
                        last = nc.tensor.transpose(tile(bank[2], 2 * kh + k), probs[:, c % 2, k, kh * P:(kh + 1) * P],
                                                   ident[:, :])
                last.then_inc(a_t, 1)

        def a_values_tensor(pe, g, after_f):
            pe.wait_ge(a_tc, CPG * (g + 1))
            if g:
                pe.wait_ge(a_on, g)
            elif after_f:
                pe.wait_ge(f_x, 1)
            pt = probs_t[:, :, :, :].rearrange("p k i (g r a) -> p k i g r a", g=G, r=H // G)
            for kh in range(2):
                for r in range(H // G):
                    last = nc.tensor.matmul(
                        bank[3][32 * r:32 * r + 32, :].rearrange("p (i g a) -> p i g a", g=G, a=QB),
                        v_s[:, 2 * (g // 2) + kh, :], pt[:, kh, :, :, r, :], start=(kh == 0), stop=(kh == 1))
            last.then_inc(a_pv, 1)

        def a_chunk_vector(dve, c):
            if c < CHUNKS:
                dve.wait_ge(a_s, c + 1)
                nc.vector.tensor_reduce(nmax[:, 2 * c:2 * c + 2], bank[c % 2][:, :].rearrange("p (k t) -> p k t", k=2),
                                        AX_X, ALU.max, negate=True).then_inc(a_max, 1)
            g = group_at(c, VALUES)
            if g is not None:
                dve.wait_ge(a_exp, CPG * (g + 1))
                cols = slice(BPG * g, BPG * (g + 1))
                nc.vector.reciprocal(rinv[:, cols], rsum[:, cols]).then_inc(a_inv, 1)
                dve.wait_ge(a_inv, g + 1)
                if g:
                    dve.wait_ge(a_r, g)
                nc.vector.tensor_tensor(dg[:, :, :], rinv[:, cols].unsqueeze(2).broadcast_to([P, BPG, G * QB]),
                                        mask_d[:, :].unsqueeze(1).broadcast_to([P, BPG, G * QB]), ALU.mult).then_inc(a_dg, 1)
            g = group_at(c, SCALED)
            if g is not None:
                dve.wait_ge(a_r, g + 1)
                cols = slice(BPG * g, BPG * (g + 1))
                nc.vector.tensor_tensor(ao[:, cols, :, :].rearrange("p i g a -> p (i g a)"), ao_raw[:, :], bank[3][:, :],
                                        ALU.mult).then_inc(a_on, 1)
            c -= 2
            if 0 <= c < CHUNKS:
                if c and c % CPG == 0:
                    dve.wait_ge(a_pv, c // CPG)
                dve.wait_ge(a_t, c + 1)
                i0 = 2 * (c % CPG)
                nc.vector.tensor_copy(probs_t[:, :, i0:i0 + 2, :].rearrange("p k i c -> p k (i c)"),
                                      bank[2][:, :].rearrange("p (k c) -> p k c", k=2)).then_inc(a_tc, 1)

        def a_chunk_scalar(act, c):
            if c < CHUNKS:
                act.wait_ge(a_max, c + 1)
                if c >= 2:
                    act.wait_ge(a_t, c - 1)
                for k in range(2):
                    i = 2 * c + k
                    last = nc.scalar.activation(probs[:, c % 2, k, :], bank[c % 2][:, k * T:(k + 1) * T], ACT.Exp,
                                                bias=nmax[:, i:i + 1], accum_out=rsum[:, i:i + 1])
                last.then_inc(a_exp, 1)
            g = group_at(c, VALUES)
            if g is not None:
                act.wait_ge(a_pv, g + 1)
                if g:
                    act.wait_ge(a_on, g)
                nc.scalar.activation(ao_raw[:, :], bank[3][:, :], ACT.Copy).then_inc(a_ao, 1)
        def a_end_tensor(pe):
            pe.wait_ge(a_on, GROUPS)
            for g in range(G):
                last = nc.tensor.matmul(bank[3][:, :].rearrange("p (i a) -> p i a", a=QB), wo_x[:, g, :], ao[:, :, g, :],
                                        start=(g == 0), stop=(g == G - 1))
            last.then_inc(a_wo, 1)

        def a_back_tensor(pe):
            pe.wait_ge(a_y, 1)
            back_tensor(y_a, bank[2], a_back)

        def a_end_scalar(act, p):
            act.wait_ge(a_wo, 1)
            gate_scalar(bank[3], y_a, p, GA, a_y)

        def a_end_vector(dve, with_b):
            dve.wait_ge(a_back, 1)
            dve.wait_ge(xr_in, 16)
            if with_b:
                dve.wait_ge(b_x, 1)
            nc.vector.tensor_tensor(x1[:, :, :], x_res[:, :, :], tokens(bank[2]), ALU.add).then_inc(a_res, 1)

        def m_logits_tensor(pe):
            pe.wait_ge(b_h, 1)
            for t in range(TILES):
                last = nc.tensor.matmul(tile(bank[3], t), tile(h_b, t), wg_t[:, :], start=True, stop=True)
            last.then_inc(m_logit, 1)

        def m_logits_scalar(act):
            act.wait_ge(m_logit, 1)
            nc.scalar.activation(gate[:, :, :], tokens(bank[3])[:, :, 0:NE], ACT.Exp, scale=-1.0).then_inc(m_exp, 1)

        def m_route_tensor(pe):
            pe.wait_ge(m_ch, ROUTE_STEPS)
            for t in range(TILES):
                last = nc.tensor.transpose(tile(bank[2], t)[0:SROWS, :], we96[:, t, :], ident[:, :])
            last.then_inc(m_wt, 1)

        def split_first_scalar(act, src, keep, parts, ready, s_cp):
            act.wait_ge(ready, 1)
            last = nc.scalar.activation(parts[:, :], src[0:SROWS, :], ACT.Copy)
            if keep is not None:
                last = nc.scalar.activation(keep[0:SROWS, :], src[0:SROWS, :], ACT.Copy)
            last.then_inc(s_cp, 1)

        def split_first_vector(dve, src, parts, rest, s_cp, s_rest):
            dve.wait_ge(s_cp, 1)
            nc.vector.tensor_tensor(rest[0:SROWS, :], src[0:SROWS, :], parts[:, :], ALU.subtract).then_inc(s_rest, 1)

        def split_next_scalar(act, parts, rest, s_rest, s_mid):
            act.wait_ge(s_rest, 1)
            for k in range(1, PARTS):
                last = nc.scalar.activation(parts[32 * k:32 * k + 32, :], rest[32 * k:32 * k + 32, :], ACT.Copy)
            last.then_inc(s_mid, 1)

        def split_last_vector(dve, parts, rest, s_mid, s_done):
            dve.wait_ge(s_mid, 1)
            nc.vector.tensor_tensor(parts[64:96, :], rest[64:96, :], parts[64:96, :], ALU.subtract).then_inc(s_done, 1)

        ROUTE_STEPS = 21

        def m_route_vector(dve, k):
            if k == 0:
                dve.wait_ge(m_exp, 1)
            else:
                dve.wait_ge(m_ch, k)
            by_group = [P, TILES, NG, NG]
            other, own = gmax[:, :, :].unsqueeze(2).broadcast_to(by_group), gmax[:, :, :].unsqueeze(3).broadcast_to(by_group)
            flat_g, flat_e = "p t j i -> p t (j i)", "p t (g k) -> p (t g) k"
            open_ = grank[:, :, :].rearrange("p t g -> p (t g)").unsqueeze(2).broadcast_to([P, TILES * NG, NE // NG])
            fourth = top8[:, :, TOPK - 1:TOPK].broadcast_to([P, TILES, NE])
            few_e = few[:, :].unsqueeze(2).broadcast_to([P, TILES, NE])
            if k == 0:
                nc.vector.tensor_scalar(gate[:, :, :], gate[:, :, :], 1.0, None, ALU.add).then_inc(m_ch, 1)
            elif k == 1:
                nc.vector.reciprocal(score[:, :, :], gate[:, :, :]).then_inc(m_ch, 1)
            elif k == 2:
                nc.vector.tensor_reduce(gmax[:, :, :], score[:, :, :].rearrange("p t (g k) -> p t g k", g=NG), AX_X,
                                        ALU.max).then_inc(m_ch, 1)
            elif k == 3:
                nc.vector.tensor_tensor(beats[:, :, :, :], other, own, ALU.is_gt)
                nc.vector.tensor_tensor(ties[:, :, :, :], other, own, ALU.is_equal).then_inc(m_ch, 1)
            elif k == 4:
                nc.vector.tensor_tensor(ties[:, :, :, :].rearrange(flat_g), ties[:, :, :, :].rearrange(flat_g),
                                        tie[:, :].unsqueeze(1).broadcast_to([P, TILES, NG * NG]), ALU.mult).then_inc(m_ch, 1)
            elif k == 5:
                nc.vector.tensor_tensor(beats[:, :, :, :], beats[:, :, :, :], ties[:, :, :, :], ALU.add).then_inc(m_ch, 1)
            elif k == 6:
                nc.vector.tensor_reduce(grank[:, :, :], beats[:, :, :, :], AX_X, ALU.add).then_inc(m_ch, 1)
            elif k == 7:
                nc.vector.tensor_scalar(grank[:, :, :], grank[:, :, :], TOPG - 0.5, None, ALU.is_lt).then_inc(m_ch, 1)
            elif k == 8:
                nc.vector.tensor_tensor(masked[:, :, :].rearrange(flat_e, g=NG), score[:, :, :].rearrange(flat_e, g=NG), open_,
                                        ALU.mult).then_inc(m_ch, 1)
            elif k == 9:
                nc.vector.scalar_tensor_tensor(masked[:, :, :].rearrange(flat_e, g=NG), open_, -1.0,
                                               masked[:, :, :].rearrange(flat_e, g=NG), ALU.add, ALU.add).then_inc(m_ch, 1)
            elif k == 10:
                for t in range(TILES):
                    last = nc.vector.max(top8[:, t, :], masked[:, t, :])
                last.then_inc(m_ch, 1)
            elif k == 11:
                nc.vector.tensor_tensor(picked[:, :, :], masked[:, :, :], fourth, ALU.is_gt)
                nc.vector.tensor_tensor(equal[:, :, :], masked[:, :, :], fourth, ALU.is_equal).then_inc(m_ch, 1)
            elif k == 12:
                for t in range(TILES):
                    nc.vector.tensor_tensor_scan(prefix[:, t, :], equal[:, t, :], zero64[:, :], 0.0, ALU.add, ALU.add)
                nc.vector.tensor_reduce(few[:, :], picked[:, :, :], AX_X, ALU.add).then_inc(m_ch, 1)
            elif k == 13:
                nc.vector.tensor_tensor(prefix[:, :, :], prefix[:, :, :], few_e, ALU.add).then_inc(m_ch, 1)
            elif k == 14:
                nc.vector.scalar_tensor_tensor(equal[:, :, :], prefix[:, :, :], TOPK + 0.5, equal[:, :, :], ALU.is_lt,
                                               ALU.mult).then_inc(m_ch, 1)
            elif k == 15:
                nc.vector.tensor_tensor(picked[:, :, :], picked[:, :, :], equal[:, :, :], ALU.add).then_inc(m_ch, 1)
            elif k == 16:
                nc.vector.tensor_tensor(picked[:, :, :], picked[:, :, :], score[:, :, :], ALU.mult).then_inc(m_ch, 1)
            elif k == 17:
                nc.vector.tensor_reduce(few[:, :], picked[:, :, :], AX_X, ALU.add).then_inc(m_ch, 1)
            elif k == 18:
                nc.vector.reciprocal(few[:, :], few[:, :]).then_inc(m_ch, 1)
            elif k == 19:
                nc.vector.tensor_scalar(few[:, :], few[:, :], ROUTE_SCALE, None, ALU.mult).then_inc(m_ch, 1)
            else:
                for part in range(PARTS):
                    last = nc.vector.tensor_tensor(we96[:, :, 32 * part:32 * part + NE], picked[:, :, :], few_e, ALU.mult)
                last.then_inc(m_ch, 1)

        def m_up_tensor(pe, e):
            if e:
                pe.wait_ge(m_tz, e)
            nc.tensor.matmul(bank[4][:, :], w1_t[:, e, :], h_b[:, :], start=True, stop=True).then_inc(m_h1, 1)
            if e:
                pe.wait_ge(m_b, e)
            nc.tensor.matmul(bank[5][:, :], w3_t[:, e, :], h_b[:, :], start=True, stop=True).then_inc(m_h3, 1)

        def m_down_tensor(pe, e):
            pe.wait_ge(m_hh, e + 1)
            nc.tensor.matmul(bank[7][:, :], w2_t[:, e, :], zh[e % 2], start=False, stop=(e == NE - 1)).then_inc(m_w2, 1)

        def m_weight_tensor(pe, e, after_f):
            if e == 0:
                if after_f:
                    pe.wait_ge(s_g, 1)
                nc.tensor.matmul(bank[7][:, :], b2_r[:, :], w_rows[0:SROWS, :], start=True, stop=False)
            else:
                pe.wait_ge(m_hh, e)
            nc.tensor.matmul(bank[6][:, :], sel_n[:, e, :], w_parts[:, :], start=True, stop=True).then_inc(m_wb, 1)

        def m_expert_tensor(pe, e):
            if e:
                m_down_tensor(pe, e - 1)
            if e + 1 < NE:
                m_up_tensor(pe, e + 1)

        def m_expert_scalar(act, e):
            act.wait_ge(m_h1, e + 1)
            if e >= 2:
                act.wait_ge(m_w2, e - 1)
            nc.scalar.activation(th[e % 2], bank[4][:, :], ACT.Tanh, bias=b1_c[:, e:e + 1], scale=0.5)
            nc.scalar.activation(zh[e % 2], bank[4][:, :], ACT.Identity, bias=b1_c[:, e:e + 1], scale=0.5).then_inc(m_tz, 1)

        def m_expert_vector(dve, e):
            dve.wait_ge(m_tz, e + 1)
            nc.vector.scalar_tensor_tensor(zh[e % 2], th[e % 2], 1.0, zh[e % 2], ALU.add, ALU.mult).then_inc(m_a, 1)
            dve.wait_ge(m_h3, e + 1)
            dve.wait_ge(m_a, e + 1)
            nc.vector.scalar_tensor_tensor(zh[e % 2], bank[5][:, :], b3_c[:, e:e + 1], zh[e % 2], ALU.add,
                                           ALU.mult).then_inc(m_b, 1)
            dve.wait_ge(m_wb, e + 1)
            dve.wait_ge(m_b, e + 1)
            nc.vector.tensor_tensor(zh[e % 2], zh[e % 2], bank[6][:, :], ALU.mult).then_inc(m_hh, 1)

        def m_end_scalar(act, p):
            act.wait_ge(m_w2, NE)
            gate_scalar(bank[7], y_b, p, GB, b_y)

        def m_back_tensor(pe):
            pe.wait_ge(b_y, 1)
            back_tensor(y_b, bank[4], b_back)

        def m_end_vector(dve, after_f):
            dve.wait_ge(b_back, 1)
            if after_f:
                dve.wait_ge(o_out, 16)
            nc.vector.tensor_tensor(x_b[:, :, :], x1[:, :, :], tokens(bank[4]), ALU.add).then_inc(b_x, 1)
            dve.wait_ge(b_x, 1)
            ln_stats_vector(dve, LN_S, x_b)

        def s_in_tensor(pe, part):
            pe.wait_ge(n_h, 1)
            for k in (0, 1) if part == 0 else (2, 3):
                nc.tensor.matmul(bank[4 + k][:, :], win_t[:, k * P:(k + 1) * P], h_b[:, :], start=True, stop=True).then_inc(s_xz, 1)

        def s_z_scalar(act):
            for h in range(NH):
                act.wait_ge(s_xz, NH + h + 1)
                nc.scalar.activation(gz_t[:, h, :], bank[6 + h][:, :], ACT.Tanh, scale=0.5)
                nc.scalar.activation(z_gate[:, h, :], bank[6 + h][:, :], ACT.Copy, scale=0.5).then_inc(s_z, 1)

        def s_conv_vector(dve, h):
            dve.wait_ge(s_xz, h + 1)
            a, x = (ap.rearrange("p (b t) -> p b t", b=2) for ap in (acc[:, h, :], bank[4 + h][:, :]))
            nc.vector.tensor_scalar(a, x, conv_w[:, h, KC - 1:KC], None, ALU.mult).then_inc(s_cv, 1)
            for back in range(1, KC):
                dve.wait_ge(s_cv, KC * h + back)
                nc.vector.scalar_tensor_tensor(a[:, :, back:], x[:, :, 0:T - back], conv_w[:, h, KC - 1 - back:KC - back],
                                               a[:, :, back:], ALU.mult, ALU.add).then_inc(s_cv, 1)

        def s_conv_scalar(act, h):
            act.wait_ge(s_cv, KC * (h + 1))
            nc.scalar.activation(act_t[:, h, :], acc[:, h, :], ACT.Tanh, bias=conv_b[:, h:h + 1], scale=0.5)
            nc.scalar.activation(act_z[:, h, :], acc[:, h, :], ACT.Identity, bias=conv_b[:, h:h + 1], scale=0.5).then_inc(s_ct, 1)

        def s_gate_vector(dve, h):
            dve.wait_ge(s_ct, h + 1)
            nc.vector.scalar_tensor_tensor(x_conv[:, h, :], act_t[:, h, :], 1.0, act_z[:, h, :], ALU.add, ALU.mult).then_inc(s_xc, 1)

        def s_zgate_vector(dve):
            dve.wait_ge(s_z, NH)
            nc.vector.scalar_tensor_tensor(z_gate[:, :, :], gz_t[:, :, :], 1.0, z_gate[:, :, :], ALU.add, ALU.mult).then_inc(s_zg, 1)

        def s_proj_tensor(pe):
            pe.wait_ge(s_xc, NH)
            pe.wait_ge(s_z, 1)
            for h in range(NH):
                for k in range(NH):
                    last = nc.tensor.matmul(bank[5 + h][:, :], w_dtx[:, k, h * P:(h + 1) * P], x_conv[:, k, :],
                                            start=(k == 0), stop=(k == NH - 1))
                last.then_inc(s_dtp, 1)
            for k in range(NH):
                last = nc.tensor.matmul(bank[4][0:SROWS, :], wx_bc[:, k, :], x_conv[:, k, :], start=(k == 0), stop=(k == NH - 1))
            last.then_inc(s_bc, 1)

        def s_step_scalar(act, h):
            if h == 0:
                act.wait_ge(s_zg, 1)
            act.wait_ge(s_dtp, h + 1)
            nc.scalar.activation(sp_e[:, h, :], bank[5 + h][:, :], ACT.Abs, bias=b_dt[:, h:h + 1])
            nc.scalar.activation(sp_r[:, h, :], bank[5 + h][:, :], ACT.Relu, bias=b_dt[:, h:h + 1]).then_inc(s_sp1, 1)

        def s_exp_scalar(act):
            act.wait_ge(s_sp1, NH)
            nc.scalar.activation(sp_e[:, :, :], sp_e[:, :, :], ACT.Exp, scale=-1.0).then_inc(s_sp2, 1)

        def s_log_scalar(act):
            act.wait_ge(s_sp2, 1)
            nc.scalar.activation(sp_l[:, :, :], sp_e[:, :, :], ACT.Ln, bias=1.0).then_inc(s_sp3, 1)

        def s_step_vector(dve, k):
            if k == 0:
                dve.wait_ge(s_sp2, 1)
                nc.vector.tensor_scalar(sp_u[:, :, :], sp_e[:, :, :], 1.0, None, ALU.add).then_inc(s_spv, 1)
            elif k == 1:
                dve.wait_ge(s_spv, 1)
                nc.vector.scalar_tensor_tensor(sp_u[:, :, :], sp_u[:, :, :], 1.0, sp_e[:, :, :], ALU.subtract,
                                               ALU.subtract).then_inc(s_spv, 1)
            elif k == 2:
                dve.wait_ge(s_spv, 2)
                nc.vector.tensor_tensor(sp_r[:, :, :], sp_r[:, :, :], sp_u[:, :, :], ALU.subtract).then_inc(s_spv, 1)
            else:
                dve.wait_ge(s_spv, 3)
                dve.wait_ge(s_sp3, 1)
                nc.vector.tensor_tensor(dt_s[:, :, :], sp_r[:, :, :], sp_l[:, :, :], ALU.add).then_inc(s_dt, 1)
                dve.wait_ge(s_dt, 1)
                for k in range(2):
                    nc.vector.memset(segments(da[k])[:, :, 0:1], 0.0)
                nc.vector.tensor_tensor(dt_x[:, :, :], dt_s[:, :, :], x_conv[:, :, :], ALU.mult).then_inc(s_dt, 1)

        def segments(ap):
            return ap.rearrange("p h (b t) -> p (h b) t", b=2)

        def b_bank(n):
            return bank[4 if n % 2 == 0 else 1]

        def s_b_tensor(pe, n):
            if n == 0:
                pe.wait_ge(s_bcp, 1)
            elif n >= 2:
                pe.wait_ge(s_dbx, n - 1)
            nc.tensor.matmul(b_bank(n)[:, :], sel_n[:, n, :], bc_parts[:, :], start=True, stop=True).then_inc(s_bb, 1)

        def s_c_tensor(pe, n):
            if n == 0:
                pe.wait_ge(s_sp1, NH)
            else:
                pe.wait_ge(s_cs, n)
            nc.tensor.matmul(bank[5][:, :], sel_n[:, NS + n, :], bc_parts[:, :], start=True, stop=True).then_inc(s_cb, 1)

        def s_sum_tensor(pe, n):
            pe.wait_ge(s_hc, n + 1)
            for h in range(NH):
                last = nc.tensor.matmul(bank[6 + h][:, :], ident[:, :], ring[n % RING][:, h, :], start=(n == 0), stop=(n == NS - 1))
            last.then_inc(s_y, 1)

        def s_decay_scalar(act, n):
            act.wait_ge(s_dt, 2)
            if n >= 2:
                act.wait_ge(s_h, n - 1)
            for h in range(NH):
                last = nc.scalar.activation(segments(da[n % 2])[:, 2 * h:2 * h + 2, 1:], segments(dt_s[:, :, :])[:, 2 * h:2 * h + 2, 1:],
                                            ACT.Exp, scale=neg_a[:, h * NS + n:h * NS + n + 1])
            last.then_inc(s_da, 1)
            act.wait_ge(s_cb, n + 1)
            if n >= 2:
                act.wait_ge(s_hc, n - 1)
            nc.scalar.activation(c_s[n % 2], bank[5][:, :], ACT.Copy).then_inc(s_cs, 1)

        def s_input_vector(dve, n):
            dve.wait_ge(s_bb, n + 1)
            if n == 0:
                dve.wait_ge(s_dt, 2)
            if n >= RING:
                dve.wait_ge(s_y, n - RING + 1)
            nc.vector.tensor_tensor(ring[n % RING], dt_x[:, :, :], b_bank(n)[:, :].unsqueeze(1).broadcast_to([P, NH, TOK]),
                                    ALU.mult).then_inc(s_dbx, 1)

        def s_scan_vector(dve, n):
            dve.wait_ge(s_dbx, n + 1)
            dve.wait_ge(s_da, n + 1)
            r = ring[n % RING].rearrange("p h t -> p (h t)")
            nc.vector.tensor_tensor_scan(r, da[n % 2].rearrange("p h t -> p (h t)"), r, 0.0, ALU.mult, ALU.add).then_inc(s_h, 1)

        def s_read_gpsimd(pool, n):
            pool.wait_ge(s_h, n + 1)
            pool.wait_ge(s_cs, n + 1)
            r = ring[n % RING]
            nc.gpsimd.tensor_tensor(r, r, c_s[n % 2].unsqueeze(1).broadcast_to([P, NH, TOK]), ALU.mult).then_inc(s_hc, 1)

        def s_end_vector(dve):
            for h in range(NH):
                last = nc.vector.tensor_tensor(z_gate[:, h, :], z_gate[:, h, :], bank[6 + h][:, :], ALU.mult)
            last.then_inc(s_g, 1)
            dve.wait_ge(s_g, 1)
            for h in range(NH):
                last = nc.vector.scalar_tensor_tensor(z_gate[:, h, :], x_conv[:, h, :], d_par[:, h:h + 1], z_gate[:, h, :],
                                                      ALU.mult, ALU.add)
            last.then_inc(s_yv, 1)

        def f_out_tensor(pe):
            pe.wait_ge(s_yv, 1)
            for k in range(NH):
                last = nc.tensor.matmul(bank[3][:, :], wout_t[:, k, :], z_gate[:, k, :], start=(k == 0), stop=(k == NH - 1))
            last.then_inc(f_o, 1)

        def f_out_scalar(act, p):
            act.wait_ge(f_o, 1)
            gate_scalar(bank[3], y_f, p, 6 + GA, f_y)

        def f_res_tensor(pe):
            pe.wait_ge(f_y, 1)
            back_tensor(y_f, bank[3], f_back)

        def f_res_vector(dve):
            dve.wait_ge(f_back, 1)
            nc.vector.tensor_tensor(x_b[:, :, :], x_b[:, :, :], tokens(bank[3]), ALU.add).then_inc(f_x3, 1)
            dve.wait_ge(f_x3, 1)
            ln_stats_vector(dve, LN_F, x_b)

        def f_mix_tensor(pe):
            pe.wait_ge(f_h, 1)
            nc.tensor.matmul(bank[3][:, :], ffn_w[:, :], h_f[:, :], start=True, stop=True).then_inc(f_m, 1)

        def f_mix_scalar(act):
            act.wait_ge(f_m, 1)
            nc.scalar.activation(y_f[:, :], bank[3][:, :], ACT.Tanh, bias=ffn_b[:, :]).then_inc(f_t, 1)

        def f_gate_vector(dve, p):
            dve.wait_ge(f_t, 1)
            for b in range(2):
                last = nc.vector.tensor_scalar(half(y_f, b), half(y_f, b), scale_of(6 + GB, p, b), None, ALU.mult)
            last.then_inc(f_g, 1)

        def f_end_tensor(pe):
            pe.wait_ge(f_g, 1)
            back_tensor(y_f, bank[3], f_back)

        def f_end_vector(dve):
            dve.wait_ge(f_back, 2)
            nc.vector.tensor_tensor(x_b[:, :, :], x_b[:, :, :], tokens(bank[3]), ALU.add).then_inc(f_x, 1)

        FEW = NE // 2
        PREP0 = NE
        SLOTS = PREP0 + CHUNKS - FEW + VALUES + 1

        def chunk_of(slot):
            if slot < PREP0:
                return slot // 2 if slot % 2 == 0 else None
            return slot - PREP0 + FEW

        def projection_tensor(pe, slot):
            if slot == 1:
                f_out_tensor(pe)
            elif slot == 3:
                f_res_tensor(pe)
            elif slot == 6:
                ln_tensor(pe, LN_F, bank[3])
            elif slot == 7:
                f_mix_tensor(pe)
            elif slot == 9:
                f_end_tensor(pe)

        def projection_scalar(act, slot, p):
            if slot == 2:
                f_out_scalar(act, p)
            elif slot == 6:
                ln_out_scalar(act, LN_F, p, 6 + SB, 6 + CB, bank[3])
            elif slot == 8:
                f_mix_scalar(act)

        def projection_vector(dve, slot, p):
            if slot == 0:
                s_end_vector(dve)
            elif slot == 3:
                f_res_vector(dve)
            elif slot == 5:
                ln_norm_vector(dve, LN_F, x_b)
            elif slot == 8:
                f_gate_vector(dve, p)
            elif slot == 10:
                f_end_vector(dve)

        def prepare_tensor(pe, k):
            if k == 0:
                m_down_tensor(pe, NE - 1)
            elif k == 2:
                m_back_tensor(pe)
            elif k == 6:
                ln_tensor(pe, LN_S, bank[4])
            elif k == 7:
                s_in_tensor(pe, 0)
            elif k == 8:
                s_in_tensor(pe, 1)
            elif k == 14:
                s_proj_tensor(pe)
            elif k == 23:
                s_b_tensor(pe, 0)
                s_c_tensor(pe, 0)

        def prepare_scalar(act, k, p):
            if k == 1:
                m_end_scalar(act, p)
            elif k == 6:
                ln_out_scalar(act, LN_S, p, 6 + SA, 6 + CA, bank[4])
            elif k == 9:
                s_z_scalar(act)
            elif k == 10:
                s_conv_scalar(act, 0)
            elif k == 12:
                s_conv_scalar(act, 1)
            elif k in (15, 16):
                s_step_scalar(act, k - 15)
            elif k == 17:
                s_exp_scalar(act)
            elif k == 18:
                s_log_scalar(act)
            elif k == 19:
                split_first_scalar(act, bank[4], None, bc_parts, s_bc, s_bcc)
            elif k == 21:
                split_next_scalar(act, bc_parts, bc_rest, s_bcr, s_bcm)

        def prepare_vector(dve, k, after_f):
            if k == 3:
                m_end_vector(dve, after_f)
            elif k == 5:
                ln_norm_vector(dve, LN_S, x_b)
            elif k == 8:
                s_conv_vector(dve, 0)
            elif k == 10:
                s_conv_vector(dve, 1)
            elif k == 11:
                s_gate_vector(dve, 0)
                s_zgate_vector(dve)
            elif k == 13:
                s_gate_vector(dve, 1)
            elif k in (18, 19):
                s_step_vector(dve, k - 18)
            elif k == 20:
                s_step_vector(dve, 2)
                split_first_vector(dve, bank[4], bc_parts, bc_rest, s_bcc, s_bcr)
            elif k == 21:
                s_step_vector(dve, 3)
            elif k == 22:
                split_last_vector(dve, bc_parts, bc_rest, s_bcm, s_bcp)

        def next_tensor(pe, k):
            if k == 12:
                ln_tensor(pe, LN_A, bank[7])
            elif k == 15:
                a_keys_tensor(pe)

        def next_scalar(act, k, p, after_scores):
            if k == 13:
                ln_out_scalar(act, LN_A, p, SA, CA, bank[7])
            elif k == 16:
                a_keys_scalar(act, after_scores)

        def next_vector(dve, k):
            if k == 2:
                dve.wait_ge(xa_in, 16)
                ln_stats_vector(dve, LN_A, x_a)
            elif k == 4:
                ln_norm_vector(dve, LN_A, x_a)

        TAIL = (CHUNKS + INVERSE, CHUNKS + SCALED)
        ROUTE0, ROUTE_IN = 7, 4
        SPLIT0 = ROUTE0 + -(-ROUTE_STEPS // ROUTE_IN)
        assert SPLIT0 + 3 == NS == UNITS

        def start_tensor(pe, n, ps, pn):
            if ps is not None and n < len(TAIL):
                a_chunk_tensor(pe, TAIL[n], False)
            if pn is not None and n == 1:
                a_values_in_tensor(pe)
            if ps is not None:
                if n == 2:
                    a_end_tensor(pe)
                elif n == 3:
                    a_back_tensor(pe)
                elif n == 5:
                    ln_tensor(pe, LN_B, bank[2])
                elif n == 6:
                    m_logits_tensor(pe)
                elif n == SPLIT0:
                    m_route_tensor(pe)

        def start_scalar(act, n, ps, pn):
            if ps is not None and n < len(TAIL):
                a_chunk_scalar(act, TAIL[n])
            if pn is not None and n == 1:
                a_values_in_scalar(act)
            if ps is not None:
                if n == 2:
                    a_end_scalar(act, ps)
                elif n == 3:
                    ln_std_scalar(act, LN_B)
                elif n == 5:
                    ln_out_scalar(act, LN_B, ps, SB, CB, bank[2])
                elif n == 6:
                    m_logits_scalar(act)
                elif n == SPLIT0:
                    split_first_scalar(act, bank[2], w_rows, w_parts, m_wt, m_cp)
                elif n == SPLIT0 + 2:
                    split_next_scalar(act, w_parts, w_rest, m_rest, m_mid)

        def start_vector(dve, n, ps, pb):
            if ps is not None:
                if n < len(TAIL):
                    a_chunk_vector(dve, TAIL[n])
                elif n == 3:
                    a_end_vector(dve, pb is not None)
                    dve.wait_ge(a_res, 1)
                    ln_stats_vector(dve, LN_B, x1)
                elif n == 4:
                    ln_inverse_vector(dve, LN_B)
                    ln_norm_vector(dve, LN_B, x1)
                elif n == SPLIT0 + 1:
                    split_first_vector(dve, bank[2], w_parts, w_rest, m_cp, m_rest)
                elif n == SPLIT0 + 2:
                    split_last_vector(dve, w_parts, w_rest, m_mid, m_parts)

        def route_vector(dve, n, part):
            k = ROUTE_IN * (n - ROUTE0) + part
            if 0 <= k < ROUTE_STEPS:
                m_route_vector(dve, k)

        def turn(ps, pn, pb, pf):
            slots = range(SLOTS)
            scan = range(NS if ps is not None or pb is not None or pn is not None else 0)
            with nc.Block() as block:
                @block.sync
                def _(sp):
                    if pn is not None:
                        sp.dma_start(x_a[:, :, :], x_pair(pn)).then_inc(xa_in, 16)
                    if ps is not None:
                        sp.dma_start(x_res[:, :, :], x_pair(ps)).then_inc(xr_in, 16)
                    if pf is not None:
                        sp.wait_ge(f_x, 1)
                        sp.dma_start(out[pf].rearrange("(t q) d -> q t d", q=P), x_b[:, :, :]).then_inc(o_out, 16)
                    if ps is not None:
                        for q in range(PIECES):
                            sp.wait_ge(a_s, CHUNKS // 2 // PIECES * (q + 1))
                            a_spread_sync(sp, 1, q)
                    if pn is not None:
                        if ps is not None:
                            sp.wait_ge(a_s, CHUNKS)
                        sp.wait_ge(a_kc, 1)
                        for q in range(PIECES):
                            a_spread_sync(sp, 0, q)
                    for q in range(PIECES):
                        if ps is not None or pn is not None:
                            sp.wait_ge(ke_in[q], 16 if ps is None or pn is None else 32)
                    if pf is not None:
                        sp.wait_ge(o_out, 16)

                @block.gpsimd
                def _(pool):
                    if pf is not None:
                        ln_root_gpsimd(pool, LN_F)
                    if pn is not None:
                        ln_root_gpsimd(pool, LN_A)
                    if pb is not None:
                        ln_root_gpsimd(pool, LN_S)
                    if pb is not None:
                        for n in range(NS):
                            s_read_gpsimd(pool, n)

                @block.tensor
                def _(pe):
                    if pb is not None:
                        m_up_tensor(pe, 0)
                    for slot in slots:
                        if pf is not None:
                            projection_tensor(pe, slot)
                        if pb is not None:
                            if slot < NE:
                                m_weight_tensor(pe, slot, pf is not None)
                            else:
                                prepare_tensor(pe, slot - PREP0)
                        if pn is not None:
                            next_tensor(pe, slot - PREP0)
                        if ps is not None and chunk_of(slot) is not None:
                            a_chunk_tensor(pe, chunk_of(slot), pf is not None)
                        if pb is not None and slot < NE:
                            m_expert_tensor(pe, slot)
                    for n in scan:
                        if pn is not None:
                            a_query_tensor(pe, n)
                        if pb is not None and n == 0:
                            s_b_tensor(pe, 1)
                        if pb is not None and n + 2 < NS:
                            s_b_tensor(pe, n + 2)
                        if pb is not None and n + 1 < NS:
                            s_c_tensor(pe, n + 1)
                        start_tensor(pe, n, ps, pn)
                        if pb is not None and n:
                            s_sum_tensor(pe, n - 1)
                    if pb is not None:
                        s_sum_tensor(pe, NS - 1)

                @block.scalar
                def _(act):
                    for slot in slots:
                        if pf is not None:
                            projection_scalar(act, slot, pf)
                        if pb is not None:
                            if slot < NE:
                                m_expert_scalar(act, slot)
                            else:
                                prepare_scalar(act, slot - PREP0, pb)
                        if pn is not None:
                            next_scalar(act, slot - PREP0, pn, ps is not None)
                        if ps is not None and chunk_of(slot) is not None:
                            a_chunk_scalar(act, chunk_of(slot))
                    if pb is not None:
                        s_decay_scalar(act, 0)
                    for n in scan:
                        if pb is not None and n + 1 < NS:
                            s_decay_scalar(act, n + 1)
                        start_scalar(act, n, ps, pn)

                @block.vector
                def _(dve):
                    for slot in slots:
                        if pf is not None:
                            projection_vector(dve, slot, pf)
                        if pb is not None and slot >= PREP0:
                            prepare_vector(dve, slot - PREP0, pf is not None)
                        if pn is not None:
                            next_vector(dve, slot - PREP0)
                        if pb is not None and slot < NE:
                            m_expert_vector(dve, slot)
                        if ps is not None and chunk_of(slot) is not None:
                            a_chunk_vector(dve, chunk_of(slot))
                    for n in scan:
                        if pb is not None:
                            s_input_vector(dve, n)
                        if ps is not None:
                            route_vector(dve, n, 0)
                        if pb is not None:
                            s_scan_vector(dve, n)
                        if ps is not None:
                            route_vector(dve, n, 1)
                        if pn is not None:
                            a_query_vector(dve, n)
                        if ps is not None:
                            route_vector(dve, n, 2)
                        start_vector(dve, n, ps, pb)
                        if ps is not None:
                            route_vector(dve, n, 3)
            clear_semaphores()

        turn(None, 0, None, None)
        turn(0, 1, None, None)
        turn(1, 2, 0, None)
        with nc.Fori(2, PAIRS - 1) as t:
            turn(t, t + 1, t - 1, t - 2)
        turn(PAIRS - 1, None, PAIRS - 2, PAIRS - 3)
        turn(None, None, PAIRS - 1, PAIRS - 2)
        turn(None, None, None, PAIRS - 1)


def kernel(**inputs):
    import numpy as np
    import concourse.bacc as bacc
    from concourse.bass_utils import run_bass_kernel_spmd as run

    f = {k: np.asarray(v) for k, v in inputs.items()}
    one = np.float32

    def cols(w):
        return w.transpose(2, 0, 1).reshape(w.shape[2], -1)

    def halves(w):
        return w.reshape(NH, P, -1).transpose(1, 0, 2).reshape(P, -1)

    wq = f["L0_attn_Wq"].reshape(H, HD, D)
    wo = f["L0_attn_Wo"].reshape(D, G, H // G, HD)
    wo_x = np.zeros((H // G, G, HD, G, D), one)
    for g in range(G):
        wo_x[:, g, :, g, :] = wo[:, g].transpose(1, 2, 0)
    i, a, k = np.arange(NB), np.arange(QB), np.arange(T)
    dist = np.clip(QB * i[None, :, None] + a[:, None, None] - k[None, None, :], 1 - MAX_POS, MAX_POS - 1) + MAX_POS - 1
    e_shift = f["L0_attn_E"][dist].transpose(0, 3, 1, 2)
    b2 = np.zeros((SROWS, D), one)
    b2[:NE] = f["L0_ffn_b2"]
    w_x = f["L1_attn_W_x"]
    rows = np.arange(QROWS)
    mask_q = np.zeros((QROWS, G, QB), one)
    for r in rows:
        if r < KROWS:
            mask_q[r, r // HD, :] = (1.0 / HD) ** 0.5
        else:
            mask_q[r, :, (r - KROWS) // HD] = (1.0 / HD) ** 0.5
    ha = np.arange(P)
    mask_d = ((ha[:, None] // QB // (H // G) == np.arange(G * QB)[None, :] // QB)
              & (ha[:, None] % QB == np.arange(G * QB)[None, :] % QB)).astype(one)
    sel_r = (ha[:, None] // QB % (H // G) == np.arange(P)[None, :] // 32).astype(one)
    j = np.arange(NG)
    tie = np.tile((j[None, :] < j[:, None]).astype(one).reshape(1, -1), (P, 1))
    bf16 = mybir.dt.np(BF16)
    sel_n = np.repeat((np.arange(SROWS)[:, None] % 32 == np.arange(32)[None, :]), P, axis=1).astype(bf16)

    arrays = {
        "x": f["L0_attn_x"], "wq_rep": np.tile(wq.transpose(2, 0, 1), (1, 1, QROWS // HD)), "wk_t": f["L0_attn_Wk"].T,
        "wv_t": np.tile(f["L0_attn_Wv"].T, (1, P // KROWS)), "wo_x": wo_x, "e_shift": e_shift,
        "wg_t": np.tile(f["L0_ffn_Wg"].T, (1, P // NE)), "w1_t": cols(f["L0_ffn_W1"]), "w3_t": cols(f["L0_ffn_W3"]),
        "w2_t": cols(f["L0_ffn_W2"]), "b1_c": f["L0_ffn_b1"].T, "b3_c": f["L0_ffn_b3"].T, "b2_r": b2,
        "c_t": np.concatenate([f["L0_c"].T, f["L1_c"].T], 1), "wmod": np.concatenate([f["L0_wmod"], f["L1_wmod"]], 1),
        "win_t": f["L1_attn_W_in"].T, "conv_w": halves(f["L1_attn_conv_w"][:, 0, :]), "conv_b": halves(f["L1_attn_conv_b"][:, None]),
        "wx_bc": halves(np.tile(w_x[DTR:].T, (1, PARTS))), "wx_dt": w_x[:DTR], "wdt_t": f["L1_attn_W_dt"].T,
        "b_dt": halves(f["L1_attn_b_dt"][:, None]), "a_log": halves(f["L1_attn_A_log"]), "d_par": halves(f["L1_attn_D_param"][:, None]),
        "wout_t": halves(f["L1_attn_W_out"].T), "ffn_w_t": f["L1_ffn_weight"].T, "ffn_a1": f["L1_ffn_aux_weight1"],
        "ffn_a2": f["L1_ffn_aux_weight2"], "ffn_b": f["L1_ffn_bias"][:, None], "ident": np.eye(P, dtype=one),
        "mask_q": mask_q, "mask_d": mask_d, "sel_r": sel_r, "tie": tie, "sel_n": sel_n,
    }
    nc = bacc.Bacc("TRN2", target_bir_lowering=False, num_devices=1)
    dram, given = {}, {}
    for name, shape in IN_SHAPES:
        v = np.ascontiguousarray(arrays[name].reshape(shape))
        given[f"in_{name}"] = v
        dram[name] = nc.dram_tensor(f"in_{name}", shape, BF16 if name == "sel_n" else F32, kind="ExternalInput").ap()
    out = nc.dram_tensor("out", (PAIRS, TOK, D), F32, kind="ExternalOutput").ap()
    build(nc, dram, out)
    r = run(nc, [given], core_ids=[0])
    return r.results[0]["out"].reshape(B, T, D)
```

```python
from contextlib import ExitStack

import concourse.bass as bass
from concourse import mybir

F32 = mybir.dt.float32
BF16 = mybir.dt.bfloat16
I32 = mybir.dt.int32
ALU = mybir.AluOpType
ACT = mybir.ActivationFunctionType
AX_X = mybir.AxisListType.X

P = 128
B, T, D = 32, 256, 128
PAIRS = B // 2
TOK = 2 * T
TILES = TOK // P
EPS = 1e-5
H, G, HD = 16, 4, 8
QB = 8
NB = T // QB
KROWS = G * HD
QROWS = KROWS + QB * HD
MAX_POS = 128
CHUNKS = 2 * NB // 2
GROUPS = 4
CPG = CHUNKS // GROUPS
BPG = 2 * CPG
PIECES = 4
NE, NG, TOPK, TOPG, ROUTE_SCALE = 16, 4, 4, 2, 2.5
DI, NH, NS, DTR, KC = 256, 2, 16, 8, 4
PARTS = 3
SROWS = PARTS * 32
LATE = 2
RING = 6
ROOT_SEED = 0x5F3759DF
ROOT_STEPS = 3
SA, CA, GA, SB, CB, GB = range(6)

IN_SHAPES = [
    ("x", (PAIRS, TOK, D)), ("wq_rep", (P, H * QROWS)), ("wk_t", (P, KROWS)), ("wv_t", (P, P)),
    ("wo_x", (P, G * D)), ("e_shift", (QB * HD, NB * T)), ("wg_t", (P, P)), ("w1_t", (P, NE * P)),
    ("w3_t", (P, NE * P)), ("w2_t", (P, NE * P)), ("b1_c", (P, NE)), ("b3_c", (P, NE)), ("b2_r", (SROWS, D)),
    ("c_t", (P, 2 * B)), ("wmod", (P, 2 * 6 * D)), ("win_t", (P, 2 * DI)), ("conv_w", (P, NH * KC)),
    ("conv_b", (P, NH)), ("wx_bc", (P, NH * SROWS)), ("wx_dt", (DTR, DI)), ("wdt_t", (DTR, DI)),
    ("b_dt", (P, NH)), ("a_log", (P, NH * NS)), ("d_par", (P, NH)), ("wout_t", (P, NH * D)),
    ("ffn_w_t", (P, D)), ("ffn_a1", (P, D)), ("ffn_a2", (P, D)), ("ffn_b", (P, 1)),
    ("ident", (P, P)), ("mask_q", (QROWS, G * QB)), ("mask_d", (P, G * QB)), ("sel_r", (P, P)),
    ("tie", (P, NG * NG)), ("sel_n", (SROWS, 32 * P)),
]


def build(nc, dram, out):
    ctx = ExitStack()
    with ctx:
        sems = []

        def sb(name, shape, dt=F32):
            return ctx.enter_context(nc.sbuf_tensor(name, shape, dt))

        def sem(name):
            s = ctx.enter_context(nc.semaphore(name))
            sems.append(s)
            return s

        bank = [ctx.enter_context(nc.psum_tensor(f"bank{k}", [P, 512], F32)) for k in range(8)]

        wq_rep = sb("wq_rep", [P, H, QROWS])
        wk_t = sb("wk_t", [P, KROWS])
        wv_t = sb("wv_t", [P, P])
        wo_x = sb("wo_x", [P, G, D])
        wg_t = sb("wg_t", [P, P])
        w1_t = sb("w1_t", [P, NE, P])
        w3_t = sb("w3_t", [P, NE, P])
        w2_t = sb("w2_t", [P, NE, P])
        b1_c = sb("b1_c", [P, NE])
        b3_c = sb("b3_c", [P, NE])
        b2_r = sb("b2_r", [SROWS, D])
        win_t = sb("win_t", [P, 2 * DI])
        conv_w = sb("conv_w", [P, NH, KC])
        conv_b = sb("conv_b", [P, NH])
        wx_bc = sb("wx_bc", [P, NH, SROWS])
        w_dtx = sb("w_dtx", [P, NH, DI])
        b_dt = sb("b_dt", [P, NH])
        neg_a = sb("neg_a", [P, NH * NS])
        d_par = sb("d_par", [P, NH])
        wout_t = sb("wout_t", [P, NH, D])
        ffn_w = sb("ffn_w", [P, D])
        ffn_b = sb("ffn_b", [P, 1])
        ident = sb("ident", [P, P])
        mask_q = sb("mask_q", [QROWS, G, QB])
        mask_d = sb("mask_d", [P, G * QB])
        sel_r = sb("sel_r", [P, P])
        tie = sb("tie", [P, NG * NG])
        sel_n = sb("sel_n", [SROWS, 32, P], BF16)
        mod = sb("mod", [P, 12, B])
        eps_c = sb("eps_c", [P, 1])
        zero64 = sb("zero64", [P, NE])

        x_a = sb("x_a", [P, TILES, D])
        x_res = sb("x_res", [P, TILES, D])
        st_a = sb("st_a", [P, TILES, 6])
        mv_a = sb("mv_a", [P, TILES, 2])
        sd_a = sb("sd_a", [P, TILES])
        rstd_a = sb("rstd_a", [P, TILES])
        nw_a = sb("nw_a", [P, TILES])
        h_a = sb("h_a", [P, TOK])
        k_t = sb("k_t", [KROWS, TOK])
        v_s = sb("v_s", [P, TILES, KROWS])
        q_all = sb("q_all", [P, 2 * NB, H, QB])
        q_st = q_all[0:QROWS]
        ke = sb("ke", [QROWS, NB, T])
        nmax = sb("nmax", [P, 2 * NB])
        rsum = sb("rsum", [P, 2 * NB])
        rinv = sb("rinv", [P, 2 * NB])
        probs = sb("probs", [P, 2, 2, T])
        probs_t = sb("probs_t", [P, 2, BPG, P])
        ao_raw = sb("ao_raw", [P, 512])
        ao = q_all[:, 0:BPG].rearrange("p i h a -> p (i h a)").rearrange("p (i g a) -> p i g a", g=G, a=QB)
        y_a = sb("y_a", [P, TOK])
        xn_a = y_a[:, :].rearrange("p (t d) -> p t d", t=TILES)
        x1 = sb("x1", [P, TILES, D])

        x_b = sb("x_b", [P, TILES, D])
        st_b = sb("st_b", [P, TILES, 6])
        mv_b = sb("mv_b", [P, TILES, 2])
        sd_b = sb("sd_b", [P, TILES])
        rstd_b = sb("rstd_b", [P, TILES])
        nw_b = sb("nw_b", [P, TILES])
        h_b = sb("h_b", [P, TOK])
        y_b = sb("y_b", [P, TOK])
        xn_b = y_b[:, :].rearrange("p (t d) -> p t d", t=TILES)
        st_f = sb("st_f", [P, TILES, 6])
        mv_f = sb("mv_f", [P, TILES, 2])
        sd_f = sb("sd_f", [P, TILES])
        rstd_f = sb("rstd_f", [P, TILES])
        nw_f = sb("nw_f", [P, TILES])
        h_f = sb("h_f", [P, TOK])
        dg = h_f[:, :].rearrange("p (i c) -> p i c", i=BPG)
        y_f = sb("y_f", [P, TOK])
        xn_f = y_f[:, :].rearrange("p (t d) -> p t d", t=TILES)
        gate = sb("gate", [P, TILES, NE])
        score = sb("score", [P, TILES, NE])
        masked = sb("masked", [P, TILES, NE])
        picked = sb("picked", [P, TILES, NE])
        equal = sb("equal", [P, TILES, NE])
        prefix = sb("prefix", [P, TILES, NE])
        top8 = sb("top8", [P, TILES, 8])
        few = sb("few", [P, TILES])
        gmax = sb("gmax", [P, TILES, NG])
        beats = sb("beats", [P, TILES, NG, NG])
        ties = sb("ties", [P, TILES, NG, NG])
        grank = sb("grank", [P, TILES, NG])
        we96 = sb("we96", [P, TILES, SROWS])
        w_parts = sb("w_parts", [SROWS, TOK], BF16)
        bc_parts = sb("bc_parts", [SROWS, TOK], BF16)
        x_conv = sb("x_conv", [P, NH, TOK])
        z_gate = sb("z_gate", [P, NH, TOK])
        dt_s = sb("dt_s", [P, NH, TOK])
        dt_x = sb("dt_x", [P, NH, TOK])
        work = sb("work", [P, 6 * 1024])

        def cut(lo, n):
            return work[:, lo:lo + n]

        th = [cut(2048 + k * 512, 512) for k in range(2)]
        zh = [cut(5120 + k * 512, 512) for k in range(2)]
        uh = [cut(3072 + k * 512, 512) for k in range(2)]
        w_rest = h_f[:, :]
        w_rows = ao_raw[:, :]
        CONV = 512
        acc = cut(CONV, 1024).rearrange("p (h t) -> p h t", h=NH)
        act_t = cut(CONV + 1024, 1024).rearrange("p (h t) -> p h t", h=NH)
        act_z = cut(CONV + 2048, 1024).rearrange("p (h t) -> p h t", h=NH)
        gz_t = cut(CONV + 3072, 1024).rearrange("p (h t) -> p h t", h=NH)
        sp_e = acc
        sp_l = act_t
        sp_u = act_z
        sp_r = gz_t
        bc_rest = cut(5120, 512)
        da = [cut(k * 1024, 1024).rearrange("p (h t) -> p h t", h=NH) for k in range(2)]
        ring = [cut(2048 + k * 1024, 1024).rearrange("p (h t) -> p h t", h=NH) for k in range(3)]
        spare = probs_t[:, :, :, :].rearrange("p k i c -> p (k i c)")
        ring += [spare[:, k * 1024:(k + 1) * 1024].rearrange("p (h t) -> p h t", h=NH) for k in range(RING - 3)]
        c_s = [cut(5120 + k * 512, 512) for k in range(2)] + [spare[:, 3072 + k * 512:3584 + k * 512] for k in range(2)]

        loaded_late = ctx.enter_context(nc.semaphore("loaded_late"))
        loaded = sem("loaded")
        cleared = sem("cleared")
        g0 = sem("g0")
        s_silu = sem("s_silu")
        s_mod = sem("s_mod")
        s_modv = sem("s_modv")
        s_nega = sem("s_nega")
        s_dtx = sem("s_dtx")
        s_m1 = sem("s_m1")
        s_m1c = sem("s_m1c")
        s_wc = sem("s_wc")

        wmod = probs_t[:, :, :, :].rearrange("p a b c -> p (a b c)")[:, 0:2 * 6 * D]
        c_t = h_f[:, 0:2 * B]
        c_silu = h_f[:, 2 * B:4 * B]
        ffn_w_t, ffn_a1, ffn_a2, ffn_m1 = (x_b[:, k, :] for k in range(4))
        wx_dt = y_b[0:DTR, 0:DI]
        wdt_t = y_b[0:DTR, DI:2 * DI]
        sgn = y_a[:, 0:B]

        def flat(t):
            n = len(t.shape)
            return t[:, :] if n == 2 else t[:, :, :].rearrange("p a b -> p (a b)")

        loads = [("wq_rep", flat(wq_rep)), ("wk_t", flat(wk_t)), ("wv_t", flat(wv_t)), ("wo_x", flat(wo_x)),
                 ("e_shift", ke[KROWS:QROWS, :, :].rearrange("p a b -> p (a b)")), ("wg_t", flat(wg_t)),
                 ("w1_t", flat(w1_t)), ("w3_t", flat(w3_t)), ("w2_t", flat(w2_t)), ("b1_c", flat(b1_c)),
                 ("b3_c", flat(b3_c)), ("b2_r", flat(b2_r)), ("c_t", c_t), ("wmod", wmod), ("win_t", flat(win_t)),
                 ("conv_w", flat(conv_w)), ("conv_b", flat(conv_b)), ("wx_bc", flat(wx_bc)), ("wx_dt", wx_dt),
                 ("wdt_t", wdt_t), ("b_dt", flat(b_dt)), ("a_log", flat(neg_a)), ("d_par", flat(d_par)),
                 ("wout_t", flat(wout_t)), ("ffn_w_t", ffn_w_t), ("ffn_a1", ffn_a1), ("ffn_a2", ffn_a2),
                 ("ffn_b", flat(ffn_b)), ("ident", flat(ident)), ("mask_q", flat(mask_q)), ("mask_d", flat(mask_d)),
                 ("sel_r", flat(sel_r)), ("tie", flat(tie)), ("sel_n", flat(sel_n))]
        late_names = ("w1_t", "w3_t", "w2_t", "e_shift", "sel_n", "win_t", "wo_x", "wout_t", "wx_bc", "wg_t", "b2_r", "b3_c",
                      "mask_d", "sel_r", "tie")
        late_loads = [load for load in loads if load[0] in late_names]
        loads = [load for load in loads if load[0] not in late_names]
        LOADED, LOADED_LATE = 16 * len(loads), 16 * len(late_loads)

        def x_pair(p):
            return dram["x"][p].rearrange("(t q) d -> q t d", q=P)

        with nc.Block() as block:
            @block.sync
            def _(sp):
                for name, dst in loads:
                    sp.dma_start(dst, dram[name]).then_inc(loaded, 16)

            @block.gpsimd
            def _(pool):
                nc.gpsimd.memset(we96[:, :, :], 0.0)
                nc.gpsimd.memset(eps_c[:, :], EPS)
                nc.gpsimd.memset(zero64[:, :], 0.0)

            @block.tensor
            def _(pe):
                pe.wait_ge(loaded, LOADED)
                pe.wait_ge(s_silu, 1)
                for m in range(12):
                    last = nc.tensor.matmul(bank[0][:, m * B:(m + 1) * B], wmod[:, m * D:(m + 1) * D],
                                            c_silu[:, (m // 6) * B:(m // 6 + 1) * B], start=True, stop=True)
                last.then_inc(s_mod, 1)
                for k in range(NH):
                    last = nc.tensor.matmul(bank[1 + k][:, 0:DI], wx_dt[:, k * P:(k + 1) * P], wdt_t, start=True, stop=True)
                last.then_inc(s_dtx, 1)
                nc.tensor.matmul(bank[3][:, 0:D], ffn_a1, ffn_w_t, start=True, stop=True).then_inc(s_m1, 1)
                pe.wait_ge(s_m1c, 1)
                nc.tensor.matmul(bank[4][:, 0:D], ffn_m1, ffn_a2, start=True, stop=True).then_inc(s_wc, 1)

            @block.scalar
            def _(act):
                act.wait_ge(loaded, LOADED)
                nc.scalar.activation(c_silu, c_t, ACT.Silu).then_inc(s_silu, 1)
                nc.scalar.activation(neg_a[:, :], neg_a[:, :], ACT.Exp).then_inc(s_nega, 1)
                act.wait_ge(s_dtx, 1)
                for k in range(NH):
                    nc.scalar.activation(w_dtx[:, k, :], bank[1 + k][:, 0:DI], ACT.Copy)
                act.wait_ge(s_m1, 1)
                nc.scalar.activation(ffn_m1, bank[3][:, 0:D], ACT.Copy).then_inc(s_m1c, 1)
                act.wait_ge(s_wc, 1)
                nc.scalar.activation(ffn_w[:, :], bank[4][:, 0:D], ACT.Copy)

            @block.vector
            def _(dve):
                dve.wait_ge(loaded, LOADED)
                nc.vector.tensor_scalar(b1_c[:, :], b1_c[:, :], 0.5, None, ALU.mult)
                nc.vector.tensor_scalar(conv_b[:, :], conv_b[:, :], 0.5, None, ALU.mult)
                dve.wait_ge(s_nega, 1)
                nc.vector.tensor_scalar(neg_a[:, :], neg_a[:, :], -1.0, None, ALU.mult)
                dve.wait_ge(s_mod, 1)
                n = 0
                for m in range(12):
                    src = bank[0][:, m * B:(m + 1) * B]
                    if m % 6 in (SA, SB):
                        nc.vector.tensor_copy(mod[:, m, :], src)
                    elif m % 6 in (CA, CB):
                        nc.vector.tensor_scalar(mod[:, m, :], src, 1.0, None, ALU.add)
                    else:
                        nc.vector.tensor_scalar(sgn, src, 0.0, 2.0, ALU.is_ge, ALU.mult).then_inc(s_modv, 1)
                        nc.vector.tensor_scalar(mod[:, m, :], src, -1.0, None, ALU.mult).then_inc(s_modv, 1)
                        dve.wait_ge(s_modv, n + 2)
                        nc.vector.tensor_tensor(mod[:, m, :], mod[:, m, :], src, ALU.max).then_inc(s_modv, 1)
                        dve.wait_ge(s_modv, n + 3)
                        nc.vector.tensor_scalar(mod[:, m, :], mod[:, m, :], 0.25, None, ALU.max).then_inc(s_modv, 1)
                        n += 4
                        dve.wait_ge(s_modv, n)
                        nc.vector.scalar_tensor_tensor(mod[:, m, :], sgn, -1.0, mod[:, m, :], ALU.add, ALU.mult).then_inc(s_modv, 1)
                        n += 1
                        dve.wait_ge(s_modv, n)

        xa_in, xr_in = sem("xa_in"), sem("xr_in")
        ke_in = [sem(f"ke_in{q}") for q in range(PIECES)]
        a_st, a_mv, a_sd, a_rstd, a_xn, a_tr, a_h = (sem("a_" + n) for n in ("st", "mv", "sd", "rstd", "xn", "tr", "h"))
        b_st, b_mv, b_sd, b_rstd, b_xn, b_tr, b_h = (sem("b_" + n) for n in ("st", "mv", "sd", "rstd", "xn", "tr", "h"))
        a_k, a_kc, a_v, a_vc, a_q, a_qm = (sem("a_" + n) for n in ("k", "kc", "v", "vc", "q", "qm"))
        a_s, a_max, a_exp, a_t, a_tc, a_pv, a_ao, a_inv, a_dg, a_r, a_on = (
            sem("a_" + n) for n in ("s", "max", "exp", "t", "tc", "pv", "ao", "inv", "dg", "r", "on"))
        a_wo, a_y, a_back, a_res = (sem("a_" + n) for n in ("wo", "y", "back", "res"))
        m_logit, m_exp, m_ch, m_wt, m_cp, m_rest, m_mid, m_parts = (
            sem("m_" + n) for n in ("logit", "exp", "ch", "wt", "cp", "rest", "mid", "parts"))
        m_h1, m_h3, m_wb, m_tz, m_u, m_a, m_b, m_hh, m_w2 = (sem("m_" + n) for n in ("h1", "h3", "wb", "tz", "u", "a", "b", "hh", "w2"))
        b_y, b_back, b_x = sem("b_y"), sem("b_back"), sem("b_x")
        s_xz, s_z, s_zg, s_cv, s_cz, s_ct, s_xc, s_bc, s_bcc, s_bcr, s_bcm, s_bcp = (
            sem("s_" + n) for n in ("xz", "z", "zg", "cv", "cz", "ct", "xc", "bc", "bcc", "bcr", "bcm", "bcp"))
        s_dtp, s_spr, s_sp1, s_sp2, s_sp3, s_spv, s_dt = (sem("s_" + n) for n in ("dtp", "spr", "sp1", "sp2", "sp3", "spv", "dt"))
        s_bb, s_cb, s_da, s_cs, s_dbx, s_h, s_hc, s_hs, s_late, s_y, s_g, s_yv = (
            sem("s_" + n) for n in ("bb", "cb", "da", "cs", "dbx", "h", "hc", "hs", "late", "y", "g", "yv"))
        a_nw, n_nw, f_nw = sem("a_nw"), sem("n_nw"), sem("f_nw")
        n_st, n_mv, n_sd, n_rstd, n_xn, n_tr, n_h = (sem("n_" + n) for n in ("st", "mv", "sd", "rstd", "xn", "tr", "h"))
        s_hl, s_yl, f_o, f_y, f_back, f_x3, f_m, f_t, f_g, f_x, o_out = (
            sem(n) for n in ("s_hl", "s_yl", "f_o", "f_y", "f_back", "f_x3", "f_m", "f_t", "f_g", "f_x", "o_out"))
        f_st, f_mv, f_sd, f_rstd, f_xn, f_tr, f_h = (sem("f_" + n) for n in ("st", "mv", "sd", "rstd", "xn", "tr", "h"))
        numbers = sorted(s.num for s in sems)
        assert numbers == list(range(numbers[0], numbers[0] + len(sems)))

        def clear_semaphores():
            with nc.Block() as block:
                @block.sync
                def _(sp):
                    sp.sem_clear(range(numbers[0], numbers[-1] + 1))

        clear_semaphores()

        LN_A = dict(nw=nw_a, s_nw=a_nw, st=st_a, mv=mv_a, sd=sd_a, rstd=rstd_a, xn=xn_a, h=h_a, s_st=a_st, s_mv=a_mv, s_sd=a_sd,
                    s_rstd=a_rstd, s_xn=a_xn, s_tr=a_tr, s_h=a_h)
        LN_B = dict(st=st_b, mv=mv_b, sd=sd_b, rstd=rstd_b, xn=xn_b, h=h_b, s_st=b_st, s_mv=b_mv, s_sd=b_sd,
                    s_rstd=b_rstd, s_xn=b_xn, s_tr=b_tr, s_h=b_h)
        LN_S = dict(nw=nw_b, s_nw=n_nw, st=st_b, mv=mv_b, sd=sd_b, rstd=rstd_b, xn=xn_b, h=h_b, s_st=n_st, s_mv=n_mv, s_sd=n_sd,
                    s_rstd=n_rstd, s_xn=n_xn, s_tr=n_tr, s_h=n_h)
        LN_F = dict(nw=nw_f, s_nw=f_nw, st=st_f, mv=mv_f, sd=sd_f, rstd=rstd_f, xn=xn_f, h=h_f, s_st=f_st, s_mv=f_mv, s_sd=f_sd,
                    s_rstd=f_rstd, s_xn=f_xn, s_tr=f_tr, s_h=f_h)

        def scale_of(m, p, b):
            return mod[:, m, bass.ds(2 * p + b, 1)]

        def half(ap, b):
            return ap[:, b * T:(b + 1) * T]

        def tile(ap, t):
            return ap[:, t * P:(t + 1) * P]

        def ln_stats_vector(dve, L, x):
            for t in range(TILES):
                last = nc.vector.bn_stats(L["st"][:, t, :], x[:, t, :])
            last.then_inc(L["s_st"], 1)
            dve.wait_ge(L["s_st"], 1)
            for t in range(TILES):
                last = nc.vector.bn_aggr(L["mv"][:, t, :], L["st"][:, t, :])
            last.then_inc(L["s_mv"], 1)

        def ln_std_scalar(act, L):
            act.wait_ge(L["s_mv"], 1)
            nc.scalar.activation(L["sd"][:, :], L["mv"][:, :, 1], ACT.Sqrt, bias=eps_c[:, :]).then_inc(L["s_sd"], 1)

        def ln_inverse_vector(dve, L):
            dve.wait_ge(L["s_sd"], 1)
            nc.vector.reciprocal(L["rstd"][:, :], L["sd"][:, :]).then_inc(L["s_rstd"], 1)

        def ln_root_gpsimd(pool, L):
            v, y, t, n = L["sd"][:, :], L["rstd"][:, :], L["nw"][:, :], 2
            pool.wait_ge(L["s_mv"], 1)
            nc.gpsimd.tensor_scalar(v, L["mv"][:, :, 1], EPS, None, ALU.add).then_inc(L["s_nw"], 1)
            pool.wait_ge(L["s_nw"], 1)
            nc.gpsimd.tensor_scalar(y.bitcast(I32), v.bitcast(I32), -0.5, float(ROOT_SEED), ALU.mult, ALU.add).then_inc(L["s_nw"], 1)
            for k in range(ROOT_STEPS):
                pool.wait_ge(L["s_nw"], n)
                nc.gpsimd.tensor_tensor(t, v, y, ALU.mult).then_inc(L["s_nw"], 1)
                pool.wait_ge(L["s_nw"], n + 1)
                nc.gpsimd.tensor_tensor(t, t, y, ALU.mult).then_inc(L["s_nw"], 1)
                pool.wait_ge(L["s_nw"], n + 2)
                nc.gpsimd.tensor_scalar(t, t, -0.5, 1.5, ALU.mult, ALU.add).then_inc(L["s_nw"], 1)
                pool.wait_ge(L["s_nw"], n + 3)
                nc.gpsimd.tensor_tensor(y, y, t, ALU.mult).then_inc(L["s_rstd"] if k == ROOT_STEPS - 1 else L["s_nw"], 1)
                n += 4

        def ln_norm_vector(dve, L, x):
            dve.wait_ge(L["s_rstd"], 1)
            for t in range(TILES):
                last = nc.vector.tensor_scalar(L["xn"][:, t, :], x[:, t, :], L["mv"][:, t, 0:1], L["rstd"][:, t:t + 1],
                                               ALU.subtract, ALU.mult)
            last.then_inc(L["s_xn"], 1)

        def ln_tensor(pe, L, dst):
            pe.wait_ge(L["s_xn"], 1)
            for t in range(TILES):
                last = nc.tensor.transpose(tile(dst, t), L["xn"][:, t, :], ident[:, :])
            last.then_inc(L["s_tr"], 1)

        def ln_out_scalar(act, L, p, shift, scale, src):
            act.wait_ge(L["s_tr"], 1)
            for b in range(2):
                last = nc.scalar.activation(half(L["h"], b), half(src, b), ACT.Identity, bias=scale_of(shift, p, b),
                                            scale=scale_of(scale, p, b))
            last.then_inc(L["s_h"], 1)

        def gate_scalar(src, y, p, m, done):
            for b in range(2):
                last = nc.scalar.activation(half(y, b), half(src, b), ACT.Identity, bias=0.0, scale=scale_of(m, p, b))
            last.then_inc(done, 1)

        def back_tensor(y, dst, done):
            for t in range(TILES):
                last = nc.tensor.transpose(tile(dst, t), tile(y, t), ident[:, :])
            last.then_inc(done, 1)

        def tokens(ap):
            return ap.rearrange("p (t d) -> p t d", t=TILES)

        def a_keys_tensor(pe, with_b):
            pe.wait_ge(a_h, 1)
            if with_b:
                pe.wait_ge(s_zg, NH)
            nc.tensor.matmul(bank[7][0:KROWS, :], wk_t[:, :], h_a[:, :], start=True, stop=True).then_inc(a_k, 1)

        def a_values_in_tensor(pe):
            for t in range(TILES):
                last = nc.tensor.matmul(tile(bank[7], t), tile(h_a, t), wv_t[:, :], start=True, stop=True)
            last.then_inc(a_v, 1)

        def a_keys_scalar(act, after_scores):
            act.wait_ge(a_k, 1)
            if after_scores:
                for q in range(PIECES):
                    act.wait_ge(ke_in[q], 16)
            nc.scalar.activation(k_t[:, :], bank[7][0:KROWS, :], ACT.Copy).then_inc(a_kc, 1)

        def a_values_in_scalar(act):
            act.wait_ge(a_v, 1)
            nc.scalar.activation(v_s[:, :, :], tokens(bank[7])[:, :, 0:KROWS], ACT.Copy).then_inc(a_vc, 1)

        def a_spread_sync(sp, b, q):
            n = NB // PIECES
            sp.dma_start(ke[0:KROWS, q * n:(q + 1) * n, :],
                         half(k_t, b).unsqueeze(1).broadcast_to([KROWS, n, T])).then_inc(ke_in[q], 16)

        LONE = 3
        UNITS = H
        assert H // 2 * 2 == UNITS

        def unit(u):
            return 1 - u // (H // 2), 2 * (u % (H // 2))

        def query_bank(u):
            return bank[6 if u >= LONE and (u - LONE) % 2 == 0 else 0]

        def a_query_tensor(pe, u, after_scores):
            b, h = unit(u)
            if u == 0:
                pe.wait_ge(a_kc, 1)
            elif u < LONE:
                pe.wait_ge(a_qm, u)
            elif u > LONE:
                pe.wait_ge(a_qm, u - 1)
            elif after_scores:
                pe.wait_ge(a_on, GROUPS)
            for k in range(2):
                last = nc.tensor.matmul(half(query_bank(u), k)[0:QROWS, :], wq_rep[:, h + k, :], half(h_a, b), start=True, stop=True)
            last.then_inc(a_q, 1)

        def a_query_vector(dve, u):
            b, h = unit(u)
            dve.wait_ge(a_q, u + 1)
            m = mask_q[:, h // (H // G), :].unsqueeze(1).unsqueeze(1).broadcast_to([QROWS, NB, 2, QB])
            nc.vector.tensor_tensor(q_st[:, NB * b:NB * (b + 1), h:h + 2, :],
                                    query_bank(u)[0:QROWS, :].rearrange("p (h i a) -> p i h a", h=2, a=QB), m, ALU.mult).then_inc(a_qm, 1)

        VALUES, INVERSE, SCALED = 2, 4, 5

        def group_at(c, k):
            return c // CPG - 1 if c % CPG == k and c >= CPG else None

        def inverse_bank(g):
            return bank[3 if g < GROUPS - 1 else 6]

        def a_chunk_tensor(pe, c, after_f):
            if c < CHUNKS:
                b, i0 = c // (CHUNKS // 2), 2 * (c % (CHUNKS // 2))
                if b:
                    pe.wait_ge(ke_in[i0 // (NB // PIECES)], 16)
                if c >= 2:
                    pe.wait_ge(a_exp, c - 1)
                for k in range(2):
                    last = nc.tensor.matmul(bank[c % 2][:, k * T:(k + 1) * T],
                                            q_st[:, 2 * c + k, :, :].rearrange("p h a -> p (h a)"), ke[:, i0 + k, :],
                                            start=True, stop=True)
                last.then_inc(a_s, 1)
            g = group_at(c, VALUES)
            if g is not None:
                a_values_tensor(pe, g, after_f)
            g = group_at(c, INVERSE)
            if g is not None:
                pe.wait_ge(a_dg, g + 1)
                pe.wait_ge(a_ao, g + 1)
                nc.tensor.matmul(inverse_bank(g)[:, :], sel_r[:, :], dg[:, :, :].rearrange("p i c -> p (i c)"), start=True,
                                 stop=True).then_inc(a_r, 1)
            c -= 2
            if 0 <= c < CHUNKS:
                pe.wait_ge(a_exp, c + 1)
                if c:
                    pe.wait_ge(a_tc, c)
                elif after_f:
                    pe.wait_ge(s_g, 1)
                for kh in range(2):
                    for k in range(2):
                        last = nc.tensor.transpose(tile(bank[2], 2 * kh + k), probs[:, c % 2, k, kh * P:(kh + 1) * P],
                                                   ident[:, :])
                last.then_inc(a_t, 1)

        def a_values_tensor(pe, g, after_f):
            pe.wait_ge(a_tc, CPG * (g + 1))
            if g:
                pe.wait_ge(a_on, g)
            elif after_f:
                pe.wait_ge(f_x, 1)
            pt = probs_t[:, :, :, :].rearrange("p k i (g r a) -> p k i g r a", g=G, r=H // G)
            for kh in range(2):
                for r in range(H // G):
                    last = nc.tensor.matmul(
                        bank[3][32 * r:32 * r + 32, :].rearrange("p (i g a) -> p i g a", g=G, a=QB),
                        v_s[:, 2 * (g // 2) + kh, :], pt[:, kh, :, :, r, :], start=(kh == 0), stop=(kh == 1))
            last.then_inc(a_pv, 1)

        def a_max_vector(dve, c):
            if c < CHUNKS:
                dve.wait_ge(a_s, c + 1)
                nc.vector.tensor_reduce(nmax[:, 2 * c:2 * c + 2], bank[c % 2][:, :].rearrange("p (k t) -> p k t", k=2),
                                        AX_X, ALU.max, negate=True).then_inc(a_max, 1)

        def a_chunk_vector(dve, c):
            g = group_at(c, VALUES)
            if g is not None:
                dve.wait_ge(a_exp, CPG * (g + 1))
                cols = slice(BPG * g, BPG * (g + 1))
                nc.vector.reciprocal(rinv[:, cols], rsum[:, cols]).then_inc(a_inv, 1)
                dve.wait_ge(a_inv, g + 1)
                if g:
                    dve.wait_ge(a_r, g)
                nc.vector.tensor_tensor(dg[:, :, :], rinv[:, cols].unsqueeze(2).broadcast_to([P, BPG, G * QB]),
                                        mask_d[:, :].unsqueeze(1).broadcast_to([P, BPG, G * QB]), ALU.mult).then_inc(a_dg, 1)
            g = group_at(c, SCALED)
            if g is not None:
                dve.wait_ge(a_r, g + 1)
                cols = slice(BPG * g, BPG * (g + 1))
                nc.vector.tensor_tensor(ao[:, cols, :, :].rearrange("p i g a -> p (i g a)"), ao_raw[:, :], inverse_bank(g)[:, :],
                                        ALU.mult).then_inc(a_on, 1)

        def a_chunk_scalar(act, c, after_f):
            k = c - 2
            if 0 <= k < CHUNKS:
                if k and k % CPG == 0:
                    act.wait_ge(a_pv, k // CPG)
                elif k == 0 and after_f:
                    act.wait_ge(s_hl, LATE + 1)
                act.wait_ge(a_t, k + 1)
                i0 = 2 * (k % CPG)
                nc.scalar.activation(probs_t[:, :, i0:i0 + 2, :].rearrange("p k i c -> p k (i c)"),
                                     bank[2][:, :].rearrange("p (k c) -> p k c", k=2), ACT.Copy).then_inc(a_tc, 1)
            if c < CHUNKS:
                act.wait_ge(a_max, c + 1)
                if c >= 2:
                    act.wait_ge(a_t, c - 1)
                for k in range(2):
                    i = 2 * c + k
                    last = nc.scalar.activation(probs[:, c % 2, k, :], bank[c % 2][:, k * T:(k + 1) * T], ACT.Exp,
                                                bias=nmax[:, i:i + 1], accum_out=rsum[:, i:i + 1])
                last.then_inc(a_exp, 1)
            g = group_at(c, VALUES)
            if g is not None:
                act.wait_ge(a_pv, g + 1)
                if g:
                    act.wait_ge(a_on, g)
                nc.scalar.activation(ao_raw[:, :], bank[3][:, :], ACT.Copy).then_inc(a_ao, 1)
        def a_end_tensor(pe, with_next):
            pe.wait_ge(a_on, GROUPS)
            if with_next:
                pe.wait_ge(a_vc, 1)
            for g in range(G):
                last = nc.tensor.matmul(bank[7][:, :].rearrange("p (i a) -> p i a", a=QB), wo_x[:, g, :], ao[:, :, g, :],
                                        start=(g == 0), stop=(g == G - 1))
            last.then_inc(a_wo, 1)

        def a_back_tensor(pe):
            pe.wait_ge(a_y, 1)
            back_tensor(y_a, bank[7], a_back)

        def a_end_scalar(act, p):
            act.wait_ge(a_wo, 1)
            gate_scalar(bank[7], y_a, p, GA, a_y)

        def a_end_vector(dve, with_b):
            dve.wait_ge(a_back, 1)
            dve.wait_ge(xr_in, 16)
            if with_b:
                dve.wait_ge(b_x, 1)
            nc.vector.tensor_tensor(x1[:, :, :], x_res[:, :, :], tokens(bank[7]), ALU.add).then_inc(a_res, 1)

        def m_logits_tensor(pe):
            pe.wait_ge(b_h, 1)
            for t in range(TILES):
                last = nc.tensor.matmul(tile(bank[7], t), tile(h_b, t), wg_t[:, :], start=True, stop=True)
            last.then_inc(m_logit, 1)

        def m_logits_scalar(act):
            act.wait_ge(m_logit, 1)
            nc.scalar.activation(gate[:, :, :], tokens(bank[7])[:, :, 0:NE], ACT.Exp, scale=-1.0).then_inc(m_exp, 1)

        def m_route_tensor(pe):
            pe.wait_ge(m_ch, ROUTE_STEPS)
            for t in range(TILES):
                last = nc.tensor.transpose(tile(bank[7], t)[0:SROWS, :], we96[:, t, :], ident[:, :])
            last.then_inc(m_wt, 1)

        def split_first_scalar(act, src, keep, parts, ready, s_cp):
            act.wait_ge(ready, 1)
            last = nc.scalar.activation(parts[:, :], src[0:SROWS, :], ACT.Copy)
            if keep is not None:
                last = nc.scalar.activation(keep[0:SROWS, :], src[0:SROWS, :], ACT.Copy)
            last.then_inc(s_cp, 1)

        def split_first_vector(dve, src, parts, rest, s_cp, s_rest):
            dve.wait_ge(s_cp, 1)
            nc.vector.tensor_tensor(rest[0:SROWS, :], src[0:SROWS, :], parts[:, :], ALU.subtract).then_inc(s_rest, 1)

        def split_next_scalar(act, parts, rest, s_rest, s_mid):
            act.wait_ge(s_rest, 1)
            for k in range(1, PARTS):
                last = nc.scalar.activation(parts[32 * k:32 * k + 32, :], rest[32 * k:32 * k + 32, :], ACT.Copy)
            last.then_inc(s_mid, 1)

        def split_last_vector(dve, parts, rest, s_mid, s_done):
            dve.wait_ge(s_mid, 1)
            nc.vector.tensor_tensor(parts[64:96, :], rest[64:96, :], parts[64:96, :], ALU.subtract).then_inc(s_done, 1)

        ROUTE_STEPS = 21

        def m_route_vector(dve, k):
            if k == 0:
                dve.wait_ge(m_exp, 1)
            else:
                dve.wait_ge(m_ch, k)
            by_group = [P, TILES, NG, NG]
            other, own = gmax[:, :, :].unsqueeze(2).broadcast_to(by_group), gmax[:, :, :].unsqueeze(3).broadcast_to(by_group)
            flat_g, flat_e = "p t j i -> p t (j i)", "p t (g k) -> p (t g) k"
            open_ = grank[:, :, :].rearrange("p t g -> p (t g)").unsqueeze(2).broadcast_to([P, TILES * NG, NE // NG])
            fourth = top8[:, :, TOPK - 1:TOPK].broadcast_to([P, TILES, NE])
            few_e = few[:, :].unsqueeze(2).broadcast_to([P, TILES, NE])
            if k == 0:
                nc.vector.tensor_scalar(gate[:, :, :], gate[:, :, :], 1.0, None, ALU.add).then_inc(m_ch, 1)
            elif k == 1:
                nc.vector.reciprocal(score[:, :, :], gate[:, :, :]).then_inc(m_ch, 1)
            elif k == 2:
                nc.vector.tensor_reduce(gmax[:, :, :], score[:, :, :].rearrange("p t (g k) -> p t g k", g=NG), AX_X,
                                        ALU.max).then_inc(m_ch, 1)
            elif k == 3:
                nc.vector.tensor_tensor(beats[:, :, :, :], other, own, ALU.is_gt)
                nc.vector.tensor_tensor(ties[:, :, :, :], other, own, ALU.is_equal).then_inc(m_ch, 1)
            elif k == 4:
                nc.vector.tensor_tensor(ties[:, :, :, :].rearrange(flat_g), ties[:, :, :, :].rearrange(flat_g),
                                        tie[:, :].unsqueeze(1).broadcast_to([P, TILES, NG * NG]), ALU.mult).then_inc(m_ch, 1)
            elif k == 5:
                nc.vector.tensor_tensor(beats[:, :, :, :], beats[:, :, :, :], ties[:, :, :, :], ALU.add).then_inc(m_ch, 1)
            elif k == 6:
                nc.vector.tensor_reduce(grank[:, :, :], beats[:, :, :, :], AX_X, ALU.add).then_inc(m_ch, 1)
            elif k == 7:
                nc.vector.tensor_scalar(grank[:, :, :], grank[:, :, :], TOPG - 0.5, None, ALU.is_lt).then_inc(m_ch, 1)
            elif k == 8:
                nc.vector.tensor_tensor(masked[:, :, :].rearrange(flat_e, g=NG), score[:, :, :].rearrange(flat_e, g=NG), open_,
                                        ALU.mult).then_inc(m_ch, 1)
            elif k == 9:
                nc.vector.scalar_tensor_tensor(masked[:, :, :].rearrange(flat_e, g=NG), open_, -1.0,
                                               masked[:, :, :].rearrange(flat_e, g=NG), ALU.add, ALU.add).then_inc(m_ch, 1)
            elif k == 10:
                for t in range(TILES):
                    last = nc.vector.max(top8[:, t, :], masked[:, t, :])
                last.then_inc(m_ch, 1)
            elif k == 11:
                nc.vector.tensor_tensor(picked[:, :, :], masked[:, :, :], fourth, ALU.is_gt)
                nc.vector.tensor_tensor(equal[:, :, :], masked[:, :, :], fourth, ALU.is_equal).then_inc(m_ch, 1)
            elif k == 12:
                for t in range(TILES):
                    nc.vector.tensor_tensor_scan(prefix[:, t, :], equal[:, t, :], zero64[:, :], 0.0, ALU.add, ALU.add)
                nc.vector.tensor_reduce(few[:, :], picked[:, :, :], AX_X, ALU.add).then_inc(m_ch, 1)
            elif k == 13:
                nc.vector.tensor_tensor(prefix[:, :, :], prefix[:, :, :], few_e, ALU.add).then_inc(m_ch, 1)
            elif k == 14:
                nc.vector.scalar_tensor_tensor(equal[:, :, :], prefix[:, :, :], TOPK + 0.5, equal[:, :, :], ALU.is_lt,
                                               ALU.mult).then_inc(m_ch, 1)
            elif k == 15:
                nc.vector.tensor_tensor(picked[:, :, :], picked[:, :, :], equal[:, :, :], ALU.add).then_inc(m_ch, 1)
            elif k == 16:
                nc.vector.tensor_tensor(picked[:, :, :], picked[:, :, :], score[:, :, :], ALU.mult).then_inc(m_ch, 1)
            elif k == 17:
                nc.vector.tensor_reduce(few[:, :], picked[:, :, :], AX_X, ALU.add).then_inc(m_ch, 1)
            elif k == 18:
                nc.vector.reciprocal(few[:, :], few[:, :]).then_inc(m_ch, 1)
            elif k == 19:
                nc.vector.tensor_scalar(few[:, :], few[:, :], ROUTE_SCALE, None, ALU.mult).then_inc(m_ch, 1)
            else:
                for part in range(PARTS):
                    last = nc.vector.tensor_tensor(we96[:, :, 32 * part:32 * part + NE], picked[:, :, :], few_e, ALU.mult)
                last.then_inc(m_ch, 1)

        def m_up_tensor(pe, e):
            if e:
                pe.wait_ge(m_tz, e)
            nc.tensor.matmul(bank[4][:, :], w1_t[:, e, :], h_b[:, :], start=True, stop=True).then_inc(m_h1, 1)
            if e:
                pe.wait_ge(m_u, e)
            nc.tensor.matmul(bank[5][:, :], w3_t[:, e, :], h_b[:, :], start=True, stop=True).then_inc(m_h3, 1)

        def m_down_tensor(pe, e):
            pe.wait_ge(m_hh, e + 1)
            nc.tensor.matmul(bank[7][:, :], w2_t[:, e, :], zh[e % 2], start=False, stop=(e == NE - 1)).then_inc(m_w2, 1)

        def m_weight_tensor(pe, e):
            if e == 0:
                nc.tensor.matmul(bank[7][:, :], b2_r[:, :], w_rows[0:SROWS, :], start=True, stop=False)
            else:
                pe.wait_ge(m_hh, e)
            nc.tensor.matmul(bank[6][:, :], sel_n[:, e, :], w_parts[:, :], start=True, stop=True).then_inc(m_wb, 1)

        def m_expert_tensor(pe, e):
            if e:
                m_down_tensor(pe, e - 1)
            if e + 1 < NE:
                m_up_tensor(pe, e + 1)

        def m_expert_scalar(act, e):
            act.wait_ge(m_h1, e + 1)
            if e >= 2:
                act.wait_ge(m_w2, e - 1)
            nc.scalar.activation(th[e % 2], bank[4][:, :], ACT.Tanh, bias=b1_c[:, e:e + 1], scale=0.5)
            nc.scalar.activation(zh[e % 2], bank[4][:, :], ACT.Identity, bias=b1_c[:, e:e + 1], scale=0.5).then_inc(m_tz, 1)
            act.wait_ge(m_h3, e + 1)
            if e >= 2:
                act.wait_ge(m_b, e - 1)
            nc.scalar.activation(uh[e % 2], bank[5][:, :], ACT.Identity, bias=b3_c[:, e:e + 1]).then_inc(m_u, 1)

        def m_expert_vector(dve, e):
            dve.wait_ge(m_tz, e + 1)
            nc.vector.scalar_tensor_tensor(zh[e % 2], th[e % 2], 1.0, zh[e % 2], ALU.add, ALU.mult).then_inc(m_a, 1)
            dve.wait_ge(m_u, e + 1)
            dve.wait_ge(m_a, e + 1)
            nc.vector.tensor_tensor(zh[e % 2], zh[e % 2], uh[e % 2], ALU.mult).then_inc(m_b, 1)
            dve.wait_ge(m_wb, e + 1)
            dve.wait_ge(m_b, e + 1)
            nc.vector.tensor_tensor(zh[e % 2], zh[e % 2], bank[6][:, :], ALU.mult).then_inc(m_hh, 1)

        def m_end_scalar(act, p):
            act.wait_ge(m_w2, NE)
            gate_scalar(bank[7], y_b, p, GB, b_y)

        def m_back_tensor(pe):
            pe.wait_ge(b_y, 1)
            back_tensor(y_b, bank[4], b_back)

        def m_end_vector(dve, after_f):
            dve.wait_ge(b_back, 1)
            if after_f:
                dve.wait_ge(o_out, 16)
            nc.vector.tensor_tensor(x_b[:, :, :], x1[:, :, :], tokens(bank[4]), ALU.add).then_inc(b_x, 1)
            dve.wait_ge(b_x, 1)
            ln_stats_vector(dve, LN_S, x_b)

        def s_in_tensor(pe, part):
            pe.wait_ge(n_h, 1)
            for k in (0, 1) if part == 0 else (2, 3):
                nc.tensor.matmul(bank[4 + k][:, :], win_t[:, k * P:(k + 1) * P], h_b[:, :], start=True, stop=True).then_inc(s_xz, 1)

        def s_z_scalar(act, h):
            act.wait_ge(s_xz, NH + h + 1)
            nc.scalar.activation(gz_t[:, h, :], bank[6 + h][:, :], ACT.Tanh, scale=0.5).then_inc(s_z, 1)

        def s_conv_vector(dve, h, part):
            a, x = (ap.rearrange("p (b t) -> p b t", b=2) for ap in (acc[:, h, :], bank[4 + h][:, :]))
            if part == 0:
                dve.wait_ge(s_xz, h + 1)
                nc.vector.tensor_scalar(a, x, conv_w[:, h, KC - 1:KC], None, ALU.mult).then_inc(s_cv, 1)
            for back in (1,) if part == 0 else range(2, KC):
                dve.wait_ge(s_cv, KC * h + back)
                nc.vector.scalar_tensor_tensor(a[:, :, back:], x[:, :, 0:T - back], conv_w[:, h, KC - 1 - back:KC - back],
                                               a[:, :, back:], ALU.mult, ALU.add).then_inc(s_cv, 1)

        def s_conv_scalar(act, h):
            act.wait_ge(s_cv, KC * (h + 1))
            nc.scalar.activation(act_t[:, h, :], acc[:, h, :], ACT.Tanh, bias=conv_b[:, h:h + 1], scale=0.5).then_inc(s_ct, 1)

        def s_half_vector(dve, h):
            dve.wait_ge(s_cv, KC * (h + 1))
            nc.vector.tensor_scalar(act_z[:, h, :], acc[:, h, :], 0.5, conv_b[:, h:h + 1], ALU.mult, ALU.add).then_inc(s_cz, 1)

        def s_gate_vector(dve, h):
            dve.wait_ge(s_cz, h + 1)
            dve.wait_ge(s_ct, h + 1)
            nc.vector.scalar_tensor_tensor(x_conv[:, h, :], act_t[:, h, :], 1.0, act_z[:, h, :], ALU.add, ALU.mult).then_inc(s_xc, 1)

        def s_zgate_vector(dve, h):
            dve.wait_ge(s_z, h + 1)
            nc.vector.scalar_tensor_tensor(z_gate[:, h, :], gz_t[:, h, :], 1.0, bank[6 + h][:, :], ALU.add, ALU.mult).then_inc(s_zg, 1)

        def s_step_tensor(pe, h):
            if h == 0:
                pe.wait_ge(s_xc, NH)
                pe.wait_ge(s_zg, 1)
            for k in range(NH):
                last = nc.tensor.matmul(bank[5 + h][:, :], w_dtx[:, k, h * P:(h + 1) * P], x_conv[:, k, :],
                                        start=(k == 0), stop=(k == NH - 1))
            last.then_inc(s_dtp, 1)

        def s_rows_tensor(pe, with_next):
            if with_next:
                pe.wait_ge(a_h, 1)
            for k in range(NH):
                last = nc.tensor.matmul(bank[4][0:SROWS, :], wx_bc[:, k, :], x_conv[:, k, :], start=(k == 0), stop=(k == NH - 1))
            last.then_inc(s_bc, 1)

        def s_step_scalar(act, h):
            act.wait_ge(s_dtp, h + 1)
            nc.scalar.activation(sp_e[:, h, :], bank[5 + h][:, :], ACT.Abs, bias=b_dt[:, h:h + 1]).then_inc(s_sp1, 1)

        def s_relu_vector(dve, h):
            if h == 0:
                dve.wait_ge(s_zg, NH)
            dve.wait_ge(s_sp1, h + 1)
            nc.vector.tensor_scalar(sp_r[:, h, :], bank[5 + h][:, :], b_dt[:, h:h + 1], 0.0, ALU.add, ALU.max).then_inc(s_spr, 1)

        def s_exp_scalar(act):
            act.wait_ge(s_sp1, NH)
            nc.scalar.activation(sp_e[:, :, :], sp_e[:, :, :], ACT.Exp, scale=-1.0).then_inc(s_sp2, 1)

        def s_log_scalar(act):
            act.wait_ge(s_sp2, 1)
            nc.scalar.activation(sp_l[:, :, :], sp_e[:, :, :], ACT.Ln, bias=1.0).then_inc(s_sp3, 1)

        def s_step_vector(dve, k):
            if k == 0:
                dve.wait_ge(s_sp2, 1)
                nc.vector.tensor_scalar(sp_u[:, :, :], sp_e[:, :, :], 1.0, None, ALU.add).then_inc(s_spv, 1)
            elif k == 1:
                dve.wait_ge(s_spv, 1)
                nc.vector.scalar_tensor_tensor(sp_u[:, :, :], sp_u[:, :, :], 1.0, sp_e[:, :, :], ALU.subtract,
                                               ALU.subtract).then_inc(s_spv, 1)
            elif k == 2:
                dve.wait_ge(s_spv, 2)
                dve.wait_ge(s_spr, NH)
                nc.vector.tensor_tensor(sp_r[:, :, :], sp_r[:, :, :], sp_u[:, :, :], ALU.subtract).then_inc(s_spv, 1)
            else:
                dve.wait_ge(s_spv, 3)
                dve.wait_ge(s_sp3, 1)
                nc.vector.tensor_tensor(dt_s[:, :, :], sp_r[:, :, :], sp_l[:, :, :], ALU.add).then_inc(s_dt, 1)
                dve.wait_ge(s_dt, 1)
                nc.vector.tensor_tensor(dt_x[:, :, :], dt_s[:, :, :], x_conv[:, :, :], ALU.mult).then_inc(s_dt, 1)

        def segments(ap):
            return ap.rearrange("p h (b t) -> p (h b) t", b=2)

        def b_bank(n):
            return bank[4 if n % 2 == 0 else 1]

        def s_b_tensor(pe, n):
            if n == 0:
                pe.wait_ge(s_bcp, 1)
            elif n >= 2:
                pe.wait_ge(s_dbx, n - 1)
            nc.tensor.matmul(b_bank(n)[:, :], sel_n[:, n, :], bc_parts[:, :], start=True, stop=True).then_inc(s_bb, 1)

        def s_c_tensor(pe, n):
            if n == 0:
                pe.wait_ge(s_sp1, 1)
                pe.wait_ge(s_spr, 1)
            else:
                pe.wait_ge(s_cs, n)
            nc.tensor.matmul(bank[5][:, :], sel_n[:, NS + n, :], bc_parts[:, :], start=True, stop=True).then_inc(s_cb, 1)

        assert LATE == 2
        PAIRS_N = NS // 2
        ADDED = (3, 4, 5, 6, PAIRS_N - 1)
        SUM_AT = (4, 5, 8, 10, 12, 14, 15)

        def sum_at(n):
            return [k for k in range(PAIRS_N - 1) if SUM_AT[k] == n]

        def s_sum_tensor(pe, k, with_scores):
            if k == 0 and with_scores:
                pe.wait_ge(a_ao, GROUPS)
            if k == PAIRS_N - 1:
                pe.wait_ge(s_hl, LATE + 1)
            elif k in ADDED:
                pe.wait_ge(s_hs, ADDED.index(k) + 1)
            else:
                pe.wait_ge(s_hc, 2 * k + 2)
            states = (2 * k,) if k in ADDED else (2 * k, 2 * k + 1)
            for h in range(NH):
                for n in states:
                    last = nc.tensor.matmul(bank[2 + h][:, :], ident[:, :], ring[n % RING][:, h, :], start=(n == 0),
                                            stop=(n == NS - 2))
            last.then_inc(s_y if k < PAIRS_N - 1 else s_yl, 1)

        def s_decay_scalar(act, n):
            if n < 2:
                act.wait_ge(s_dt, 1)
            if n >= 2:
                act.wait_ge(s_h, n - 1)
            for h in range(NH):
                last = nc.scalar.activation(segments(da[n % 2])[:, 2 * h:2 * h + 2, 1:], segments(dt_s[:, :, :])[:, 2 * h:2 * h + 2, 1:],
                                            ACT.Exp, scale=neg_a[:, h * NS + n:h * NS + n + 1])
            last.then_inc(s_da, 1)

        def s_c_scalar(act, n):
            act.wait_ge(s_cb, n + 1)
            if n >= len(c_s):
                act.wait_ge(s_hc, n - len(c_s) + 1)
            nc.scalar.activation(c_s[n % len(c_s)], bank[5][:, :], ACT.Copy).then_inc(s_cs, 1)

        def s_input_vector(dve, n, with_scores):
            dve.wait_ge(s_bb, n + 1)
            if n == 0:
                dve.wait_ge(s_dt, 2)
                for k in range(2):
                    last = nc.vector.memset(segments(da[k])[:, :, 0:1], 0.0)
                last.then_inc(s_dt, 1)
            if n == 3 and with_scores:
                dve.wait_ge(a_pv, GROUPS)
            if n >= RING:
                dve.wait_ge(s_y, (n - RING) // 2 + 1)
            nc.vector.tensor_tensor(ring[n % RING], dt_x[:, :, :], b_bank(n)[:, :].unsqueeze(1).broadcast_to([P, NH, TOK]),
                                    ALU.mult).then_inc(s_dbx, 1)

        def s_scan_vector(dve, n):
            if n < NS - LATE:
                dve.wait_ge(s_dbx, n + 1)
                dve.wait_ge(s_da, n + 1)
            if n == 0:
                dve.wait_ge(s_dt, 3)
            r = ring[n % RING].rearrange("p h t -> p (h t)")
            nc.vector.tensor_tensor_scan(r, da[n % 2].rearrange("p h t -> p (h t)"), r, 0.0, ALU.mult,
                                         ALU.add).then_inc(s_h if n < NS - LATE else s_late, 1)

        def s_read_gpsimd(pool, n):
            late = n - (NS - LATE)
            if late < 0:
                pool.wait_ge(s_h, n + 1)
                pool.wait_ge(s_cs, n + 1)
            else:
                pool.wait_ge(s_late, late + 1)
            r = ring[n % RING]
            nc.gpsimd.tensor_tensor(r, r, c_s[n % len(c_s)].unsqueeze(1).broadcast_to([P, NH, TOK]),
                                    ALU.mult).then_inc(s_hc if late < 0 else s_hl, 1)
            if n % 2 and n // 2 in ADDED:
                if late < 0:
                    pool.wait_ge(s_hc, n + 1)
                else:
                    pool.wait_ge(s_hl, late + 1)
                nc.gpsimd.tensor_tensor(ring[(n - 1) % RING], ring[(n - 1) % RING], r, ALU.add).then_inc(s_hs if late < 0 else s_hl, 1)

        def s_end_vector(dve, h):
            dve.wait_ge(s_yl, 1)
            nc.vector.scalar_tensor_tensor(z_gate[:, h, :], z_gate[:, h, :], 0.5, bank[2 + h][:, :], ALU.mult, ALU.mult).then_inc(s_g, 1)
            dve.wait_ge(s_g, h + 1)
            nc.vector.scalar_tensor_tensor(z_gate[:, h, :], x_conv[:, h, :], d_par[:, h:h + 1], z_gate[:, h, :],
                                           ALU.mult, ALU.add).then_inc(s_yv, 1)

        def f_out_tensor(pe):
            pe.wait_ge(s_yv, NH)
            for k in range(NH):
                last = nc.tensor.matmul(bank[3][:, :], wout_t[:, k, :], z_gate[:, k, :], start=(k == 0), stop=(k == NH - 1))
            last.then_inc(f_o, 1)

        def f_out_scalar(act, p):
            act.wait_ge(f_o, 1)
            gate_scalar(bank[3], y_f, p, 6 + GA, f_y)

        def f_res_tensor(pe):
            pe.wait_ge(f_y, 1)
            back_tensor(y_f, bank[3], f_back)

        def f_res_vector(dve):
            dve.wait_ge(f_back, 1)
            nc.vector.tensor_tensor(x_b[:, :, :], x_b[:, :, :], tokens(bank[3]), ALU.add).then_inc(f_x3, 1)
            dve.wait_ge(f_x3, 1)
            ln_stats_vector(dve, LN_F, x_b)

        def f_mix_tensor(pe):
            pe.wait_ge(f_h, 1)
            nc.tensor.matmul(bank[3][:, :], ffn_w[:, :], h_f[:, :], start=True, stop=True).then_inc(f_m, 1)

        def f_mix_scalar(act):
            act.wait_ge(f_m, 1)
            nc.scalar.activation(y_f[:, :], bank[3][:, :], ACT.Tanh, bias=ffn_b[:, :]).then_inc(f_t, 1)

        def f_gate_vector(dve, p):
            dve.wait_ge(f_t, 1)
            for b in range(2):
                last = nc.vector.tensor_scalar(half(y_f, b), half(y_f, b), scale_of(6 + GB, p, b), None, ALU.mult)
            last.then_inc(f_g, 1)

        def f_end_tensor(pe):
            pe.wait_ge(f_g, 1)
            back_tensor(y_f, bank[3], f_back)

        def f_end_vector(dve):
            dve.wait_ge(f_back, 2)
            nc.vector.tensor_tensor(x_b[:, :, :], x_b[:, :, :], tokens(bank[3]), ALU.add).then_inc(f_x, 1)

        FEW = NE // 2
        PREP0 = NE
        SLOTS = PREP0 + CHUNKS - FEW + 2

        def chunk_of(slot):
            if slot < PREP0:
                return slot // 2 if slot % 2 == 0 else None
            return slot - PREP0 + FEW

        def exp_of(slot):
            if slot < PREP0:
                return slot // 2 if slot % 2 else None
            return chunk_of(slot)

        def projection_tensor(pe, slot):
            if slot == 3:
                s_sum_tensor(pe, PAIRS_N - 1, False)
            elif slot == 6:
                f_out_tensor(pe)
            elif slot == 7:
                f_res_tensor(pe)
            elif slot == 10:
                ln_tensor(pe, LN_F, bank[3])
            elif slot == 11:
                f_mix_tensor(pe)
            elif slot == 13:
                f_end_tensor(pe)

        def projection_scalar(act, slot, p):
            if slot == 6:
                f_out_scalar(act, p)
            elif slot == 10:
                ln_out_scalar(act, LN_F, p, 6 + SB, 6 + CB, bank[3])
            elif slot == 11:
                f_mix_scalar(act)

        def projection_vector(dve, slot, p):
            if slot in (3, 4):
                s_end_vector(dve, slot - 3)
            elif slot == 7:
                f_res_vector(dve)
            elif slot == 9:
                ln_norm_vector(dve, LN_F, x_b)
            elif slot == 12:
                f_gate_vector(dve, p)
            elif slot == 14:
                f_end_vector(dve)

        AT = dict(down=1, gate=1, back=3, add=4, norm=7, turned=9, in_x=10, in_z=11, conv=10, tanh_z=11, tanh_x=12,
                  silu=14, dt0=16, dt1=17, bc=20, step=17, exp=18, log=20, add_log=20, split=21, split_rest=22,
                  split_next=23, split_last=24, decay=24, first=24, next_stats=3, next_norm=5, next_turned=14,
                  next_out=15, keys=18, keys_out=19)

        def prepare_tensor(pe, k, with_next):
            if k == AT["down"]:
                m_down_tensor(pe, NE - 1)
            if k == AT["back"]:
                m_back_tensor(pe)
            if k == AT["turned"]:
                ln_tensor(pe, LN_S, bank[4])
            if k == AT["in_x"]:
                s_in_tensor(pe, 0)
            if k == AT["in_z"]:
                s_in_tensor(pe, 1)
            if k == AT["dt0"]:
                s_step_tensor(pe, 0)
            if k == AT["dt1"]:
                s_step_tensor(pe, 1)
            if k == AT["bc"]:
                s_rows_tensor(pe, with_next)
            if k == AT["first"]:
                s_b_tensor(pe, 0)
                s_c_tensor(pe, 0)

        def prepare_scalar(act, k, p):
            if k == AT["gate"]:
                m_end_scalar(act, p)
            if k == AT["turned"]:
                ln_out_scalar(act, LN_S, p, 6 + SA, 6 + CA, bank[4])
            for h in range(NH):
                if k == AT["tanh_z"] + 2 * h:
                    s_z_scalar(act, h)
                if k == AT["tanh_x"] + 2 * h:
                    s_conv_scalar(act, h)
                if k == AT["step"] + h:
                    s_step_scalar(act, h)
            if k == AT["exp"]:
                s_exp_scalar(act)
            if k == AT["log"]:
                s_log_scalar(act)
            if k == AT["split"]:
                split_first_scalar(act, bank[4], None, bc_parts, s_bc, s_bcc)
            if k == AT["split_next"]:
                split_next_scalar(act, bc_parts, bc_rest, s_bcr, s_bcm)
            if k == AT["decay"]:
                s_decay_scalar(act, 0)

        def prepare_vector(dve, k, after_f):
            if k == AT["add"]:
                m_end_vector(dve, after_f)
            if k == AT["norm"]:
                ln_norm_vector(dve, LN_S, x_b)
            for h in range(NH):
                if k == AT["conv"] + 2 * h:
                    s_conv_vector(dve, h, 0)
                if k == AT["conv"] + 2 * h + 1:
                    s_conv_vector(dve, h, 1)
                    s_half_vector(dve, h)
                if k == AT["silu"] + h:
                    s_gate_vector(dve, h)
                    s_zgate_vector(dve, h)
                if k == AT["step"] + h:
                    s_relu_vector(dve, h)
            for part in range(4):
                if k == AT["add_log"] + part:
                    s_step_vector(dve, part)
            if k == AT["split_rest"]:
                split_first_vector(dve, bank[4], bc_parts, bc_rest, s_bcc, s_bcr)
            if k == AT["split_last"]:
                split_last_vector(dve, bc_parts, bc_rest, s_bcm, s_bcp)

        def next_tensor(pe, k, with_b):
            if k == AT["next_turned"]:
                if with_b:
                    pe.wait_ge(s_cv, NH * KC)
                ln_tensor(pe, LN_A, bank[4])
            if k == AT["keys"]:
                a_keys_tensor(pe, with_b)

        def next_scalar(act, k, p, after_scores):
            if k == AT["next_out"]:
                ln_out_scalar(act, LN_A, p, SA, CA, bank[4])
            if k == AT["keys_out"]:
                a_keys_scalar(act, after_scores)

        def next_vector(dve, k):
            if k == AT["next_stats"]:
                dve.wait_ge(xa_in, 16)
                ln_stats_vector(dve, LN_A, x_a)
            if k == AT["next_norm"]:
                ln_norm_vector(dve, LN_A, x_a)

        TAIL = (CHUNKS + VALUES, CHUNKS + INVERSE, CHUNKS + SCALED)
        BESIDE = dict(end=3, back=4, add=4, norm=5, turned=6, logits=7, choice=8)
        ROUTE0, ROUTE_IN = BESIDE["choice"], 5
        SPLIT0 = ROUTE0 + -(-ROUTE_STEPS // ROUTE_IN)
        assert SPLIT0 + 3 <= NS == UNITS

        def start_tensor(pe, n, ps, pn):
            if ps is not None and n < len(TAIL):
                a_chunk_tensor(pe, TAIL[n], False)
            if pn is not None and n == 1:
                a_values_in_tensor(pe)
            if ps is not None:
                if n == BESIDE["end"]:
                    a_end_tensor(pe, pn is not None)
                if n == BESIDE["back"]:
                    a_back_tensor(pe)
                if n == BESIDE["turned"]:
                    ln_tensor(pe, LN_B, bank[7])
                if n == BESIDE["logits"]:
                    m_logits_tensor(pe)
                if n == SPLIT0:
                    m_route_tensor(pe)

        def start_scalar(act, n, ps, pn):
            if ps is not None and n < len(TAIL):
                a_chunk_scalar(act, TAIL[n], False)
            if pn is not None and n == 1:
                a_values_in_scalar(act)
            if ps is not None:
                if n == BESIDE["end"]:
                    a_end_scalar(act, ps)
                if n == BESIDE["add"]:
                    ln_std_scalar(act, LN_B)
                if n == BESIDE["turned"]:
                    ln_out_scalar(act, LN_B, ps, SB, CB, bank[7])
                if n == BESIDE["logits"]:
                    m_logits_scalar(act)
                if n == SPLIT0:
                    split_first_scalar(act, bank[7], w_rows, w_parts, m_wt, m_cp)
                if n == SPLIT0 + 2:
                    split_next_scalar(act, w_parts, w_rest, m_rest, m_mid)

        def start_vector(dve, n, ps, pb):
            if ps is not None:
                if n < len(TAIL):
                    a_chunk_vector(dve, TAIL[n])
                if n == BESIDE["add"]:
                    a_end_vector(dve, pb is not None)
                    dve.wait_ge(a_res, 1)
                    ln_stats_vector(dve, LN_B, x1)
                if n == BESIDE["norm"]:
                    ln_inverse_vector(dve, LN_B)
                    ln_norm_vector(dve, LN_B, x1)
                if n == SPLIT0 + 1:
                    split_first_vector(dve, bank[7], w_parts, w_rest, m_cp, m_rest)
                if n == SPLIT0 + 2:
                    split_last_vector(dve, w_parts, w_rest, m_mid, m_parts)

        def route_vector(dve, n, part):
            k = ROUTE_IN * (n - ROUTE0) + part
            if 0 <= k < ROUTE_STEPS:
                m_route_vector(dve, k)

        def turn(ps, pn, pb, pf, further_loads=()):
            slots = range(SLOTS)
            scan = range(NS if ps is not None or pb is not None or pn is not None else 0)
            with nc.Block() as block:
                @block.sync
                def _(sp):
                    if pn is not None:
                        sp.dma_start(x_a[:, :, :], x_pair(pn)).then_inc(xa_in, 16)
                    for name, dst in further_loads:
                        sp.dma_start(dst, dram[name]).then_inc(loaded_late, 16)
                    if ps is not None:
                        sp.dma_start(x_res[:, :, :], x_pair(ps)).then_inc(xr_in, 16)
                    if pf is not None:
                        sp.wait_ge(f_x, 1)
                        sp.dma_start(out[pf].rearrange("(t q) d -> q t d", q=P), x_b[:, :, :]).then_inc(o_out, 16)
                    if ps is not None:
                        for q in range(PIECES):
                            sp.wait_ge(a_s, CHUNKS // 2 // PIECES * (q + 1))
                            a_spread_sync(sp, 1, q)
                    if pn is not None:
                        if ps is not None:
                            sp.wait_ge(a_s, CHUNKS)
                        sp.wait_ge(a_kc, 1)
                        for q in range(PIECES):
                            a_spread_sync(sp, 0, q)
                    for q in range(PIECES):
                        if ps is not None or pn is not None:
                            sp.wait_ge(ke_in[q], 16 if ps is None or pn is None else 32)
                    if pf is not None:
                        sp.wait_ge(o_out, 16)

                @block.gpsimd
                def _(pool):
                    if pf is not None:
                        for n in range(NS - LATE, NS):
                            s_read_gpsimd(pool, n)
                        ln_root_gpsimd(pool, LN_F)
                    if pn is not None:
                        ln_root_gpsimd(pool, LN_A)
                    if pb is not None:
                        ln_root_gpsimd(pool, LN_S)
                    if pb is not None:
                        for n in range(NS - LATE):
                            s_read_gpsimd(pool, n)

                @block.tensor
                def _(pe):
                    if pb is not None:
                        m_up_tensor(pe, 0)
                    for slot in slots:
                        if pf is not None:
                            projection_tensor(pe, slot)
                        if pb is not None:
                            if slot < NE:
                                m_weight_tensor(pe, slot)
                            else:
                                prepare_tensor(pe, slot - PREP0, pn is not None)
                        if pn is not None:
                            next_tensor(pe, slot - PREP0, pb is not None)
                        if ps is not None and chunk_of(slot) is not None:
                            a_chunk_tensor(pe, chunk_of(slot), pf is not None)
                        if pb is not None and slot < NE:
                            m_expert_tensor(pe, slot)
                    for n in scan:
                        if pn is not None and n < LONE:
                            a_query_tensor(pe, n, ps is not None)
                        if n == 0:
                            if pb is not None:
                                s_b_tensor(pe, 1)
                            start_tensor(pe, 0, ps, pn)
                        if pb is not None and n + 2 < NS:
                            s_b_tensor(pe, n + 2)
                        if pb is not None and n + 1 < NS:
                            s_c_tensor(pe, n + 1)
                        if n:
                            start_tensor(pe, n, ps, pn)
                            if pn is not None and LONE <= n + 1 < UNITS:
                                a_query_tensor(pe, n + 1, ps is not None)
                            if pb is not None:
                                for k in sum_at(n):
                                    s_sum_tensor(pe, k, ps is not None)

                @block.scalar
                def _(act):
                    for slot in slots:
                        if pf is not None:
                            projection_scalar(act, slot, pf)
                        if pb is not None:
                            if slot < NE:
                                m_expert_scalar(act, slot)
                            else:
                                prepare_scalar(act, slot - PREP0, pb)
                        if pn is not None:
                            next_scalar(act, slot - PREP0, pn, ps is not None)
                        if ps is not None and exp_of(slot) is not None:
                            a_chunk_scalar(act, exp_of(slot), pf is not None)
                    if pb is not None:
                        s_c_scalar(act, 0)
                    for n in scan:
                        if pb is not None and n + 1 < NS:
                            s_decay_scalar(act, n + 1)
                            s_c_scalar(act, n + 1)
                        start_scalar(act, n, ps, pn)

                @block.vector
                def _(dve):
                    if pf is not None:
                        for n in range(NS - LATE, NS):
                            s_scan_vector(dve, n)
                    for slot in slots:
                        if pb is not None and slot >= PREP0:
                            prepare_vector(dve, slot - PREP0, pf is not None)
                        if pn is not None:
                            next_vector(dve, slot - PREP0)
                        if pb is not None and slot < NE:
                            m_expert_vector(dve, slot)
                        if pf is not None:
                            projection_vector(dve, slot, pf)
                        if ps is not None and chunk_of(slot) is not None:
                            a_max_vector(dve, chunk_of(slot))
                            a_chunk_vector(dve, chunk_of(slot))
                    for n in scan:
                        if pb is not None:
                            s_input_vector(dve, n, ps is not None)
                        if ps is not None:
                            route_vector(dve, n, 0)
                        if pb is not None and n < NS - LATE:
                            s_scan_vector(dve, n)
                        if ps is not None:
                            route_vector(dve, n, 1)
                        if pn is not None:
                            a_query_vector(dve, n)
                        if ps is not None:
                            route_vector(dve, n, 2)
                        start_vector(dve, n, ps, pb)
                        if ps is not None:
                            for part in range(3, ROUTE_IN):
                                route_vector(dve, n, part)
            clear_semaphores()

        turn(None, 0, None, None, late_loads)
        with nc.Block() as block:
            @block.sync
            def _(sp):
                sp.wait_ge(loaded_late, LOADED_LATE)
        turn(0, 1, None, None)
        turn(1, 2, 0, None)
        with nc.Fori(2, PAIRS - 1) as t:
            turn(t, t + 1, t - 1, t - 2)
        turn(PAIRS - 1, None, PAIRS - 2, PAIRS - 3)
        turn(None, None, PAIRS - 1, PAIRS - 2)
        turn(None, None, None, PAIRS - 1)


def kernel(**inputs):
    import numpy as np
    import concourse.bacc as bacc
    from concourse.bass_utils import run_bass_kernel_spmd as run

    f = {k: np.asarray(v) for k, v in inputs.items()}
    one = np.float32

    def cols(w):
        return w.transpose(2, 0, 1).reshape(w.shape[2], -1)

    def halves(w):
        return w.reshape(NH, P, -1).transpose(1, 0, 2).reshape(P, -1)

    wq = f["L0_attn_Wq"].reshape(H, HD, D)
    wo = f["L0_attn_Wo"].reshape(D, G, H // G, HD)
    wo_x = np.zeros((H // G, G, HD, G, D), one)
    for g in range(G):
        wo_x[:, g, :, g, :] = wo[:, g].transpose(1, 2, 0)
    i, a, k = np.arange(NB), np.arange(QB), np.arange(T)
    dist = np.clip(QB * i[None, :, None] + a[:, None, None] - k[None, None, :], 1 - MAX_POS, MAX_POS - 1) + MAX_POS - 1
    e_shift = f["L0_attn_E"][dist].transpose(0, 3, 1, 2)
    b2 = np.zeros((SROWS, D), one)
    b2[:NE] = f["L0_ffn_b2"]
    w_x = f["L1_attn_W_x"]
    rows = np.arange(QROWS)
    mask_q = np.zeros((QROWS, G, QB), one)
    for r in rows:
        if r < KROWS:
            mask_q[r, r // HD, :] = (1.0 / HD) ** 0.5
        else:
            mask_q[r, :, (r - KROWS) // HD] = (1.0 / HD) ** 0.5
    ha = np.arange(P)
    mask_d = ((ha[:, None] // QB // (H // G) == np.arange(G * QB)[None, :] // QB)
              & (ha[:, None] % QB == np.arange(G * QB)[None, :] % QB)).astype(one)
    sel_r = (ha[:, None] // QB % (H // G) == np.arange(P)[None, :] // 32).astype(one)
    j = np.arange(NG)
    tie = np.tile((j[None, :] < j[:, None]).astype(one).reshape(1, -1), (P, 1))
    bf16 = mybir.dt.np(BF16)
    sel_n = np.repeat((np.arange(SROWS)[:, None] % 32 == np.arange(32)[None, :]), P, axis=1).astype(bf16)

    arrays = {
        "x": f["L0_attn_x"], "wq_rep": np.tile(wq.transpose(2, 0, 1), (1, 1, QROWS // HD)), "wk_t": f["L0_attn_Wk"].T,
        "wv_t": np.tile(f["L0_attn_Wv"].T, (1, P // KROWS)), "wo_x": wo_x, "e_shift": e_shift,
        "wg_t": np.tile(f["L0_ffn_Wg"].T, (1, P // NE)), "w1_t": cols(f["L0_ffn_W1"]), "w3_t": cols(f["L0_ffn_W3"]),
        "w2_t": cols(f["L0_ffn_W2"]), "b1_c": f["L0_ffn_b1"].T, "b3_c": f["L0_ffn_b3"].T, "b2_r": b2,
        "c_t": np.concatenate([f["L0_c"].T, f["L1_c"].T], 1), "wmod": np.concatenate([f["L0_wmod"], f["L1_wmod"]], 1),
        "win_t": f["L1_attn_W_in"].T, "conv_w": halves(f["L1_attn_conv_w"][:, 0, :]), "conv_b": halves(f["L1_attn_conv_b"][:, None]),
        "wx_bc": halves(np.tile(w_x[DTR:].T, (1, PARTS))), "wx_dt": w_x[:DTR], "wdt_t": f["L1_attn_W_dt"].T,
        "b_dt": halves(f["L1_attn_b_dt"][:, None]), "a_log": halves(f["L1_attn_A_log"]), "d_par": halves(f["L1_attn_D_param"][:, None]),
        "wout_t": halves(f["L1_attn_W_out"].T), "ffn_w_t": f["L1_ffn_weight"].T, "ffn_a1": f["L1_ffn_aux_weight1"],
        "ffn_a2": f["L1_ffn_aux_weight2"], "ffn_b": f["L1_ffn_bias"][:, None], "ident": np.eye(P, dtype=one),
        "mask_q": mask_q, "mask_d": mask_d, "sel_r": sel_r, "tie": tie, "sel_n": sel_n,
    }
    nc = bacc.Bacc("TRN2", target_bir_lowering=False, num_devices=1)
    dram, given = {}, {}
    for name, shape in IN_SHAPES:
        v = np.ascontiguousarray(arrays[name].reshape(shape))
        given[f"in_{name}"] = v
        dram[name] = nc.dram_tensor(f"in_{name}", shape, BF16 if name == "sel_n" else F32, kind="ExternalInput").ap()
    out = nc.dram_tensor("out", (PAIRS, TOK, D), F32, kind="ExternalOutput").ap()
    build(nc, dram, out)
    r = run(nc, [given], core_ids=[0])
    return r.results[0]["out"].reshape(B, T, D)
```
